# Optimizing a Trainium2 kernel written in Bass

```python
import numpy as np
import jax
import jax.numpy as jnp

def _softmax(x, axis=-1):
    return jax.nn.softmax(x, axis=axis)

def _gelu(x):
    return jax.nn.gelu(x, approximate=True)

def _silu(x):
    return jax.nn.silu(x)

def _sigmoid(x):
    return jax.nn.sigmoid(x)

def _layernorm(x, axis=-1, eps=1e-05):
    m = jnp.mean(x, axis=axis, keepdims=True)
    v = jnp.var(x, axis=axis, keepdims=True)
    return (x - m) / jnp.sqrt(v + eps)

def _scatter_add(tgt, idx, src, axis=0):
    return tgt.at[idx].add(src)

def _segment_sum(src, seg, n):
    return jax.ops.segment_sum(src, seg, n)
kernel_name = 'mk_vit_tower_d4_tok_img256_r4_57e772'

def setup_inputs(seed: int=0):
    np.random.seed(seed)
    _w = jnp.asarray

    def _rec_inputs():
        import jax
        import jax.numpy as jnp
        _rk = jax.random.key(seed)
        x = -0.000596345 + 1.00056 * jax.random.normal(jax.random.fold_in(_rk, 1), (128, 64, 64, 3), jnp.float32)
        return x
    x = _rec_inputs()

    def _L0_tok_setup():
        import jax, jax.numpy as jnp
        import numpy as np
        from jax import lax
        NEG_SLOPE = 0.01

        def leaky(v):
            return jnp.where(v >= 0, v, NEG_SLOPE * v)
        key = jax.random.key(seed)
        ks = jax.random.split(key, 12)
        B, H, W = (16, 64, 64)
        width, mx, my, L, nl = (32, 16, 16, 3, 4)
        scale = 1.0 / (width * width)
        return {'x': jax.random.normal(ks[0], (B, H, W, 3), jnp.float32), 'input_grid': jax.random.uniform(ks[1], (H, W, 2), jnp.float32), 'P_w': jax.random.normal(ks[2], (5, width), jnp.float32) * 0.3, 'P_b': jax.random.normal(ks[3], (width,), jnp.float32) * 0.05, 'spec_wr': jax.random.uniform(ks[4], (nl, width, width, mx, my), jnp.float32) * scale, 'spec_wi': jax.random.uniform(ks[5], (nl, width, width, mx, my), jnp.float32) * scale, 'conv_w': jax.random.normal(ks[6], (nl, width, width, L, L), jnp.float32) * 0.05, 'conv_b': jax.random.normal(ks[7], (nl, width), jnp.float32) * 0.05, 'Q1_w': jax.random.normal(ks[8], (width, width), jnp.float32) * 0.15, 'Q1_b': jax.random.normal(ks[9], (width,), jnp.float32) * 0.05, 'Q2_w': jax.random.normal(ks[10], (width, 1), jnp.float32) * 0.15, 'Q2_b': jax.random.normal(ks[11], (1,), jnp.float32) * 0.05}
    _L0_tok_all = _L0_tok_setup()
    _L0_tok_in = {k: v for k, v in _L0_tok_all.items() if k in ('input_grid', 'P_w', 'P_b', 'spec_wr', 'spec_wi', 'conv_w', 'conv_b', 'Q1_w', 'Q1_b', 'Q2_w', 'Q2_b')}
    del _L0_tok_all

    def _L0_attn_setup():
        import jax, jax.numpy as jnp
        import numpy as np
        BN_EPS = 1e-05
        key = jax.random.key(seed)
        ks = jax.random.split(key, 12)
        B, N, d_e, d_a = (16, 512, 64, 64)
        s_e = 1.0 / np.sqrt(d_e)
        return {'x': jax.random.normal(ks[0], (B, N, d_e), dtype=jnp.float32), 'Wq': jax.random.uniform(ks[1], (d_e, d_a), jnp.float32, -s_e, s_e), 'bq': jax.random.uniform(ks[2], (d_a,), jnp.float32, -s_e, s_e), 'Wk': jax.random.uniform(ks[3], (d_e, d_a), jnp.float32, -s_e, s_e), 'bk': jax.random.uniform(ks[4], (d_a,), jnp.float32, -s_e, s_e), 'Wv': jax.random.uniform(ks[5], (d_e, d_e), jnp.float32, -s_e, s_e), 'bv': jax.random.uniform(ks[6], (d_e,), jnp.float32, -s_e, s_e), 'Wl': jax.random.uniform(ks[7], (d_e, d_e), jnp.float32, -s_e, s_e), 'bl': jax.random.uniform(ks[8], (d_e,), jnp.float32, -s_e, s_e), 'gamma': jnp.ones((d_e,), jnp.float32), 'beta': jnp.zeros((d_e,), jnp.float32)}
    _L0_attn_all = _L0_attn_setup()
    _L0_attn_in = {k: v for k, v in _L0_attn_all.items() if k in ('Wq', 'bq', 'Wk', 'bk', 'Wv', 'bv', 'Wl', 'bl', 'gamma', 'beta')}
    del _L0_attn_all

    def _L0_ffn_setup():
        import jax, jax.numpy as jnp
        import numpy as np
        B, T, C = (64, 96, 64)
        NH, NKV = (4, 2)
        HD = C // NH
        NREP = NH // NKV
        NE, TOPK = (8, 2)
        HID = int(8 / 3 * C)
        EPS_RMS = 1e-06

        def _rope_tables(t_len):
            inv_freq = 1.0 / 10000.0 ** (np.arange(0, HD, 2, dtype=np.float32) / HD)
            t = np.arange(t_len, dtype=np.float32)
            freqs = np.outer(t, inv_freq)
            emb = np.concatenate([freqs, freqs], axis=-1)
            return (jnp.asarray(np.cos(emb)), jnp.asarray(np.sin(emb)))

        def _rotate_half(x):
            h = x.shape[-1] // 2
            return jnp.concatenate([-x[..., h:], x[..., :h]], axis=-1)

        def _rmsnorm(v, w):
            return v * jax.lax.rsqrt(jnp.mean(v * v, axis=-1, keepdims=True) + EPS_RMS) * w
        key = jax.random.key(seed)
        ks = jax.random.split(key, 10)
        s = lambda k, shape: jax.random.normal(k, shape, jnp.float32) * 0.02
        return {'x': jax.random.normal(ks[0], (B, T, C), jnp.float32), 'ln1_w': jnp.ones((C,), jnp.float32), 'ln2_w': jnp.ones((C,), jnp.float32), 'wq': s(ks[1], (NH * HD, C)), 'wk': s(ks[2], (NKV * HD, C)), 'wv': s(ks[3], (NKV * HD, C)), 'wo': s(ks[4], (C, C)), 'router_w': s(ks[5], (NE, C)), 'w1': s(ks[6], (NE, HID, C)), 'w2': s(ks[7], (NE, C, HID)), 'w3': s(ks[8], (NE, HID, C))}
    _L0_ffn_all = _L0_ffn_setup()
    _L0_ffn_in = {k: v for k, v in _L0_ffn_all.items() if k in ('ln1_w', 'ln2_w', 'wq', 'wk', 'wv', 'wo', 'router_w', 'w1', 'w2', 'w3')}
    del _L0_ffn_all

    def _L1_attn_setup():
        import jax, jax.numpy as jnp
        import numpy as np
        SEQ_LEN = 512
        EMBED_DIM = 64
        BATCH = 8
        LN_EPS = 1e-05

        def _layernorm(x, g, b):
            mu = jnp.mean(x, axis=-1, keepdims=True)
            var = jnp.mean(jnp.square(x - mu), axis=-1, keepdims=True)
            return (x - mu) * jax.lax.rsqrt(var + LN_EPS) * g + b
        key = jax.random.key(seed)
        ks = jax.random.split(key, 8)
        C = EMBED_DIM
        x = jax.random.normal(ks[0], (BATCH, SEQ_LEN, C), dtype=jnp.float32)
        qkv_w = jax.random.normal(ks[1], (C, 3 * C), dtype=jnp.float32) * 0.02
        qkv_b = jnp.zeros((3 * C,), dtype=jnp.float32)
        proj_w = jax.random.normal(ks[2], (C, C), dtype=jnp.float32) * 0.02
        proj_b = jnp.zeros((C,), dtype=jnp.float32)
        ln1_g = jnp.ones((C,), dtype=jnp.float32)
        ln1_b = jnp.zeros((C,), dtype=jnp.float32)
        ln2_g = jnp.ones((C,), dtype=jnp.float32)
        ln2_b = jnp.zeros((C,), dtype=jnp.float32)
        bias_table = jax.random.truncated_normal(ks[3], -2.0, 2.0, (2 * SEQ_LEN - 1,), dtype=jnp.float32) * 0.02
        scale = jnp.asarray(1.0 / np.sqrt(C), dtype=jnp.float32)
        return {'x': x, 'ln1_g': ln1_g, 'ln1_b': ln1_b, 'qkv_w': qkv_w, 'qkv_b': qkv_b, 'bias_table': bias_table, 'scale': scale, 'proj_w': proj_w, 'proj_b': proj_b, 'ln2_g': ln2_g, 'ln2_b': ln2_b}
    _L1_attn_all = _L1_attn_setup()
    _L1_attn_in = {k: v for k, v in _L1_attn_all.items() if k in ('ln1_g', 'ln1_b', 'qkv_w', 'qkv_b', 'bias_table', 'scale', 'proj_w', 'proj_b', 'ln2_g', 'ln2_b')}
    del _L1_attn_all

    def _L1_ffn_setup():
        import jax, jax.numpy as jnp
        import numpy as np
        C = 64
        HID = 256
        E = 8
        TEMP = 1.0
        key = jax.random.key(seed)
        ks = jax.random.split(key, 7)
        x = jax.random.normal(ks[0], (8, 4096, C), dtype=jnp.float32)
        W1 = jax.random.normal(ks[1], (C, HID), dtype=jnp.float32) * 0.02
        b1 = jnp.zeros((HID,), dtype=jnp.float32)
        Wg = jax.random.normal(ks[2], (HID, E), dtype=jnp.float32) * 0.02
        bg = jnp.zeros((E,), dtype=jnp.float32)
        Wd = jax.random.normal(ks[3], (E, HID, C), dtype=jnp.float32) * 0.02
        bd = jnp.zeros((E, C), dtype=jnp.float32)
        return {'x': x, 'W1': W1, 'b1': b1, 'Wg': Wg, 'bg': bg, 'Wd': Wd, 'bd': bd}
    _L1_ffn_all = _L1_ffn_setup()
    _L1_ffn_in = {k: v for k, v in _L1_ffn_all.items() if k in ('W1', 'b1', 'Wg', 'bg', 'Wd', 'bd')}
    del _L1_ffn_all

    def _L2_attn_setup():
        import jax, jax.numpy as jnp
        import numpy as np
        B, N, C = (8, 2048, 64)
        HEADS, DH, KR = (8, 32, 4)
        INNER = HEADS * DH
        FF = 4 * C
        EPS = 1e-05

        def layernorm(x, g, b):
            mu = jnp.mean(x, axis=-1, keepdims=True)
            var = jnp.mean((x - mu) ** 2, axis=-1, keepdims=True)
            return (x - mu) * jax.lax.rsqrt(var + EPS) * g + b
        key = jax.random.key(seed)
        ks = jax.random.split(key, 16)
        s = 0.02
        return {'x': jax.random.normal(ks[0], (B, N, C), jnp.float32), 'ln1_g': jnp.ones((C,), jnp.float32), 'ln1_b': jnp.zeros((C,), jnp.float32), 'Wx': jax.random.normal(ks[1], (C, INNER), jnp.float32) * s, 'bx': jnp.zeros((INNER,), jnp.float32), 'Wq': jax.random.normal(ks[2], (DH, KR), jnp.float32) * s, 'Wk': jax.random.normal(ks[3], (DH, KR), jnp.float32) * s, 'Wv': jax.random.normal(ks[4], (DH, DH), jnp.float32) * s, 'Wo': jax.random.normal(ks[5], (INNER, C), jnp.float32) * s, 'bo': jnp.zeros((C,), jnp.float32), 'ln2_g': jnp.ones((C,), jnp.float32), 'ln2_b': jnp.zeros((C,), jnp.float32), 'W1': jax.random.normal(ks[6], (C, FF), jnp.float32) * s, 'b1': jnp.zeros((FF,), jnp.float32), 'W2': jax.random.normal(ks[7], (FF, C), jnp.float32) * s, 'b2': jnp.zeros((C,), jnp.float32)}
    _L2_attn_all = _L2_attn_setup()
    _L2_attn_in = {k: v for k, v in _L2_attn_all.items() if k in ('ln1_g', 'ln1_b', 'Wx', 'bx', 'Wq', 'Wk', 'Wv', 'Wo', 'bo', 'ln2_g', 'ln2_b', 'W1', 'b1', 'W2', 'b2')}
    del _L2_attn_all

    def _L2_ffn_setup():
        import jax, jax.numpy as jnp
        import numpy as np
        B, A = (1024, 8)
        IN, OUT = (64, 64)
        SH1, SH2 = (64, 128)
        EH1, EH2 = (128, 64)
        E, TOPK = (4, 2)

        def _shared_mlp(x, W1, b1, W2, b2, W3, b3):
            h = jax.nn.relu(x @ W1 + b1)
            h = jax.nn.relu(h @ W2 + b2)
            return h @ W3 + b3

        def _experts_mlp(x, eW1, eb1, eW2, eb2, eW3, eb3):
            h = jax.nn.relu(jnp.einsum('baf,efh->ebah', x, eW1) + eb1[:, None, None, :])
            h = jax.nn.relu(jnp.einsum('ebah,ehg->ebag', h, eW2) + eb2[:, None, None, :])
            o = jnp.einsum('ebag,ego->ebao', h, eW3) + eb3[:, None, None, :]
            return jnp.moveaxis(o, 0, -1)
        key = jax.random.key(seed)
        ks = jax.random.split(key, 16)
        s = 0.05
        return {'x': jax.random.normal(ks[0], (B, A, IN), jnp.float32), 'sW1': jax.random.normal(ks[1], (IN, SH1), jnp.float32) * s, 'sb1': jnp.zeros((SH1,), jnp.float32), 'sW2': jax.random.normal(ks[2], (SH1, SH2), jnp.float32) * s, 'sb2': jnp.zeros((SH2,), jnp.float32), 'sW3': jax.random.normal(ks[3], (SH2, OUT), jnp.float32) * s, 'sb3': jnp.zeros((OUT,), jnp.float32), 'eW1': jax.random.normal(ks[4], (E, IN, EH1), jnp.float32) * s, 'eb1': jnp.zeros((E, EH1), jnp.float32), 'eW2': jax.random.normal(ks[5], (E, EH1, EH2), jnp.float32) * s, 'eb2': jnp.zeros((E, EH2), jnp.float32), 'eW3': jax.random.normal(ks[6], (E, EH2, OUT), jnp.float32) * s, 'eb3': jnp.zeros((E, OUT), jnp.float32), 'gW': jax.random.normal(ks[7], (IN, E), jnp.float32) * s, 'gb': jnp.zeros((E,), jnp.float32)}
    _L2_ffn_all = _L2_ffn_setup()
    _L2_ffn_in = {k: v for k, v in _L2_ffn_all.items() if k in ('sW1', 'sb1', 'sW2', 'sb2', 'sW3', 'sb3', 'eW1', 'eb1', 'eW2', 'eb2', 'eW3', 'eb3', 'gW', 'gb')}
    del _L2_ffn_all

    def _L3_attn_setup():
        import jax, jax.numpy as jnp
        import numpy as np
        B, S, F, H = (4, 256, 64, 8)
        SCALE = float(F) ** 0.5
        key = jax.random.key(seed)
        ks = jax.random.split(key, 5)
        return {'q_input': jax.random.normal(ks[0], (B, S, F), dtype=jnp.float32), 'Wq': jax.random.normal(ks[1], (F, F * H), dtype=jnp.float32) * 0.02, 'Wk': jax.random.normal(ks[2], (F, F * H), dtype=jnp.float32) * 0.02, 'Wv': jax.random.normal(ks[3], (F, F * H), dtype=jnp.float32) * 0.02, 'Wo': jax.random.normal(ks[4], (F * H, F), dtype=jnp.float32) * 0.02}
    _L3_attn_all = _L3_attn_setup()
    _L3_attn_in = {k: v for k, v in _L3_attn_all.items() if k in ('Wq', 'Wk', 'Wv', 'Wo')}
    del _L3_attn_all

    def _L3_ffn_setup():
        import jax, jax.numpy as jnp
        import numpy as np
        B, S, D, E, H, K = (4, 1024, 64, 8, 128, 2)
        key = jax.random.key(seed)
        ks = jax.random.split(key, 6)
        x = jax.random.normal(ks[0], (B, S, D), jnp.float32)
        Wg = jax.random.normal(ks[1], (D, E), jnp.float32) * 0.02
        bg = jnp.zeros((E,), jnp.float32)
        W1 = jax.random.normal(ks[2], (E, D, H), jnp.float32) * 0.02
        b1 = jnp.zeros((E, H), jnp.float32)
        W2 = jax.random.normal(ks[3], (E, H, D), jnp.float32) * 0.02
        b2 = jnp.zeros((E, D), jnp.float32)
        return {'x': x, 'Wg': Wg, 'bg': bg, 'W1': W1, 'b1': b1, 'W2': W2, 'b2': b2}
    _L3_ffn_all = _L3_ffn_setup()
    _L3_ffn_in = {k: v for k, v in _L3_ffn_all.items() if k in ('Wg', 'bg', 'W1', 'b1', 'W2', 'b2')}
    del _L3_ffn_all
    return {'x': x, 'L0_tok_input_grid': _L0_tok_in['input_grid'], 'L0_tok_P_w': _L0_tok_in['P_w'], 'L0_tok_P_b': _L0_tok_in['P_b'], 'L0_tok_spec_wr': _L0_tok_in['spec_wr'], 'L0_tok_spec_wi': _L0_tok_in['spec_wi'], 'L0_tok_conv_w': _L0_tok_in['conv_w'], 'L0_tok_conv_b': _L0_tok_in['conv_b'], 'L0_tok_Q1_w': _L0_tok_in['Q1_w'], 'L0_tok_Q1_b': _L0_tok_in['Q1_b'], 'L0_tok_Q2_w': _L0_tok_in['Q2_w'], 'L0_tok_Q2_b': _L0_tok_in['Q2_b'], 'L0_attn_Wq': _L0_attn_in['Wq'], 'L0_attn_bq': _L0_attn_in['bq'], 'L0_attn_Wk': _L0_attn_in['Wk'], 'L0_attn_bk': _L0_attn_in['bk'], 'L0_attn_Wv': _L0_attn_in['Wv'], 'L0_attn_bv': _L0_attn_in['bv'], 'L0_attn_Wl': _L0_attn_in['Wl'], 'L0_attn_bl': _L0_attn_in['bl'], 'L0_attn_gamma': _L0_attn_in['gamma'], 'L0_attn_beta': _L0_attn_in['beta'], 'L0_ffn_ln1_w': _L0_ffn_in['ln1_w'], 'L0_ffn_ln2_w': _L0_ffn_in['ln2_w'], 'L0_ffn_wq': _L0_ffn_in['wq'], 'L0_ffn_wk': _L0_ffn_in['wk'], 'L0_ffn_wv': _L0_ffn_in['wv'], 'L0_ffn_wo': _L0_ffn_in['wo'], 'L0_ffn_router_w': _L0_ffn_in['router_w'], 'L0_ffn_w1': _L0_ffn_in['w1'], 'L0_ffn_w2': _L0_ffn_in['w2'], 'L0_ffn_w3': _L0_ffn_in['w3'], 'L1_attn_ln1_g': _L1_attn_in['ln1_g'], 'L1_attn_ln1_b': _L1_attn_in['ln1_b'], 'L1_attn_qkv_w': _L1_attn_in['qkv_w'], 'L1_attn_qkv_b': _L1_attn_in['qkv_b'], 'L1_attn_bias_table': _L1_attn_in['bias_table'], 'L1_attn_scale': _L1_attn_in['scale'], 'L1_attn_proj_w': _L1_attn_in['proj_w'], 'L1_attn_proj_b': _L1_attn_in['proj_b'], 'L1_attn_ln2_g': _L1_attn_in['ln2_g'], 'L1_attn_ln2_b': _L1_attn_in['ln2_b'], 'L1_ffn_W1': _L1_ffn_in['W1'], 'L1_ffn_b1': _L1_ffn_in['b1'], 'L1_ffn_Wg': _L1_ffn_in['Wg'], 'L1_ffn_bg': _L1_ffn_in['bg'], 'L1_ffn_Wd': _L1_ffn_in['Wd'], 'L1_ffn_bd': _L1_ffn_in['bd'], 'L2_attn_ln1_g': _L2_attn_in['ln1_g'], 'L2_attn_ln1_b': _L2_attn_in['ln1_b'], 'L2_attn_Wx': _L2_attn_in['Wx'], 'L2_attn_bx': _L2_attn_in['bx'], 'L2_attn_Wq': _L2_attn_in['Wq'], 'L2_attn_Wk': _L2_attn_in['Wk'], 'L2_attn_Wv': _L2_attn_in['Wv'], 'L2_attn_Wo': _L2_attn_in['Wo'], 'L2_attn_bo': _L2_attn_in['bo'], 'L2_attn_ln2_g': _L2_attn_in['ln2_g'], 'L2_attn_ln2_b': _L2_attn_in['ln2_b'], 'L2_attn_W1': _L2_attn_in['W1'], 'L2_attn_b1': _L2_attn_in['b1'], 'L2_attn_W2': _L2_attn_in['W2'], 'L2_attn_b2': _L2_attn_in['b2'], 'L2_ffn_sW1': _L2_ffn_in['sW1'], 'L2_ffn_sb1': _L2_ffn_in['sb1'], 'L2_ffn_sW2': _L2_ffn_in['sW2'], 'L2_ffn_sb2': _L2_ffn_in['sb2'], 'L2_ffn_sW3': _L2_ffn_in['sW3'], 'L2_ffn_sb3': _L2_ffn_in['sb3'], 'L2_ffn_eW1': _L2_ffn_in['eW1'], 'L2_ffn_eb1': _L2_ffn_in['eb1'], 'L2_ffn_eW2': _L2_ffn_in['eW2'], 'L2_ffn_eb2': _L2_ffn_in['eb2'], 'L2_ffn_eW3': _L2_ffn_in['eW3'], 'L2_ffn_eb3': _L2_ffn_in['eb3'], 'L2_ffn_gW': _L2_ffn_in['gW'], 'L2_ffn_gb': _L2_ffn_in['gb'], 'L3_attn_Wq': _L3_attn_in['Wq'], 'L3_attn_Wk': _L3_attn_in['Wk'], 'L3_attn_Wv': _L3_attn_in['Wv'], 'L3_attn_Wo': _L3_attn_in['Wo'], 'L3_ffn_Wg': _L3_ffn_in['Wg'], 'L3_ffn_bg': _L3_ffn_in['bg'], 'L3_ffn_W1': _L3_ffn_in['W1'], 'L3_ffn_b1': _L3_ffn_in['b1'], 'L3_ffn_W2': _L3_ffn_in['W2'], 'L3_ffn_b2': _L3_ffn_in['b2']}

def reference(x, L0_tok_input_grid, L0_tok_P_w, L0_tok_P_b, L0_tok_spec_wr, L0_tok_spec_wi, L0_tok_conv_w, L0_tok_conv_b, L0_tok_Q1_w, L0_tok_Q1_b, L0_tok_Q2_w, L0_tok_Q2_b, L0_attn_Wq, L0_attn_bq, L0_attn_Wk, L0_attn_bk, L0_attn_Wv, L0_attn_bv, L0_attn_Wl, L0_attn_bl, L0_attn_gamma, L0_attn_beta, L0_ffn_ln1_w, L0_ffn_ln2_w, L0_ffn_wq, L0_ffn_wk, L0_ffn_wv, L0_ffn_wo, L0_ffn_router_w, L0_ffn_w1, L0_ffn_w2, L0_ffn_w3, L1_attn_ln1_g, L1_attn_ln1_b, L1_attn_qkv_w, L1_attn_qkv_b, L1_attn_bias_table, L1_attn_scale, L1_attn_proj_w, L1_attn_proj_b, L1_attn_ln2_g, L1_attn_ln2_b, L1_ffn_W1, L1_ffn_b1, L1_ffn_Wg, L1_ffn_bg, L1_ffn_Wd, L1_ffn_bd, L2_attn_ln1_g, L2_attn_ln1_b, L2_attn_Wx, L2_attn_bx, L2_attn_Wq, L2_attn_Wk, L2_attn_Wv, L2_attn_Wo, L2_attn_bo, L2_attn_ln2_g, L2_attn_ln2_b, L2_attn_W1, L2_attn_b1, L2_attn_W2, L2_attn_b2, L2_ffn_sW1, L2_ffn_sb1, L2_ffn_sW2, L2_ffn_sb2, L2_ffn_sW3, L2_ffn_sb3, L2_ffn_eW1, L2_ffn_eb1, L2_ffn_eW2, L2_ffn_eb2, L2_ffn_eW3, L2_ffn_eb3, L2_ffn_gW, L2_ffn_gb, L3_attn_Wq, L3_attn_Wk, L3_attn_Wv, L3_attn_Wo, L3_ffn_Wg, L3_ffn_bg, L3_ffn_W1, L3_ffn_b1, L3_ffn_W2, L3_ffn_b2):
    import jax
    import jax.numpy as jnp

    def _L0_tok_ref(x, input_grid, P_w, P_b, spec_wr, spec_wi, conv_w, conv_b, Q1_w, Q1_b, Q2_w, Q2_b):
        import jax, jax.numpy as jnp
        import numpy as np
        from jax import lax
        NEG_SLOPE = 0.01

        def leaky(v):
            return jnp.where(v >= 0, v, NEG_SLOPE * v)
        B, H, W, _ = x.shape
        nl, _, _, mx, my = spec_wr.shape
        grid = jnp.broadcast_to(input_grid[None], (B, H, W, input_grid.shape[-1]))
        h = jnp.concatenate([grid, x], axis=-1) @ P_w + P_b
        h = jnp.transpose(h, (0, 3, 1, 2))
        dn = ('NCHW', 'OIHW', 'NCHW')
        for i in range(nl):
            h_ft = jnp.fft.rfft2(h)
            w_c = spec_wr[i] + 1j * spec_wi[i]
            out_modes = jnp.einsum('bixy,ioxy->boxy', h_ft[:, :, :mx, :my], w_c)
            spec = jnp.fft.irfft2(out_modes, s=(H, W))
            conv = lax.conv_general_dilated(h, conv_w[i], (1, 1), 'SAME', dimension_numbers=dn)
            conv = conv + conv_b[i][None, :, None, None]
            h = leaky(spec + conv)
        h = jnp.transpose(h, (0, 2, 3, 1))
        h = leaky(h @ Q1_w + Q1_b)
        out = (h @ Q2_w + Q2_b)[..., 0]
        return out

    def _L0_attn_ref(x, Wq, bq, Wk, bk, Wv, bv, Wl, bl, gamma, beta):
        import jax, jax.numpy as jnp
        import numpy as np
        BN_EPS = 1e-05
        q = x @ Wq + bq
        k = x @ Wk + bk
        v = x @ Wv + bv
        d_a = q.shape[-1]
        score = jnp.einsum('bnd,bmd->bnm', q, k) / jnp.asarray(d_a, q.dtype)
        score = jax.nn.softmax(score, axis=2)
        attn = jnp.einsum('bnm,bmd->bnd', score, v)
        h = attn @ Wl + bl
        mean = jnp.mean(h, axis=(0, 1))
        var = jnp.mean((h - mean) ** 2, axis=(0, 1))
        y = jax.nn.relu((h - mean) * jax.lax.rsqrt(var + BN_EPS) * gamma + beta)
        return y + x

    def _L0_ffn_ref(x, ln1_w, ln2_w, wq, wk, wv, wo, router_w, w1, w2, w3):
        import jax, jax.numpy as jnp
        import numpy as np
        B, T, C = (64, 96, 64)
        NH, NKV = (4, 2)
        HD = C // NH
        NREP = NH // NKV
        NE, TOPK = (8, 2)
        HID = int(8 / 3 * C)
        EPS_RMS = 1e-06

        def _rope_tables(t_len):
            inv_freq = 1.0 / 10000.0 ** (np.arange(0, HD, 2, dtype=np.float32) / HD)
            t = np.arange(t_len, dtype=np.float32)
            freqs = np.outer(t, inv_freq)
            emb = np.concatenate([freqs, freqs], axis=-1)
            return (jnp.asarray(np.cos(emb)), jnp.asarray(np.sin(emb)))

        def _rotate_half(x):
            h = x.shape[-1] // 2
            return jnp.concatenate([-x[..., h:], x[..., :h]], axis=-1)

        def _rmsnorm(v, w):
            return v * jax.lax.rsqrt(jnp.mean(v * v, axis=-1, keepdims=True) + EPS_RMS) * w
        Bx, Tx, Cx = x.shape
        h = _rmsnorm(x, ln1_w)
        q = (h @ wq.T).reshape(Bx, Tx, NH, HD).transpose(0, 2, 1, 3)
        k = (h @ wk.T).reshape(Bx, Tx, NKV, HD).transpose(0, 2, 1, 3)
        v = (h @ wv.T).reshape(Bx, Tx, NKV, HD).transpose(0, 2, 1, 3)
        cos, sin = _rope_tables(Tx)
        cos, sin = (cos[None, None], sin[None, None])
        q = q * cos + _rotate_half(q) * sin
        k = k * cos + _rotate_half(k) * sin
        k = jnp.repeat(k, NREP, axis=1)
        v = jnp.repeat(v, NREP, axis=1)
        scores = jnp.einsum('bhtd,bhsd->bhts', q, k) / jnp.sqrt(jnp.float32(HD))
        causal = jnp.tril(jnp.ones((Tx, Tx), dtype=bool))
        scores = jnp.where(causal[None, None], scores, jnp.float32(-1e+30))
        att = jax.nn.softmax(scores, axis=-1)
        y = jnp.einsum('bhts,bhsd->bhtd', att, v).transpose(0, 2, 1, 3).reshape(Bx, Tx, Cx)
        x = x + y @ wo.T
        flat = _rmsnorm(x, ln2_w).reshape(-1, Cx)
        probs = jax.nn.softmax(flat @ router_w.T, axis=-1)
        tp, ti = jax.lax.top_k(probs, TOPK)
        tp = tp / (jnp.sum(tp, axis=-1, keepdims=True) + 1e-09)
        weights = jnp.sum(tp[..., None] * jax.nn.one_hot(ti, NE, dtype=flat.dtype), axis=1)
        out = jnp.zeros_like(flat)
        for e in range(NE):
            hh = jax.nn.silu(flat @ w1[e].T) * (flat @ w3[e].T)
            out = out + weights[:, e:e + 1] * (hh @ w2[e].T)
        return x + out.reshape(Bx, Tx, Cx)

    def _L1_attn_ref(x, ln1_g, ln1_b, qkv_w, qkv_b, bias_table, scale, proj_w, proj_b, ln2_g, ln2_b):
        import jax, jax.numpy as jnp
        import numpy as np
        SEQ_LEN = 512
        EMBED_DIM = 64
        BATCH = 8
        LN_EPS = 1e-05

        def _layernorm(x, g, b):
            mu = jnp.mean(x, axis=-1, keepdims=True)
            var = jnp.mean(jnp.square(x - mu), axis=-1, keepdims=True)
            return (x - mu) * jax.lax.rsqrt(var + LN_EPS) * g + b
        B, N, C = x.shape
        h = _layernorm(x, ln1_g, ln1_b)
        qkv = h @ qkv_w + qkv_b
        q, k, v = jnp.split(qkv, 3, axis=-1)
        coords = jnp.arange(N)
        rel_idx = coords[None, :] - coords[:, None] + (N - 1)
        rel_bias = bias_table[rel_idx]
        attn = jnp.einsum('bnc,bmc->bnm', q, k) + rel_bias
        attn = jax.nn.softmax(attn, axis=-1) * scale
        out = jnp.einsum('bnm,bmc->bnc', attn, v)
        out = out @ proj_w + proj_b
        out = _layernorm(out, ln2_g, ln2_b)
        return out

    def _L1_ffn_ref(x, W1, b1, Wg, bg, Wd, bd):
        import jax, jax.numpy as jnp
        import numpy as np
        C = 64
        HID = 256
        E = 8
        TEMP = 1.0
        orig_shape = x.shape
        xf = x.reshape(-1, orig_shape[-1])
        H = jax.nn.gelu(xf @ W1 + b1, approximate=False)
        probs = jax.nn.softmax((H @ Wg + bg) / TEMP, axis=-1)
        assign = jnp.argmax(probs, axis=-1)
        out = jnp.zeros_like(xf)
        for e in range(Wd.shape[0]):
            y = H @ Wd[e] + bd[e]
            sel = (assign == e)[:, None]
            out = out + jnp.where(sel, probs[:, e:e + 1] * y, 0.0)
        return out.reshape(orig_shape)

    def _L2_attn_ref(x, ln1_g, ln1_b, Wx, bx, Wq, Wk, Wv, Wo, bo, ln2_g, ln2_b, W1, b1, W2, b2):
        import jax, jax.numpy as jnp
        import numpy as np
        B, N, C = (8, 2048, 64)
        HEADS, DH, KR = (8, 32, 4)
        INNER = HEADS * DH
        FF = 4 * C
        EPS = 1e-05

        def layernorm(x, g, b):
            mu = jnp.mean(x, axis=-1, keepdims=True)
            var = jnp.mean((x - mu) ** 2, axis=-1, keepdims=True)
            return (x - mu) * jax.lax.rsqrt(var + EPS) * g + b
        b, n, c = x.shape
        h = layernorm(x, ln1_g, ln1_b)
        xm = h @ Wx + bx
        xm = xm.reshape(b, n, HEADS, DH).transpose(0, 2, 1, 3)
        q = jax.nn.softmax(xm @ Wq, axis=-1)
        k = jax.nn.softmax(xm @ Wk, axis=-2)
        v = xm @ Wv
        kv = jnp.einsum('bhnr,bhnd->bhrd', k, v)
        qkv = jnp.einsum('bhnr,bhrd->bhnd', q, kv)
        attn = qkv.transpose(0, 2, 1, 3).reshape(b, n, INNER) @ Wo + bo
        fx = attn + x
        h2 = layernorm(fx, ln2_g, ln2_b)
        m = jax.nn.gelu(h2 @ W1 + b1, approximate=False) @ W2 + b2
        return m + fx

    def _L2_ffn_ref(x, sW1, sb1, sW2, sb2, sW3, sb3, eW1, eb1, eW2, eb2, eW3, eb3, gW, gb):
        import jax, jax.numpy as jnp
        import numpy as np
        B, A = (1024, 8)
        IN, OUT = (64, 64)
        SH1, SH2 = (64, 128)
        EH1, EH2 = (128, 64)
        E, TOPK = (4, 2)

        def _shared_mlp(x, W1, b1, W2, b2, W3, b3):
            h = jax.nn.relu(x @ W1 + b1)
            h = jax.nn.relu(h @ W2 + b2)
            return h @ W3 + b3

        def _experts_mlp(x, eW1, eb1, eW2, eb2, eW3, eb3):
            h = jax.nn.relu(jnp.einsum('baf,efh->ebah', x, eW1) + eb1[:, None, None, :])
            h = jax.nn.relu(jnp.einsum('ebah,ehg->ebag', h, eW2) + eb2[:, None, None, :])
            o = jnp.einsum('ebag,ego->ebao', h, eW3) + eb3[:, None, None, :]
            return jnp.moveaxis(o, 0, -1)
        all_out = _experts_mlp(x, eW1, eb1, eW2, eb2, eW3, eb3)
        shared = _shared_mlp(x, sW1, sb1, sW2, sb2, sW3, sb3)
        gates = jax.nn.softmax(x @ gW + gb, axis=-1)
        topv, topi = jax.lax.top_k(gates, TOPK)
        topw = jax.nn.softmax(topv, axis=-1)
        sel = jnp.take_along_axis(all_out, topi[:, :, None, :], axis=-1)
        gated = jnp.sum(sel * topw[:, :, None, :], axis=-1)
        return shared + gated

    def _L3_attn_ref(q_input, Wq, Wk, Wv, Wo):
        import jax, jax.numpy as jnp
        import numpy as np
        B, S, F, H = (4, 256, 64, 8)
        SCALE = float(F) ** 0.5
        b, s, f = q_input.shape
        h = Wq.shape[1] // f
        q = (q_input.reshape(b * s, f) @ Wq).reshape(b, s, f, h)
        k = (q_input.reshape(b * s, f) @ Wk).reshape(b, s, f, h)
        v = (q_input.reshape(b * s, f) @ Wv).reshape(b, s, f, h)
        qkt = jnp.einsum('bifh,bjfh->bijh', q, k)
        attn = jax.nn.sigmoid(qkt * SCALE)
        wv = jnp.einsum('bijh,bjfh->bifh', attn, v)
        wv = wv.reshape(b * s, f * h)
        out = jax.nn.relu(wv @ Wo)
        return out.reshape(b, s, f)

    def _L3_ffn_ref(x, Wg, bg, W1, b1, W2, b2):
        import jax, jax.numpy as jnp
        import numpy as np
        B, S, D, E, H, K = (4, 1024, 64, 8, 128, 2)
        Bv, Sv, Dv = x.shape
        gate_scores = x @ Wg + bg
        _, idx = jax.lax.top_k(gate_scores, K)
        mask = jax.nn.one_hot(idx, E, dtype=x.dtype).sum(axis=-2)
        xf = x.reshape(-1, Dv)
        mf = mask.reshape(-1, E)
        h = jax.nn.gelu(jnp.einsum('td,edh->teh', xf, W1) + b1[None], approximate=False)
        y = jnp.einsum('teh,ehd->ted', h, W2) + b2[None]
        out = jnp.einsum('ted,te->td', y, mf)
        return out.reshape(Bv, Sv, Dv)
    h = _L0_tok_ref(x, L0_tok_input_grid, L0_tok_P_w, L0_tok_P_b, L0_tok_spec_wr, L0_tok_spec_wi, L0_tok_conv_w, L0_tok_conv_b, L0_tok_Q1_w, L0_tok_Q1_b, L0_tok_Q2_w, L0_tok_Q2_b)
    h = h + _L0_attn_ref(_layernorm(h, axis=-1), L0_attn_Wq, L0_attn_bq, L0_attn_Wk, L0_attn_bk, L0_attn_Wv, L0_attn_bv, L0_attn_Wl, L0_attn_bl, L0_attn_gamma, L0_attn_beta)
    h = h + _L0_ffn_ref(_layernorm(h, axis=-1), L0_ffn_ln1_w, L0_ffn_ln2_w, L0_ffn_wq, L0_ffn_wk, L0_ffn_wv, L0_ffn_wo, L0_ffn_router_w, L0_ffn_w1, L0_ffn_w2, L0_ffn_w3)
    h = h + _L1_attn_ref(_layernorm(h, axis=-1), L1_attn_ln1_g, L1_attn_ln1_b, L1_attn_qkv_w, L1_attn_qkv_b, L1_attn_bias_table, L1_attn_scale, L1_attn_proj_w, L1_attn_proj_b, L1_attn_ln2_g, L1_attn_ln2_b)
    h = h + _L1_ffn_ref(_layernorm(h, axis=-1), L1_ffn_W1, L1_ffn_b1, L1_ffn_Wg, L1_ffn_bg, L1_ffn_Wd, L1_ffn_bd)
    h = h + _L2_attn_ref(_layernorm(h, axis=-1), L2_attn_ln1_g, L2_attn_ln1_b, L2_attn_Wx, L2_attn_bx, L2_attn_Wq, L2_attn_Wk, L2_attn_Wv, L2_attn_Wo, L2_attn_bo, L2_attn_ln2_g, L2_attn_ln2_b, L2_attn_W1, L2_attn_b1, L2_attn_W2, L2_attn_b2)
    h = h + _L2_ffn_ref(_layernorm(h, axis=-1), L2_ffn_sW1, L2_ffn_sb1, L2_ffn_sW2, L2_ffn_sb2, L2_ffn_sW3, L2_ffn_sb3, L2_ffn_eW1, L2_ffn_eb1, L2_ffn_eW2, L2_ffn_eb2, L2_ffn_eW3, L2_ffn_eb3, L2_ffn_gW, L2_ffn_gb)
    h = h + _L3_attn_ref(_layernorm(h, axis=-1), L3_attn_Wq, L3_attn_Wk, L3_attn_Wv, L3_attn_Wo)
    h = h + _L3_ffn_ref(_layernorm(h, axis=-1), L3_ffn_Wg, L3_ffn_bg, L3_ffn_W1, L3_ffn_b1, L3_ffn_W2, L3_ffn_b2)
    return h

_drawn_inputs = setup_inputs


def setup_inputs(seed=0):
    import zlib

    import numpy as np

    out = dict(_drawn_inputs(seed))
    spreads = {'L0_attn_gamma': (1.0, 0.2),
     'L0_attn_beta': (0.0, 0.1),
     'L0_ffn_ln1_w': (1.0, 0.6),
     'L0_ffn_ln2_w': (1.0, 0.6),
     'L1_attn_ln1_g': (1.0, 0.6),
     'L1_attn_ln1_b': (0.0, 0.8),
     'L1_attn_qkv_b': (0.0, 0.8),
     'L1_attn_proj_b': (0.0, 0.1),
     'L1_attn_ln2_g': (1.0, 0.2),
     'L1_attn_ln2_b': (0.0, 0.1),
     'L1_ffn_b1': (0.0, 0.8),
     'L1_ffn_bg': (0.0, 0.8),
     'L1_ffn_bd': (0.0, 0.8),
     'L2_attn_ln1_g': (1.0, 0.6),
     'L2_attn_ln1_b': (0.0, 0.8),
     'L2_attn_bx': (0.0, 0.8),
     'L2_attn_bo': (0.0, 0.277),
     'L2_attn_ln2_g': (1.0, 0.6),
     'L2_attn_ln2_b': (0.0, 0.8),
     'L2_attn_b1': (0.0, 0.8),
     'L2_attn_b2': (0.0, 0.277),
     'L2_ffn_sb1': (0.0, 0.8),
     'L2_ffn_sb2': (0.0, 0.582),
     'L2_ffn_sb3': (0.0, 0.28),
     'L2_ffn_eb1': (0.0, 0.8),
     'L2_ffn_eb2': (0.0, 0.8),
     'L2_ffn_eb3': (0.0, 0.392),
     'L2_ffn_gb': (0.0, 0.8),
     'L3_ffn_bg': (0.0, 0.1),
     'L3_ffn_b1': (0.0, 0.8),
     'L3_ffn_b2': (0.0, 0.762)}
    factors = {'L0_tok_spec_wr': 8.0,
     'L0_tok_spec_wi': 8.0,
     'L0_attn_bq': 8.0,
     'L0_attn_bk': 200.0,
     'L0_attn_bv': 200.0,
     'L0_attn_bl': 200.0,
     'L0_ffn_wq': 8.0,
     'L0_ffn_wk': 8.0,
     'L0_ffn_wv': 7.961,
     'L0_ffn_wo': 7.644,
     'L0_ffn_router_w': 8.0,
     'L0_ffn_w1': 8.0,
     'L0_ffn_w2': 8.0,
     'L0_ffn_w3': 8.0,
     'L1_attn_qkv_w': 6.745,
     'L1_attn_bias_table': 8.0,
     'L1_attn_proj_w': 4.375,
     'L1_ffn_W1': 8.0,
     'L1_ffn_Wg': 8.0,
     'L1_ffn_Wd': 8.0,
     'L2_attn_Wx': 8.0,
     'L2_attn_Wq': 8.0,
     'L2_attn_Wk': 8.0,
     'L2_attn_Wv': 8.0,
     'L2_attn_Wo': 8.0,
     'L2_attn_W1': 6.685,
     'L2_attn_W2': 5.889,
     'L2_ffn_sW1': 5.457,
     'L2_ffn_sW2': 4.484,
     'L2_ffn_eW1': 8.0,
     'L2_ffn_eW2': 7.171,
     'L2_ffn_eW3': 5.695,
     'L2_ffn_gW': 3.625,
     'L3_ffn_W1': 8.0,
     'L3_ffn_W2': 7.412}
    for name, (base, spread) in spreads.items():
        noise = np.random.default_rng([zlib.crc32(name.encode()), seed]).standard_normal(out[name].shape)
        drawn = base * np.exp(spread * noise) if base else spread * noise
        out[name] = jnp.asarray(drawn.astype(out[name].dtype))
    for name, factor in factors.items():
        out[name] = (out[name] * factor).astype(out[name].dtype)
    return out
```

```python
import numpy as np
import concourse.bass as bass
from concourse import mybir
from contextlib import ExitStack

F32 = mybir.dt.float32
ACT = mybir.ActivationFunctionType
ALU = mybir.AluOpType
AX = mybir.AxisListType

IMGS, ROWS, COLS, WID, LAYERS = 128, 64, 64, 32, 4
MX, MY = 16, 16
J = ROWS // 2
PIX = J * COLS
MODES = 2 * MX * MY
CH = 512
NCH = PIX // CH
PAIRS = IMGS // 2
KXT = 4


def tokenizer_constants():
    j, w = np.arange(J), np.arange(COLS)
    kx, ky = np.arange(MX), np.arange(MY)
    row = 2 * j.reshape(J // 2, 2)
    ang = 2 * np.pi * (row[:, :, None, None, None] * kx[None, None, None, :, None] / ROWS
                       + w[None, None, :, None, None] * ky[None, None, None, None, :] / COLS)
    fwd = np.stack([np.cos(ang), -np.sin(ang)], 3)
    fwd = fwd.transpose(1, 2, 0, 3, 4, 5).reshape(128, J // 2, MODES)
    c = np.where(ky == 0, 1.0, 2.0) / (ROWS * COLS)
    ang = 2 * np.pi * (kx[:, None, None, None] * 2 * j[None, None, :, None] / ROWS
                       + ky[None, :, None, None] * w[None, None, None, :] / COLS)
    inv = np.stack([np.cos(ang), -np.sin(ang)], 2) * c[None, :, None, None, None]
    inv = inv.reshape(MX // KXT, 128, PIX).transpose(1, 0, 2)
    tw = np.zeros((2, 2, WID, MX, 2, 4))
    for si in range(2):
        for so in range(2):
            phi = 2 * np.pi * kx * (so - si) / ROWS
            a, b = np.cos(phi), np.sin(phi)
            for ri in range(2):
                sg = 1 if ri == 0 else -1
                tw[si, ri, :, :, so, 0] = sg * a
                tw[si, ri, :, :, so, 1] = -b
                tw[si, ri, :, :, so, 2] = a
                tw[si, ri, :, :, so, 3] = sg * b
    return (np.ascontiguousarray(fwd, np.float32), np.ascontiguousarray(inv, np.float32),
            np.ascontiguousarray(tw.reshape(128, MX, 8).transpose(1, 0, 2), np.float32),
            np.eye(128, dtype=np.float32))


def build_tokenizer(nc, x_pairs, grid_rows, embed_w, embed_b, spec_uv, conv_w, conv_b, q1_w, q1_b, q2_w, q2_b,
                    fwd_dram, inv_dram, tw_dram, eye_dram, tok, h_dram, g_dram, m_dram):
    with ExitStack() as ctx:
        sb = lambda n, s: ctx.enter_context(nc.sbuf_tensor(n, s, F32))
        pb = lambda n: ctx.enter_context(nc.psum_tensor(n, [128, CH], F32))
        sem = lambda n: ctx.enter_context(nc.semaphore(n))

        arena = sb("arena", [128, 2 * 8192])
        modes_q = [arena[:, 8192 * u:8192 * u + 8192].rearrange("p (n m) -> p n m", n=IMGS) for u in range(2)]
        rows_in = [arena[:, 4096 * u:4096 * u + 4096].rearrange("p (a n) -> p a n", a=2) for u in range(2)]
        rows_out = [arena[:, 8192 + 2048 * u:8192 + 2048 * u + 2048] for u in range(2)]
        fwd = sb("fwd_basis", [128, J // 2, MODES])
        inv = sb("inv_basis", [128, MX // KXT, PIX])
        eye = sb("eye", [128, 128])
        mode_tile = [sb(f"mode_tile{u}", [128, MX // KXT, 2, 64]) for u in range(2)]
        flipped = [sb(f"flipped{u}", [128, 4, 128]) for u in range(2)]
        scaled = [sb(f"scaled{u}", [128, CH]) for u in range(2)]
        modes_out = [sb(f"modes_out{u}", [128, MODES]) for u in range(2)]
        embed_bd = sb("embed_bd", [16, 128])
        embed_bias = sb("embed_bias", [128, 1])
        conv_bd = sb("conv_bd", [128, 3, 64])
        conv_bias = sb("conv_bias", [128, 1])
        conv_bias01 = sb("conv_bias01", [128, 1])
        q1_bd = sb("q1_bd", [128, 128])
        q1_bias = sb("q1_bias", [128, 1])
        q1_bias01 = sb("q1_bias01", [128, 1])
        q2_bd = sb("q2_bd", [128, 4])
        q2_bias = sb("q2_bias", [4, 1])
        uv = [sb(f"uv{u}", [128, 2, MY, WID]) for u in range(2)]
        twid = [sb(f"twid{u}", [128, 8]) for u in range(2)]
        partial = [sb(f"partial{u}", [128, MY, WID]) for u in range(2)]
        mix_w = [sb(f"mix_w{u}", [128, MY, 2, 2, WID]) for u in range(2)]
        mixed = [sb(f"mixed{u}", [128, MY * 128]) for u in range(2)]
        xg = [mixed[u][0:16, :] for u in range(2)]
        tok_out = [mix_w[u][0:4, :, :, :, :].rearrange("p y r s o -> p (y r s o)") for u in range(2)]

        zbank = [pb("zbank0"), pb("zbank1")]
        tbank = [pb("tbank0"), pb("tbank1")]
        gbank = [pb("gbank0"), pb("gbank1")]
        mbank = [zbank[0], zbank[1], tbank[0], tbank[1]]

        consts = sem("consts_loaded")
        zeroed = sem("tiles_zeroed")
        zeroed_v = sem("borders_zeroed")
        conv_in = sem("conv_weights_loaded")
        bias_ready = sem("bias_scaled")
        q_ready = sem("q_bias_scaled")
        xg_in = [sem(f"xg_loaded{u}") for u in range(2)]
        rows_loaded = [sem(f"rows_loaded{u}") for u in range(2)]
        modes_loaded = [sem(f"modes_loaded{u}") for u in range(2)]
        z_done = sem("z_done")
        z_scaled = sem("z_scaled")
        h_new = sem("h_new")
        flip_done = sem("flip_done")
        flip_copied = sem("flip_copied")
        fwd_done = sem("fwd_done")
        g_ready = sem("g_ready")
        h_stored = [sem(f"h_stored{u}") for u in range(2)]
        g_stored = [sem(f"g_stored{u}") for u in range(2)]
        q1_done = sem("q1_done")
        q1_scaled = sem("q1_scaled")
        q1_leaky = sem("q1_leaky")
        q2_done = sem("q2_done")
        tok_ready = sem("tok_ready")
        tok_stored = [sem(f"tok_stored{u}") for u in range(2)]
        quarter_in = [sem(f"quarter_loaded{u}") for u in range(2)]
        uv_in = [sem(f"uv_loaded{u}") for u in range(2)]
        part_ready = sem("partial_ready")
        mixw_ready = sem("mix_weights_ready")
        mix_done = sem("mix_done")
        mixed_act = sem("mixed_copied_act")
        mixed_dve = sem("mixed_copied_dve")
        m_stored = [sem(f"m_stored{u}") for u in range(2)]

        NP = PAIRS // 2

        def over_pairs(eng, body):
            body(0)
            with eng.Fori(1, NP) as i:
                body(i)

        def sp_constants(sp):
            n = 0
            def load(dst, src):
                nonlocal n
                sp.dma_start(dst, src).then_inc(consts, 16)
                n += 1
            load(fwd[:], fwd_dram)
            load(inv[:], inv_dram)
            load(eye[:], eye_dram)
            for u in range(2):
                load(xg[u][0:4, :], grid_rows)
            sp.wait_ge(zeroed, 4)
            for a in range(2):
                for s in range(2):
                    col = slice(64 * a + 32 * s, 64 * a + 32 * s + 32)
                    load(embed_bd[2 * s:2 * s + 2, col], embed_w[0:2, :])
                    load(embed_bd[4 + 6 * a + 3 * s:4 + 6 * a + 3 * s + 3, col], embed_w[2:5, :])
            for k in range(4):
                part = slice(32 * k, 32 * k + 32)
                load(embed_bias[part, :], embed_b.rearrange("(c o) -> c o", o=1))
                load(q1_bias[part, :], q1_b.rearrange("(c o) -> c o", o=1))
                load(q1_bd[part, part], q1_w)
                load(q2_bd[part, k:k + 1], q2_w)
                load(q2_bias[k:k + 1, :], q2_b.rearrange("(c o) -> c o", o=1))
            assert n == NCONSTS, n

        NCONSTS = 5 + 8 + 20

        def sp_conv_weights(sp, l):
            for so in range(2):
                for dy in range(3):
                    sp.dma_start(conv_bd[32 * (so + dy):32 * (so + dy) + 32, :, 32 * so:32 * so + 32],
                                 conv_w[bass.ds(l, 1), dy, :, :, :].rearrange("l c x o -> (l c) x o"))\
                        .then_inc(conv_in, 16)
            for k in range(4):
                sp.dma_start(conv_bias[32 * k:32 * k + 32, :],
                             conv_b[bass.ds(l, 1), :].rearrange("l (c o) -> (l c) o", o=1)).then_inc(conv_in, 16)
        NCONV = 10

        def sp_store_pair(sp, u, n, before):
            sp.wait_ge(h_new, NCH * (before + n + 1))
            sp.wait_ge(zeroed, 4)
            sp.dma_start(h_dram[bass.ds(n, 1), :, :, :, :].rearrange("a g s c n -> (a g s c) n"),
                         rows_out[u]).then_inc(h_stored[u], 16)
            sp.wait_ge(g_ready, before + n + 1)
            sp.wait_ge(zeroed, 4)
            sp.dma_start(g_dram[bass.ds(2 * n, 2), :, :, :, :].rearrange("a s c r m -> (a s c) (r m)"),
                         modes_out[u][:]).then_inc(g_stored[u], 16)

        def sp_store_tokens(sp, u, n):
            sp.wait_ge(tok_ready, NCH * (n + 1))
            sp.wait_ge(zeroed, 4)
            for a in range(2):
                sp.dma_start(tok[bass.ds(2 * n + a, 1), :, :, :].rearrange("g s j w -> (g s) j w"),
                             tok_out[u][2 * a:2 * a + 2, :].rearrange("p (j w) -> p j w", w=COLS))\
                    .then_inc(tok_stored[u], 16)

        def sp_embed(sp):
            def body(i):
                for u in range(2):
                    n = 2 * i + u
                    if not isinstance(i, int):
                        sp.wait_ge(z_done, NCH * (n - 1))
                        sp.wait_ge(zeroed, 4)
                    sp.dma_start(xg[u][4:16, :], x_pairs[bass.ds(n, 1), :, :].rearrange("a p n -> (a p) n"))\
                        .then_inc(xg_in[u], 16)
                    if not (isinstance(n, int) and n == 0):
                        sp_store_pair(sp, 1 - u, n - 1, 0)
            over_pairs(sp, body)
            sp_store_pair(sp, 1, PAIRS - 1, 0)

        def sp_layer(sp, l, last):
            for u in range(2):
                sp.wait_ge(m_stored[u], 16 * 8 * (l + 1))
                sp.wait_ge(zeroed, 4)
            sp.wait_ge(zeroed_v, l + 1)
            sp.wait_ge(zeroed, 4)
            def body(i):
                for u in range(2):
                    n = 2 * i + u
                    sp.wait_ge(z_done, NCH * ((l + 1) * PAIRS + n - 1))
                    sp.wait_ge(zeroed, 4)
                    pair = h_dram[bass.ds(n, 1), :, :, :, :]
                    sp.dma_start(rows_in[u][32:96, :, :], pair.rearrange("a g s c n -> (s c) (a g) n"))\
                        .then_inc(rows_loaded[u], 16)
                    sp.dma_start(rows_in[u][0:32, :, COLS:PIX],
                                 pair[:, :, 1, :, 0:PIX - COLS].rearrange("a g c n -> c (a g) n"))\
                        .then_inc(rows_loaded[u], 16)
                    sp.dma_start(rows_in[u][96:128, :, 0:PIX - COLS],
                                 pair[:, :, 0, :, COLS:PIX].rearrange("a g c n -> c (a g) n"))\
                        .then_inc(rows_loaded[u], 16)
                    for a in range(2):
                        sp.dma_start(mode_tile[u][:, :, a, :],
                                     m_dram[bass.ds(n, 1), a, :, :].rearrange("x (t p) c -> p (x t) c", p=128))\
                            .then_inc(modes_loaded[u], 16)
                    if not (isinstance(n, int) and n == 0):
                        store(1 - u, n - 1)
            def store(u, n):
                if last:
                    sp_store_tokens(sp, u, n)
                else:
                    sp_store_pair(sp, u, n, PAIRS * (l + 1))
            over_pairs(sp, body)
            store(1, PAIRS - 1)

        def sp_mix(sp, l):
            def store_mixed(kx):
                sp.wait_ge(mixed_act, 32 * l + 2 * (kx + 1))
                sp.wait_ge(zeroed, 4)
                sp.wait_ge(mixed_dve, 32 * l + 2 * (kx + 1))
                sp.wait_ge(zeroed, 4)
                sp.dma_start(m_dram[:, :, 32 * kx:32 * kx + 32, :].rearrange("n g m c -> (n g) (m c)"),
                             mixed[kx % 2][:]).then_inc(m_stored[kx % 2], 16)
            for u in range(2):
                sp.wait_ge(g_stored[u], 16 * NP * (l + 1))
                sp.wait_ge(zeroed, 4)
            sp.wait_ge(z_done, NCH * PAIRS * (l + 1))
            sp.wait_ge(zeroed, 4)
            for u in range(2):
                sp.wait_ge(h_stored[u], 16 * NP * (l + 1))
                sp.wait_ge(zeroed, 4)
            for q in range(4):
                u = q % 2
                if q >= 2:
                    sp.wait_ge(mix_done, 64 * l + 16 * (q - 1))
                    sp.wait_ge(zeroed, 4)
                for s in range(2):
                    for ri in range(2):
                        p = 64 * s + 32 * ri
                        sp.dma_start(modes_q[u][p:p + 32, :, :],
                                     g_dram[:, s, :, ri, 64 * q:64 * q + 64].rearrange("n c m -> c n m"))\
                            .then_inc(quarter_in[u], 16)
                for k in range(4):
                    kx = 4 * q + k
                    v = kx % 2
                    if kx >= 2:
                        store_mixed(kx - 2)
                    if kx >= 2:
                        sp.wait_ge(mixw_ready, 64 * l + 4 * (kx - 1))
                        sp.wait_ge(zeroed, 4)
                    for s in range(2):
                        sp.dma_start(uv[v][64 * s:64 * s + 64, :, :, :].rearrange("p a y o -> p (a y o)"),
                                     spec_uv[bass.ds(l, 1), kx, :, :].rearrange("l p n -> (l p) n"))\
                            .then_inc(uv_in[v], 16)
                    sp.dma_start(twid[v][:], tw_dram[kx, :, :]).then_inc(uv_in[v], 16)
            store_mixed(MX - 2)
            store_mixed(MX - 1)

        block = ctx.enter_context(nc.Block())

        @block.sync
        def _(sp):
            sp_constants(sp)
            sp_embed(sp)
            def layer(l, last):
                sp.wait_ge(z_done, NCH * PAIRS * (l + 1))
                sp.wait_ge(zeroed, 4)
                sp.wait_ge(h_new, NCH * PAIRS * (l + 1))
                sp.wait_ge(zeroed, 4)
                sp_conv_weights(sp, l)
                sp_mix(sp, l)
                sp_layer(sp, l, last)
            with sp.Fori(0, LAYERS - 1) as l:
                layer(l, False)
            layer(LAYERS - 1, True)
            for u in range(2):
                sp.wait_ge(tok_stored[u], 32 * NP)
                sp.wait_ge(h_stored[u], 16 * NP * LAYERS)
                sp.wait_ge(g_stored[u], 16 * NP * LAYERS)
                sp.wait_ge(m_stored[u], 16 * 8 * LAYERS)

        @block.gpsimd
        def _(pool):
            nc.gpsimd.memset(embed_bd[:], 0.0).then_inc(zeroed, 1)
            nc.gpsimd.memset(q1_bd[:], 0.0).then_inc(zeroed, 1)
            nc.gpsimd.memset(q2_bd[:], 0.0).then_inc(zeroed, 1)
            nc.gpsimd.memset(conv_bd[:], 0.0).then_inc(zeroed, 1)

        def pe_flip(rows, c, u, k):
            nc_t = nc.tensor
            for q in range(4):
                last = nc_t.transpose(tbank[c % 2][:, 128 * q:128 * q + 128], rows[:, CH * c + 128 * q:CH * c + 128 * q + 128],
                                      eye[:])
            last.then_inc(flip_done, 1)

        def pe_pair(pe, u, i, kind, l):
            n = 2 * i + u
            base = n if kind == "embed" else n + PAIRS * (l + 1)
            def z(c):
                k = NCH * base + c
                if not (isinstance(k, int) and k < 2):
                    pe.wait_ge(h_new, k - 1)
                bank = zbank[c % 2]
                if kind == "embed":
                    if c == 0:
                        pe.wait_ge(xg_in[u], 16 * (i + 1))
                    nc.tensor.matmul(bank[:], embed_bd[:], xg[u][:, CH * c:CH * c + CH], start=True, stop=True)\
                        .then_inc(z_done, 1)
                    return
                if c == 0:
                    pe.wait_ge(modes_loaded[u], 32 * (i + NP * l + 1))
                    pe.wait_ge(rows_loaded[u], 48 * (i + NP * l + 1))
                for t in range(MX // KXT):
                    nc.tensor.matmul(bank[:], mode_tile[u][:, t, :, :].rearrange("p a c -> p (a c)"),
                                     inv[:, t, CH * c:CH * c + CH], start=(t == 0), stop=False)
                jw = lambda ap: ap.rearrange("p (j w) -> p j w", w=COLS)
                for a in range(2):
                    out = jw(bank[64 * a:64 * a + 64, :])
                    src = jw(rows_in[u][:, a, CH * c:CH * c + CH])
                    nc.tensor.matmul(out, conv_bd[:, 1, :], src, start=False, stop=False)
                    nc.tensor.matmul(out[:, :, 1:COLS], conv_bd[:, 0, :], src[:, :, 0:COLS - 1], start=False, stop=False)
                    last = nc.tensor.matmul(out[:, :, 0:COLS - 1], conv_bd[:, 2, :], src[:, :, 1:COLS],
                                            start=False, stop=True)
                last.then_inc(z_done, 1)

            def flip(c):
                k = NCH * base + c
                pe.wait_ge(h_new, k + 1)
                if not (isinstance(k, int) and k < 2):
                    pe.wait_ge(flip_copied, k - 1)
                pe_flip(rows_out[u], c, u, k)

            def forward(c):
                k = NCH * base + c
                pe.wait_ge(flip_copied, k + 1)
                if c == 0 and not (isinstance(base, int) and base < 2):
                    pe.wait_ge(g_ready, base - 1)
                for q in range(4):
                    last = nc.tensor.matmul(gbank[u][:], flipped[c % 2][:, q, :], fwd[:, 4 * c + q, :],
                                            start=(c == 0 and q == 0), stop=(c == NCH - 1 and q == 3))
                last.then_inc(fwd_done, 1)

            def q1(c):
                k = NCH * n + c
                pe.wait_ge(h_new, NCH * base + c + 1)
                if c < 2:
                    pe.wait_ge(flip_copied, NCH * PAIRS * LAYERS)
                if not (isinstance(k, int) and k < 2):
                    pe.wait_ge(q1_leaky, k - 1)
                nc.tensor.matmul(tbank[c % 2][:], q1_bd[:], rows_out[u][:, CH * c:CH * c + CH], start=True, stop=True)\
                    .then_inc(q1_done, 1)

            def q2(c):
                k = NCH * n + c
                pe.wait_ge(q1_leaky, k + 1)
                if not (isinstance(k, int) and k < 2):
                    pe.wait_ge(tok_ready, k - 1)
                nc.tensor.matmul(gbank[c % 2][0:4, :], q2_bd[:], flipped[c % 2][:].rearrange("p a b -> p (a b)"),
                                 start=True, stop=True).then_inc(q2_done, 1)

            one, two = (q1, q2) if kind == "last" else (flip, forward)
            z(0)
            z(1)
            one(0)
            z(2)
            one(1)
            two(0)
            z(3)
            one(2)
            two(1)
            one(3)
            two(2)
            two(3)

        @block.tensor
        def _(pe):
            pe.wait_ge(consts, 16 * NCONSTS)
            def run(kind, l):
                def body(i):
                    for u in range(2):
                        pe_pair(pe, u, i, kind, l)
                over_pairs(pe, body)
            def mix(l):
                pe.wait_ge(h_new, NCH * PAIRS * (l + 1))
                pe.wait_ge(flip_copied, NCH * PAIRS * (l + 1))
                for kx in range(MX):
                    q = kx // 4
                    if kx % 4 == 0:
                        pe.wait_ge(quarter_in[q % 2], 16 * 4 * (2 * l + q // 2 + 1))
                    pe.wait_ge(mixw_ready, 64 * l + 4 * (kx + 1))
                    for y in range(4):
                        if kx >= 1:
                            pe.wait_ge(mixed_act if y % 2 == 0 else mixed_dve, 32 * l + 2 * kx - 1 + y // 2)
                        for yy in range(4):
                            ky = 4 * y + yy
                            m = 16 * (kx % 4) + ky
                            last = nc.tensor.matmul(mbank[y][:, 128 * yy:128 * yy + 128], modes_q[q % 2][:, :, m],
                                                    mix_w[kx % 2][:, ky, :, :, :].rearrange("p r s o -> p (r s o)"),
                                                    start=True, stop=True)
                        last.then_inc(mix_done, 1)
            run("embed", 0)
            def mix_out(l):
                pe.wait_ge(mixed_act, 32 * (l + 1))
                pe.wait_ge(mixed_dve, 32 * (l + 1))
            with pe.Fori(0, LAYERS - 1) as l:
                mix(l)
                mix_out(l)
                pe.wait_ge(conv_in, 16 * NCONV * (l + 1))
                run("mid", l)
            mix(LAYERS - 1)
            mix_out(LAYERS - 1)
            pe.wait_ge(conv_in, 16 * NCONV * LAYERS)
            run("last", LAYERS - 1)

        @block.scalar
        def _(act):
            def pair(u, n, kind, l):
                base = n if kind == "embed" else n + PAIRS * (l + 1)
                def scale_z(c):
                    act.wait_ge(z_done, NCH * base + c + 1)
                    nc.scalar.activation(scaled[c % 2][:], zbank[c % 2][:], ACT.Identity, bias=conv_bias01[:],
                                         scale=0.01).then_inc(z_scaled, 1)
                def copy_flip(c):
                    k = NCH * base + c
                    act.wait_ge(flip_done, k + 1)
                    if not (isinstance(k, int) and k < 2):
                        act.wait_ge(fwd_done, k - 1)
                    nc.scalar.activation(flipped[c % 2][:].rearrange("p a b -> p (a b)"), tbank[c % 2][:],
                                         ACT.Identity).then_inc(flip_copied, 1)
                def scale_q1(c):
                    k = NCH * n + c
                    act.wait_ge(q1_done, k + 1)
                    nc.scalar.activation(modes_out[c % 2][:], tbank[c % 2][:], ACT.Identity, bias=q1_bias01[:],
                                         scale=0.01).then_inc(q1_scaled, 1)
                for c in range(NCH + 1):
                    if c < NCH and kind != "embed":
                        if c < 2 and not isinstance(n, int) or True:
                            act.wait_ge(h_new, NCH * base + c - 1)
                        scale_z(c)
                    if c >= 1:
                        if kind == "last":
                            if c <= 2:
                                act.wait_ge(g_stored[0], 16 * NP * LAYERS)
                                act.wait_ge(g_stored[1], 16 * NP * LAYERS)
                            if not (isinstance(n, int) and NCH * n + c - 1 < 2):
                                act.wait_ge(q1_leaky, NCH * n + c - 2)
                            scale_q1(c - 1)
                        else:
                            copy_flip(c - 1)

            def run(kind, l):
                def body(i):
                    for u in range(2):
                        pair(u, 2 * i + u, kind, l)
                over_pairs(act, body)

            def mix(l):
                for kx in range(MX + 1):
                    if kx < MX:
                        v = kx % 2
                        act.wait_ge(uv_in[v], 48 * (8 * l + kx // 2 + 1))
                        for k, (so, r) in enumerate([(0, 0), (0, 1), (1, 0), (1, 1)]):
                            g = 4 * kx + k
                            if g >= 2:
                                act.wait_ge(mixw_ready, 64 * l + g - 1)
                            nc.scalar.activation(partial[k % 2][:], uv[v][:, r, :, :], ACT.Identity,
                                                 scale=twid[v][:, 4 * so + 2 * r:4 * so + 2 * r + 1])\
                                .then_inc(part_ready, 1)
                    if kx >= 1:
                        m = kx - 1
                        for y in (0, 2):
                            act.wait_ge(mix_done, 64 * l + 4 * m + y + 1)
                            if m >= 2:
                                act.wait_ge(m_stored[m % 2], 16 * (8 * l + m // 2))
                            nc.scalar.activation(mixed[m % 2][:, CH * y:CH * y + CH], mbank[y][:], ACT.Identity)\
                                .then_inc(mixed_act, 1)

            def layer(l, kind):
                mix(l)
                act.wait_ge(bias_ready, l + 1)
                run(kind, l)
            run("embed", 0)
            with act.Fori(0, LAYERS - 1) as l:
                layer(l, "mid")
            act.wait_ge(q_ready, 1)
            layer(LAYERS - 1, "last")

        @block.vector
        def _(dve):
            def pair(u, n, kind, l):
                base = n if kind == "embed" else n + PAIRS * (l + 1)
                def new_rows(c):
                    k = NCH * base + c
                    if c == 0 and not (isinstance(base, int) and base < 2):
                        dve.wait_ge(h_stored[u], 16 * stores_before(u, l, kind))
                        if kind == "last":
                            if not isinstance(n, int):
                                dve.wait_ge(q1_done, NCH * (n - 1))
                        else:
                            dve.wait_ge(flip_done, NCH * (base - 1))
                    out = rows_out[u][:, CH * c:CH * c + CH]
                    if kind == "embed":
                        dve.wait_ge(z_done, k + 1)
                        nc.vector.tensor_scalar(out, zbank[c % 2][:], embed_bias[:], None, ALU.add).then_inc(h_new, 1)
                    else:
                        dve.wait_ge(z_scaled, k + 1 - NCH * PAIRS)
                        nc.vector.scalar_tensor_tensor(out=out, in0=zbank[c % 2][:], scalar=conv_bias[:],
                                                       in1=scaled[c % 2][:], op0=ALU.add, op1=ALU.max)\
                            .then_inc(h_new, 1)
                def head(c):
                    k = NCH * n + c
                    dve.wait_ge(q1_scaled, k + 1)
                    if not (isinstance(k, int) and k < 2):
                        dve.wait_ge(q2_done, k - 1)
                    nc.vector.scalar_tensor_tensor(out=flipped[c % 2][:].rearrange("p a b -> p (a b)"),
                                                   in0=tbank[c % 2][:], scalar=q1_bias[:], in1=modes_out[c % 2][:],
                                                   op0=ALU.add, op1=ALU.max).then_inc(q1_leaky, 1)
                def tokens(c):
                    k = NCH * n + c
                    dve.wait_ge(q2_done, k + 1)
                    if c == 0 and not isinstance(n, int):
                        dve.wait_ge(tok_stored[u], 32 * cur[0])
                    nc.vector.tensor_scalar(tok_out[u][:, CH * c:CH * c + CH], gbank[c % 2][0:4, :], q2_bias[:], None,
                                            ALU.add).then_inc(tok_ready, 1)
                if kind == "last":
                    for c in range(NCH + 2):
                        if c < NCH:
                            new_rows(c)
                        if 1 <= c <= NCH:
                            head(c - 1)
                        if c >= 2:
                            tokens(c - 2)
                else:
                    for c in range(NCH):
                        new_rows(c)
                    dve.wait_ge(fwd_done, NCH * (base + 1))
                    if not (isinstance(base, int) and base < 2):
                        dve.wait_ge(g_stored[u], 16 * stores_before(u, l, kind))
                    nc.vector.tensor_copy(modes_out[u][:], gbank[u][:]).then_inc(g_ready, 1)

            cur = [0]
            def stores_before(u, l, kind):
                return cur[0] if kind == "embed" else (NP * LAYERS if kind == "last" else cur[0] + NP * (l + 1))

            def run(kind, l):
                def body(i):
                    cur[0] = i
                    for u in range(2):
                        pair(u, 2 * i + u, kind, l)
                over_pairs(dve, body)

            def mix(l):
                for kx in range(MX + 1):
                    if kx < MX:
                        v = kx % 2
                        if kx >= 2:
                            dve.wait_ge(mix_done, 64 * l + 4 * (kx - 1))
                        dve.wait_ge(uv_in[v], 48 * (8 * l + kx // 2 + 1))
                        for k, (so, r) in enumerate([(0, 0), (0, 1), (1, 0), (1, 1)]):
                            dve.wait_ge(part_ready, 64 * l + 4 * kx + k + 1)
                            nc.vector.scalar_tensor_tensor(out=mix_w[v][:, :, r, so, :], in0=uv[v][:, 1 - r, :, :],
                                                           scalar=twid[v][:, 4 * so + 2 * r + 1:4 * so + 2 * r + 2],
                                                           in1=partial[k % 2][:], op0=ALU.mult, op1=ALU.add)\
                                .then_inc(mixw_ready, 1)
                    if kx >= 1:
                        m = kx - 1
                        for y in (1, 3):
                            dve.wait_ge(mix_done, 64 * l + 4 * m + y + 1)
                            if m >= 2:
                                dve.wait_ge(m_stored[m % 2], 16 * (8 * l + m // 2))
                            nc.vector.tensor_copy(mixed[m % 2][:, CH * y:CH * y + CH], mbank[y][:]).then_inc(mixed_dve, 1)
                dve.wait_ge(mix_done, 64 * (l + 1))
                for u in range(2):
                    nc.vector.memset(rows_in[u][0:32, :, 0:COLS], 0.0)
                    last = nc.vector.memset(rows_in[u][96:128, :, PIX - COLS:PIX], 0.0)
                last.then_inc(zeroed_v, 1)
                dve.wait_ge(conv_in, 16 * NCONV * (l + 1))
                nc.vector.tensor_scalar(conv_bias01[:], conv_bias[:], 0.01, None, ALU.mult).then_inc(bias_ready, 1)

            dve.wait_ge(consts, 16 * NCONSTS)
            nc.vector.tensor_scalar(q1_bias01[:], q1_bias[:], 0.01, None, ALU.mult).then_inc(q_ready, 1)
            run("embed", 0)
            with dve.Fori(0, LAYERS - 1) as l:
                mix(l)
                run("mid", l)
            mix(LAYERS - 1)
            run("last", LAYERS - 1)


TOKENS, DIM, SEQ = 8192, 64, 64
U = 2
R = range(U)
T = 4
BLK = 128 * T
ITERS = TOKENS // (BLK * U)
BATCHES = BLK // SEQ
HID = 170
NTILE = -(-8 * HID // 128)


def block_constants():
    c = {}
    c["eye"] = np.eye(128)
    c["mhalf"] = np.full((128, 4), -0.5)
    hd = 16
    inv_freq = 1.0 / 10000.0 ** (np.arange(0, hd, 2, dtype=np.float32) / hd)
    freqs = np.outer(np.arange(SEQ, dtype=np.float32), inv_freq)
    emb = np.concatenate([freqs, freqs], -1).astype(np.float32)
    sign = np.where(np.arange(hd) < hd // 2, -1.0, 1.0)
    c["cos"] = np.tile(np.cos(emb).T, (4, 1))
    c["sin"] = np.tile(np.sin(emb).T * sign[:, None], (4, 1))
    c["headmask"] = np.kron(np.eye(4), np.ones((16, 1)))
    n = np.arange(128) % SEQ
    c["causal"] = np.where(np.arange(SEQ)[None, :] <= n[:, None], 0.0, -1e30)
    e = np.arange(8)
    c["before"] = np.tile((e[None, :] < e[:, None]).astype(np.float32).reshape(1, 64), (128, 1))
    e = np.arange(4)
    c["before4"] = np.tile((e[None, :] < e[:, None]).astype(np.float32).reshape(1, 16), (128, 1))
    own = np.zeros((8, NTILE * 128))
    for e in range(8):
        own[e, e * HID:(e + 1) * HID] = 1.0
    c["expand"] = own
    c["diag32"] = np.tile(np.kron(np.eye(8), np.ones((4, 32))), (4, 1))
    c["ones"] = np.ones((1, BLK))
    return c


def block_weights(i):
    w = {}
    col = lambda v: np.asarray(v).reshape(-1, 1)
    row = lambda v: np.broadcast_to(np.asarray(v).reshape(1, -1), (128, np.asarray(v).size))
    aug = lambda m, b: np.concatenate([np.asarray(m), np.asarray(b).reshape(1, -1)], 0)
    a = "L0_attn_"
    for k, b in (("q", "q"), ("k", "k"), ("v", "v"), ("l", "l")):
        w["l0a_" + k] = aug(i[a + "W" + k], i[a + "b" + b])
    w["l0a_gamma"], w["l0a_beta"] = col(i[a + "gamma"]), col(i[a + "beta"])
    a = "L0_ffn_"
    w["l0f_ln1"], w["l0f_ln2"] = col(i[a + "ln1_w"]), col(i[a + "ln2_w"])
    wq, wk, wv = (np.asarray(i[a + k]).T for k in ("wq", "wk", "wv"))
    rep = np.repeat(np.arange(2), 2)
    rot = np.concatenate([np.arange(8, 16), np.arange(8)])
    q4 = wq.reshape(64, 4, 16)
    k4 = wk.reshape(64, 2, 16)[:, rep]
    w["l0f_q"], w["l0f_qp"] = q4.reshape(64, 64), q4[:, :, rot].reshape(64, 64)
    w["l0f_k"], w["l0f_kp"] = k4.reshape(64, 64), k4[:, :, rot].reshape(64, 64)
    v4 = wv.reshape(64, 2, 16)[:, rep]
    vm = np.zeros((64, 4, 4, 16), np.float32)
    for h in range(4):
        vm[:, h, h] = v4[:, h]
    w["l0f_v"] = vm.reshape(64, 256)
    w["l0f_wo"] = np.asarray(i[a + "wo"]).T
    w["l0f_router"] = np.asarray(i[a + "router_w"]).T
    for k in ("w1", "w3"):
        m = np.zeros((64, NTILE * 128), np.float32)
        m[:, :8 * HID] = np.asarray(i[a + k]).transpose(2, 0, 1).reshape(64, 8 * HID)
        w["l0f_" + k] = m
    m = np.zeros((NTILE * 128, 64), np.float32)
    m[:8 * HID] = np.asarray(i[a + "w2"]).transpose(0, 2, 1).reshape(8 * HID, 64)
    w["l0f_w2"] = m.reshape(NTILE, 128, 64).transpose(1, 0, 2).reshape(128, NTILE * 64)
    a = "L1_attn_"
    w["l1a_g"], w["l1a_b"] = col(i[a + "ln1_g"]), col(i[a + "ln1_b"])
    qw, qb = np.asarray(i[a + "qkv_w"]), np.asarray(i[a + "qkv_b"])
    for n, k in enumerate("qkv"):
        w["l1a_" + k] = aug(qw[:, 64 * n:64 * n + 64], qb[64 * n:64 * n + 64])
    w["l1a_l"] = aug(i[a + "proj_w"], i[a + "proj_b"])
    n = np.arange(128) % SEQ
    w["l1a_rel"] = np.asarray(i[a + "bias_table"])[np.arange(SEQ)[None, :] - n[:, None] + SEQ - 1]
    w["l1a_scale"] = np.broadcast_to(np.asarray(i[a + "scale"]).reshape(1, 1), (128, 1))
    w["l1a_g2"], w["l1a_b2"] = row(i[a + "ln2_g"]), row(i[a + "ln2_b"])
    a = "L1_ffn_"
    halves = lambda m: np.asarray(m).reshape(2, 128, -1).transpose(1, 0, 2).reshape(128, -1)
    w["l1f_w1"], w["l1f_b1"] = i[a + "W1"], halves(i[a + "b1"])
    w["l1f_wg"], w["l1f_bg"] = halves(i[a + "Wg"]), row(i[a + "bg"])
    w["l1f_wd"] = halves(np.asarray(i[a + "Wd"]).transpose(1, 0, 2).reshape(256, 512))
    w["l1f_bd"] = np.asarray(i[a + "bd"]).reshape(1, 512)
    a = "L2_attn_"
    w["l2a_g"], w["l2a_b"] = col(i[a + "ln1_g"]), col(i[a + "ln1_b"])
    w["l2a_wx"], w["l2a_bx"] = i[a + "Wx"], halves(i[a + "bx"])
    for k in "qk":
        m = np.zeros((8, 32, 8, 4), np.float32)
        for h in range(8):
            m[h, :, h] = i[a + "W" + k]
        w["l2a_w" + k] = halves(m.reshape(256, 32))
    m = np.zeros((4, 32, 4, 32), np.float32)
    for h in range(4):
        m[h, :, h] = i[a + "Wv"]
    w["l2a_wv"] = m.reshape(128, 128)
    w["l2a_wo"], w["l2a_bo"] = halves(i[a + "Wo"]), row(i[a + "bo"])
    w["l2a_g2"], w["l2a_b2"] = col(i[a + "ln2_g"]), col(i[a + "ln2_b"])
    w["l2a_w1"], w["l2a_fb1"] = i[a + "W1"], halves(i[a + "b1"])
    w["l2a_w2"], w["l2a_fb2"] = halves(i[a + "W2"]), row(i[a + "b2"])
    a = "L2_ffn_"
    w["l2f_s1"], w["l2f_sb1"] = i[a + "sW1"], col(i[a + "sb1"])
    w["l2f_s2"], w["l2f_sb2"] = i[a + "sW2"], col(i[a + "sb2"])
    w["l2f_s3"], w["l2f_sb3"] = i[a + "sW3"], row(i[a + "sb3"])
    w["l2f_e1"] = np.asarray(i[a + "eW1"]).transpose(1, 0, 2).reshape(64, 512)
    w["l2f_eb1"] = np.asarray(i[a + "eb1"]).T
    w["l2f_e2"] = np.asarray(i[a + "eW2"]).transpose(1, 0, 2).reshape(128, 256)
    w["l2f_eb2"] = np.asarray(i[a + "eb2"]).reshape(2, 128).T
    m = np.zeros((2, 2, 64, 2, 64), np.float32)
    for e in range(4):
        m[e // 2, e % 2, :, e % 2] = np.asarray(i[a + "eW3"])[e]
    w["l2f_e3"] = m.reshape(2, 128, 128).transpose(1, 0, 2).reshape(128, 256)
    w["l2f_eb3"] = np.asarray(i[a + "eb3"]).reshape(1, 256)
    w["l2f_g"], w["l2f_gb"] = i[a + "gW"], row(i[a + "gb"])
    a = "L3_attn_"
    for k in "qkv":
        w["l3a_" + k] = np.asarray(i[a + "W" + k]).reshape(64, 64, 8).transpose(0, 2, 1).reshape(64, 512)
    m = np.asarray(i[a + "Wo"]).reshape(64, 8, 64).transpose(1, 0, 2).reshape(4, 128, 64)
    w["l3a_o"] = m.transpose(1, 0, 2).reshape(128, 256)
    a = "L3_ffn_"
    w["l3f_g"], w["l3f_bg"] = i[a + "Wg"], row(i[a + "bg"])
    w["l3f_w1"] = np.asarray(i[a + "W1"]).transpose(1, 0, 2).reshape(64, 1024)
    w["l3f_b1"] = np.asarray(i[a + "b1"]).T
    w["l3f_w2"] = np.asarray(i[a + "W2"]).transpose(1, 0, 2).reshape(128, 512)
    w["l3f_b2"] = np.asarray(i[a + "b2"]).reshape(1, 512)
    return w


def packed(parts):
    total = sum(np.asarray(v).shape[1] for v in parts.values())
    out, at, where = np.zeros((128, total), np.float32), 0, {}
    for name, v in parts.items():
        p, n = np.asarray(v).shape
        out[:p, at:at + n] = v
        where[name] = (p, at, n)
        at += n
    return out, where


STEPS = {('l0a', 'act'): ['x.sq', 'x.xT', 'q', 'exp', 'pT', 'oT'],
 ('l0a', 'dve'): ['x.sum', 'x.centered', 'x.sumsq', 'x.var', 'x.out', 'k', 'v', 'max', 'diff', 'sum', 'recip',
                  'p_lo', 'p_hi', 'hx', 'hl'],
 ('l0a', 'pe'): ['x.flip', 'q', 'k', 'v', 'scores', 'pT', 'attended', 'hl'],
 ('l0a', 'pool'): ['x.rstd'],
 ('l0b', 'act'): ['y'],
 ('l0b', 'dve'): ['normed', 'h'],
 ('l0b', 'pe'): ['y'],
 ('l0f', 'act'): ['x.sq', 'r.sq', 'r.xT', 'km', 'v', 'exp', 'pT0', 'pT2', 'oT', 'f.sq', 'f.xT', 'exp_router',
                  'gatesT', 'silu0', 'silu1', 'silu2', 'silu3', 'silu4', 'silu5', 'silu6', 'silu7', 'silu8',
                  'silu9', 'silu10', 'yT'],
 ('l0f', 'dve'): ['x.sum', 'x.centered', 'x.sumsq', 'x.var', 'x.out', 'r.sumsq', 'r.var', 'r.out', 'qa', 'qb',
                  'q', 'ka', 'kb', 'k', 'masked0', 'masked1', 'max', 'diff', 'sum', 'recip', 'p_lo', 'p_hi',
                  'pT1', 'pT3', 'x2', 'f.sumsq', 'f.var', 'f.out', 'emax', 'ediff', 'esum', 'erecip', 'probs',
                  'greater', 'equal', 'tied', 'ahead', 'rank', 'chosen', 'kept', 'kept_sum', 'kept_eps',
                  'kept_recip', 'gates', 'up0', 'hid0', 'up1', 'hid1', 'up2', 'hid2', 'up3', 'hid3', 'up4',
                  'hid4', 'up5', 'hid5', 'up6', 'hid6', 'up7', 'hid7', 'up8', 'hid8', 'up9', 'hid9', 'up10',
                  'hid10', 'h_x', 'h'],
 ('l0f', 'pe'): ['r.flip', 'q', 'qp', 'k', 'kp', 'v', 'scores', 'pT0', 'pT1', 'pT2', 'pT3', 'attended', 'wo',
                 'f.flip', 'logits', 'gatesT', 'gate0', 'up0', 'share0', 'gate1', 'up1', 'share1', 'down0',
                 'gate2', 'up2', 'share2', 'down1', 'gate3', 'up3', 'share3', 'down2', 'gate4', 'up4',
                 'share4', 'down3', 'gate5', 'up5', 'share5', 'down4', 'gate6', 'up6', 'share6', 'down5',
                 'gate7', 'up7', 'share7', 'down6', 'gate8', 'up8', 'share8', 'down7', 'gate9', 'up9',
                 'share9', 'down8', 'gate10', 'up10', 'share10', 'down9', 'down10', 'y'],
 ('l0f', 'pool'): ['x.rstd', 'r.rstd', 'f.rstd'],
 ('l1a', 'act'): ['x.sq', 'r.sq', 'x.xT', 'q', 'exp', 'pT', 'oT', 'o.sq'],
 ('l1a', 'dve'): ['x.sum', 'x.centered', 'x.sumsq', 'x.var', 'x.out', 'r.sum', 'r.centered', 'r.sumsq',
                  'r.var', 'r.out', 'k', 'v', 'biased', 'max', 'diff', 'sum', 'recip', 'scaled', 'p_lo',
                  'p_hi', 'proj', 'o.sum', 'o.centered', 'o.sumsq', 'o.var', 'o.out', 'o.g', 'h_b', 'h'],
 ('l1a', 'pe'): ['x.flip', 'q', 'k', 'v', 'scores', 'pT', 'attended', 'proj'],
 ('l1a', 'pool'): ['x.rstd', 'r.rstd', 'o.rstd'],
 ('l1f', 'act'): ['x.sq', 'x.xT', 'hid0', 'hid1', 'exp'],
 ('l1f', 'dve'): ['x.sum', 'x.centered', 'x.sumsq', 'x.var', 'x.out', 'biased', 'emax', 'ediff', 'esum',
                  'erecip', 'probs', 'greater', 'equal', 'tied', 'ahead', 'rank', 'chosen', 'gates',
                  'weighed0', 'summed0', 'weighed1', 'summed1', 'weighed2', 'summed2', 'weighed3', 'summed3',
                  'h'],
 ('l1f', 'pe'): ['x.flip', 'hid0', 'hid1', 'logits', 'out0', 'out1', 'out2', 'out3'],
 ('l1f', 'pool'): ['x.rstd'],
 ('l2a', 'act'): ['x.sq', 'r.sq', 'x.xT', 'hid0', 'hid1', 'exp', 'kexp', 'v', 'k4', 'q4T', 'o0', 'f.sq',
                  'f.xT', 'ff0', 'ff1'],
 ('l2a', 'dve'): ['x.sum', 'x.centered', 'x.sumsq', 'x.var', 'x.out', 'r.sum', 'r.centered', 'r.sumsq',
                  'r.var', 'r.out', 'max', 'diff', 'sum', 'recip', 'q4', 'kmax', 'kdiff', 'ksum', 'krecip',
                  'kprob', 'kv', 'o1', 'x_bo', 'fx', 'f.sum', 'f.centered', 'f.sumsq', 'f.var', 'f.out',
                  'fx_b', 'h_fx', 'h'],
 ('l2a', 'pe'): ['x.flip', 'hid0', 'hid1', 'q', 'k', 'v', 'kT', 'kv', 'q4T', 'o0', 'o1', 'wo', 'f.flip',
                 'ff0', 'ff1', 'ff'],
 ('l2a', 'pool'): ['x.rstd', 'zeros', 'r.rstd', 'f.rstd'],
 ('l2f', 'act'): ['x.sq', 'x.xT', 's1', 's2', 'exp', 'e1_0', 'e1_1', 'e1_2', 'e1_3', 'texp'],
 ('l2f', 'dve'): ['x.sum', 'x.centered', 'x.sumsq', 'x.var', 'x.out', 'biased', 'emax', 'ediff', 'esum',
                  'erecip', 'probs', 'e2_0', 'e2_1', 'greater', 'equal', 'tied', 'ahead', 'rank', 'chosen',
                  'tmax', 'tdiff', 'tkept', 'tsum', 'trecip', 'gates', 'h_b', 'h_s', 'weighed0', 'summed0',
                  'weighed1', 'summed1', 'weighed2', 'summed2', 'weighed3', 'summed3', 'h'],
 ('l2f', 'pe'): ['x.flip', 'logits', 's1', 's2', 's3', 'e1_0', 'e1_1', 'e2_0', 'e1_2', 'e2_1', 'e1_3', 'e2_2',
                 'e2_3', 'out0', 'out1'],
 ('l2f', 'pool'): ['x.rstd'],
 ('l3a', 'act'): ['x.sq', 'x.xT', 'v2', 'v0', 'q0', 'p0_0', 'p0_1', 'o0', 'q1', 'p1_0', 'p1_1', 'o1', 'q2',
                  'p2_0', 'p2_1', 'o2', 'q3', 'p3_0', 'p3_1', 'o3'],
 ('l3a', 'dve'): ['x.sum', 'x.centered', 'x.sumsq', 'x.var', 'x.out', 'v1', 'v3', 'k0', 'k1', 'k2', 'k3',
                  'h'],
 ('l3a', 'pe'): ['x.flip', 'v1', 'v2', 'v3', 'v0', 'q0', 'k0', 's0_0', 's0_1', 'o0', 'q1', 'k1', 's1_0',
                 's1_1', 'o1', 'q2', 'k2', 's2_0', 's2_1', 'o2', 'q3', 'k3', 's3_0', 's3_1', 'o3', 'wo'],
 ('l3a', 'pool'): ['x.rstd'],
 ('l3f', 'act'): ['x.sq', 'x.xT', 'hid0', 'hid1', 'hid2', 'hid3', 'hid4', 'hid5', 'hid6', 'hid7'],
 ('l3f', 'dve'): ['x.sum', 'x.centered', 'x.sumsq', 'x.var', 'x.out', 'biased', 'greater', 'equal', 'tied',
                  'ahead', 'rank', 'chosen', 'weighed0', 'summed0', 'weighed1', 'summed1', 'weighed2',
                  'summed2', 'weighed3', 'summed3', 'h'],
 ('l3f', 'pe'): ['x.flip', 'logits', 'hid0', 'hid1', 'hid2', 'hid3', 'hid4', 'hid5', 'hid6', 'hid7', 'out0',
                 'out1', 'out2', 'out3'],
 ('l3f', 'pool'): ['x.rstd']}


class Signals:

    def __init__(self, nc, ctx, steps):
        self.steps = steps
        self.sems = {}
        for key in self.steps:
            self.sems[key] = ctx.enter_context(nc.semaphore("%s_%s_done" % key))

    def sem(self, stage, who):
        return self.sems[stage, who]

    def count(self, stage, who, step, u, it):
        names = self.steps[stage, who]
        return it * (len(names) * U) + (names.index(step) * U + u + 1)


class Engine:

    def __init__(self, signals, who, eng, stage, it, apart=False):
        self.s, self.who, self.eng, self.stage, self.it, self.apart = signals, who, eng, stage, it, apart

    def need(self, who, step, u):
        self.eng.wait_ge(self.s.sem(self.stage, who), self.s.count(self.stage, who, step, u, self.it))
        if self.apart:
            self.eng.nop(nofuse=True)

    def done(self, instruction, step, u):
        instruction.then_inc(self.s.sem(self.stage, self.who), 1)


def build_blocks(nc, tok, out_dram, weights_dram, consts_dram, where_w, where_c):
    with ExitStack() as ctx:
        sb = lambda n, s: ctx.enter_context(nc.sbuf_tensor(n, s, F32))
        sem = lambda n: ctx.enter_context(nc.semaphore(n))
        wts = sb("weights", [128, weights_dram.shape[1]])
        cst = sb("constants", [128, consts_dram.shape[1]])

        def W(name):
            src, where = (wts, where_w) if name in where_w else (cst, where_c)
            p, at, n = where[name]
            return src[0:p, at:at + n]

        hl = sb("hl", [64, TOKENS])
        hx = sb("hx", [128, TOKENS // 128, 64])
        bn = sb("bn", [64, 24])
        per = lambda n, s: [sb(f"{n}{u}", s) for u in R]
        h, x, r, sq = (per(n, [128, T, 64]) for n in ("h", "x", "r", "sq"))
        xT, oT = per("xT", [65, BLK]), per("oT", [65, BLK])
        Q, K = per("qt", [128, BLK]), per("kt", [128, BLK])
        H = per("hid", [128, 2, BLK])
        A16 = per("big", [128, 4096])
        pbd = per("pbd", [128, 16, 128])
        pT = per("pT", [128, 16, 128])
        tmp = [pT[u][:, 0:4, :].rearrange("p t n -> p (t n)") for u in R]
        st = per("st", [128, 192])
        B = [[ctx.enter_context(nc.psum_tensor(f"bank{u}_{b}", [128, 512], F32)) for b in range(4)] for u in R]

        loaded = sem("weights_loaded")
        h_in = [sem(f"h_loaded{u}") for u in R]
        out_sent = [sem(f"out_sent{u}") for u in R]
        ready = sem("constant_tiles_ready")
        bn_done = {w: sem(f"bn_{w}") for w in ("dve", "act", "pool")}
        sig = Signals(nc, ctx, STEPS)
        eye = W("eye")
        lo, hi = slice(0, 64), slice(64, 128)

        def bc(ap, n):
            return ap.unsqueeze(ap.ndim).broadcast_to(list(ap.shape) + [n])

        def bmid(ap, n):
            return ap.unsqueeze(1).broadcast_to([ap.shape[0], n] + list(ap.shape[1:]))

        tf = lambda ap, t=T: ap.rearrange("p (t f) -> p t f", t=t)
        V = nc.vector

        def ln_vector(d, tag, src, dst, eps=1e-5, first=None):
            for u in R:
                if first:
                    first(u)
                else:
                    d.eng.wait_ge(sig.sem(d.before, "dve"), sig.count(d.before, "dve", "h", u, d.it))
                d.done(V.reduce_sum(st[u][:, 0:4], src[u][:], axis=AX.X), tag + ".sum", u)
            for u in R:
                d.need("dve", tag + ".sum", u)
                d.done(V.scalar_tensor_tensor(out=dst[u][:], in0=bc(st[u][:, 0:4], 64), scalar=-1.0 / 64,
                                              in1=src[u][:], op0=ALU.mult, op1=ALU.add), tag + ".centered", u)
            ln_scale(d, tag, dst, dst, eps)

        def ln_scale(d, tag, src, dst, eps):
            for u in R:
                d.need("act", tag + ".sq", u)
                d.done(V.reduce_sum(st[u][:, 4:8], sq[u][:], axis=AX.X), tag + ".sumsq", u)
            for u in R:
                d.need("dve", tag + ".sumsq", u)
                d.done(V.tensor_scalar(st[u][:, 4:8], st[u][:, 4:8], 1.0 / 64, eps, ALU.mult, ALU.add),
                       tag + ".var", u)
            for u in R:
                d.need("pool", tag + ".rstd", u)
                d.done(V.tensor_tensor(dst[u][:], src[u][:], bc(st[u][:, 8:12], 64), ALU.mult), tag + ".out", u)

        def ln_scalar(a, tag, src, after=".centered"):
            for u in R:
                a.need("dve", tag + after if after[0] == "." else after, u)
                a.done(nc.scalar.activation(sq[u][:], src[u][:], ACT.Square), tag + ".sq", u)

        def ln_pool(p, tag):
            for u in R:
                p.need("dve", tag + ".var", u)
                p.done(nc.gpsimd.tensor_tensor(st[u][:, 8:12], st[u][:, 4:8], W("mhalf"), ALU.pow), tag + ".rstd", u)

        def flip_tensor(p, tag, src, after, bank=0):
            for u in R:
                p.need("dve", after, u)
                for t in range(T):
                    last = nc.tensor.transpose(B[u][bank][lo, 128 * t:128 * t + 128], src[u][:, t, :], eye)
                p.done(last, tag + ".flip", u)

        def flip_scalar(a, tag, scale=None, bias=None):
            for u in R:
                a.need("pe", tag + ".flip", u)
                kw = {}
                if scale is not None:
                    kw["scale"] = W(scale)
                if bias is not None:
                    kw["bias"] = W(bias)
                a.done(nc.scalar.activation(xT[u][lo, :], B[u][0][lo, :], ACT.Identity, **kw), tag + ".xT", u)

        def mm(out, lhsT, rhs, start=True, stop=True):
            return nc.tensor.matmul(out, lhsT, rhs, start=start, stop=stop)

        def softmax_vector(d, src, e, g, p=128, after=None):
            for u in R:
                if after:
                    d.need(*after, u)
                d.done(V.reduce_max(st[u][0:p, 16:16 + g], src(u), axis=AX.X), "max", u)
            for u in R:
                d.need("dve", "max", u)
                n = e(u).shape[-1]
                d.done(V.tensor_tensor(e(u), src(u), bc(st[u][0:p, 16:16 + g], n), ALU.subtract), "diff", u)
            for u in R:
                d.need("act", "exp", u)
                d.done(V.reduce_sum(st[u][0:p, 48:48 + g], e(u), axis=AX.X), "sum", u)
            for u in R:
                d.need("dve", "sum", u)
                d.done(V.reciprocal(st[u][0:p, 48:48 + g], st[u][0:p, 48:48 + g]), "recip", u)

        def exp_scalar(a, e, scale=1.0):
            for u in R:
                a.need("dve", "diff", u)
                a.done(nc.scalar.activation(e(u), e(u), ACT.Exp, scale=scale), "exp", u)

        def rank_vector(d, score, n, k, before, after):
            g = lambda u: sq[u][:].rearrange("p t f -> p (t f)")[:, 0:T * n * n].rearrange("p (t e j) -> p t e j", t=T, e=n)
            q = lambda u: r[u][:].rearrange("p t f -> p (t f)")[:, 0:T * n * n].rearrange("p (t e j) -> p t e j", t=T, e=n)
            mine = lambda u: bc(score(u), n)
            other = lambda u: score(u).unsqueeze(2).broadcast_to([128, T, n, n])
            sel = lambda u: st[u][:, 128:128 + T * n].rearrange("p (t e) -> p t e", t=T)
            for u in R:
                d.need("dve", after, u)
                d.done(V.tensor_tensor(g(u), other(u), mine(u), ALU.is_gt), "greater", u)
            for u in R:
                d.done(V.tensor_tensor(q(u), other(u), mine(u), ALU.is_equal), "equal", u)
            for u in R:
                d.need("dve", "equal", u)
                d.done(V.tensor_tensor(q(u), q(u), bmid(W(before).rearrange("p (e j) -> p e j", e=n), T), ALU.mult),
                       "tied", u)
            for u in R:
                d.need("dve", "tied", u)
                d.done(V.tensor_tensor(g(u), g(u), q(u), ALU.add), "ahead", u)
            for u in R:
                d.need("dve", "ahead", u)
                d.done(V.reduce_sum(sel(u), g(u), axis=AX.X), "rank", u)
            for u in R:
                d.need("dve", "rank", u)
                d.done(V.tensor_scalar(sel(u), sel(u), k - 0.5, None, ALU.is_lt), "chosen", u)

        st8 = lambda u, at, n=8: st[u][:, at:at + T * n].rearrange("p (t e) -> p t e", t=T)

        a_q = lambda u: Q[u][lo, :]
        a_k = lambda u: K[u][lo, :]
        a_v = lambda u: tf(A16[u][:, 1024:1280])
        a_e = lambda u: tf(A16[u][:, 0:256])

        def attn_tensor(p, name):
            for u in R:
                p.need("act", "x.xT", u)
                p.done(mm(B[u][1][lo, :], W(name + "_q"), xT[u][:]), "q", u)
            for u in R:
                p.done(mm(B[u][2][lo, :], W(name + "_k"), xT[u][:]), "k", u)
            for u in R:
                for t in range(T):
                    last = mm(B[u][3][:, 64 * t:64 * t + 64], xT[u][:, 128 * t:128 * t + 128], W(name + "_v"))
                p.done(last, "v", u)
            for u in R:
                p.need("act", "q", u)
                p.need("dve", "k", u)
                for b in range(BATCHES):
                    o = slice(64 * (b % 2), 64 * (b % 2) + 64)
                    last = mm(B[u][0][o, 64 * (b // 2):64 * (b // 2) + 64], a_q(u)[:, 64 * b:64 * b + 64],
                              a_k(u)[:, 64 * b:64 * b + 64])
                p.done(last, "scores", u)
            for u in R:
                p.need("dve", "p_hi", u)
                for t in range(T):
                    last = nc.tensor.transpose(B[u][1][:, 128 * t:128 * t + 128], pbd[u][:, t, :], eye)
                p.done(last, "pT", u)
            for u in R:
                p.need("act", "pT", u)
                p.need("dve", "v", u)
                for t in range(T):
                    last = mm(B[u][2][lo, 128 * t:128 * t + 128], a_v(u)[:, t, :], pT[u][:, t, :])
                p.done(last, "attended", u)

        def attn_scalar(a, scale):
            for u in R:
                a.need("pe", "q", u)
                a.done(nc.scalar.activation(a_q(u), B[u][1][lo, :], ACT.Identity), "q", u)
            exp_scalar(a, a_e, scale)
            for u in R:
                a.need("pe", "pT", u)
                a.done(nc.scalar.activation(pT[u][:, 0:T, :].rearrange("p t n -> p (t n)"), B[u][1][:], ACT.Identity),
                       "pT", u)
            for u in R:
                a.need("pe", "attended", u)
                a.done(nc.scalar.activation(oT[u][lo, :], B[u][2][lo, :], ACT.Identity), "oT", u)

        def attn_vector(d, rel=None, scale=None):
            for u in R:
                d.need("pe", "k", u)
                d.done(V.tensor_copy(a_k(u), B[u][2][lo, :]), "k", u)
            for u in R:
                d.need("pe", "v", u)
                d.done(V.tensor_copy(a_v(u), tf(B[u][3][:, 0:256])), "v", u)
            src = lambda u: tf(B[u][0][:, 0:256])
            if rel:
                for u in R:
                    d.need("pe", "scores", u)
                    d.done(V.tensor_tensor(a_e(u), tf(B[u][0][:, 0:256]), bmid(W(rel), T), ALU.add), "biased", u)
                softmax_vector(d, a_e, a_e, T, after=("dve", "biased"))
            else:
                softmax_vector(d, src, a_e, T, after=("pe", "scores"))
            last = "recip"
            if scale:
                for u in R:
                    d.need("dve", "recip", u)
                    d.done(V.tensor_scalar(st[u][:, 48:52], st[u][:, 48:52], W(scale), None, ALU.mult), "scaled", u)
                last = "scaled"
            diag_vector(d, last)

        def diag_vector(d, after):
            for name, part in (("p_lo", lo), ("p_hi", hi)):
                for u in R:
                    d.need("dve", after, u)
                    d.done(V.tensor_tensor(pbd[u][part, 0:T, part], a_e(u)[part], bc(st[u][part, 48:52], 64), ALU.mult),
                           name, u)

        def blk(it, u):
            return U * it + u

        def l0a_tensor(p):
            flip_tensor(p, "x", x, "x.out")
            attn_tensor(p, "l0a")
            for u in R:
                p.need("act", "oT", u)
                p.done(mm(B[u][3][lo, :], W("l0a_l"), oT[u][:]), "hl", u)

        def l0a_scalar(a):
            ln_scalar(a, "x", x)
            flip_scalar(a, "x")
            attn_scalar(a, 1.0 / 64)

        def l0a_vector(d):
            def first(u):
                d.eng.wait_ge(h_in[u], d.it * 16 + 16)
            ln_vector(d, "x", h, x, first=first)
            attn_vector(d)
            for u in R:
                d.done(V.tensor_tensor(hx[:, bass.ds(T * blk(d.it, u), T), :], h[u][:], x[u][:], ALU.add), "hx", u)
            for u in R:
                d.need("pe", "hl", u)
                d.done(V.tensor_copy(hl[:, bass.ds(BLK * blk(d.it, u), BLK)], B[u][3][lo, :]), "hl", u)

        def l0b_scalar(a):
            for u in R:
                a.need("dve", "normed", u)
                a.done(nc.scalar.activation(Q[u][lo, :], Q[u][lo, :], ACT.Relu, bias=W("l0a_beta")), "y", u)

        def l0b_tensor(p):
            for u in R:
                p.need("act", "y", u)
                for t in range(T):
                    last = nc.tensor.transpose(B[u][0][:, 64 * t:64 * t + 64], Q[u][lo, 128 * t:128 * t + 128],
                                               eye[lo, lo])
                p.done(last, "y", u)

        def l0b_vector(d):
            for u in R:
                d.done(V.tensor_scalar(Q[u][lo, :], hl[:, bass.ds(BLK * blk(d.it, u), BLK)], bn[:, 17:18],
                                       bn[:, 20:21], ALU.add, ALU.mult), "normed", u)
            for u in R:
                d.need("pe", "y", u)
                d.eng.wait_ge(out_sent[u], d.it * 16)
                d.done(V.tensor_tensor(h[u][:], tf(B[u][0][:, 0:256]), hx[:, bass.ds(T * blk(d.it, u), T), :],
                                       ALU.add), "h", u)

        km = lambda u: A16[u][lo, 0:2048].rearrange("p (h n) -> p h n", h=4)
        vm = lambda u: tf(A16[u][:, 2048:3072])
        f_e = lambda u: A16[u][:, 3072:4096].rearrange("p (g n) -> p g n", g=16)
        rope = lambda ap: ap.rearrange("p (b n) -> p b n", n=SEQ)

        def l0f_tensor(p):
            flip_tensor(p, "r", r, "r.out")
            for name, b in (("q", 1), ("qp", 2), ("k", 3)):
                for u in R:
                    if b == 1:
                        p.need("act", "r.xT", u)
                    p.done(mm(B[u][b][lo, :], W("l0f_" + name), xT[u][lo, :]), name, u)
            for u in R:
                p.done(mm(B[u][0][lo, :], W("l0f_kp"), xT[u][lo, :]), "kp", u)
            for u in R:
                p.need("dve", "qb", u)
                for t in range(T):
                    last = mm(B[u][1 + t // 2][:, 256 * (t % 2):256 * (t % 2) + 256], xT[u][lo, 128 * t:128 * t + 128],
                              W("l0f_v"))
                p.done(last, "v", u)
            for u in R:
                p.need("act", "km", u)
                p.need("dve", "kb", u)
                for b in range(BATCHES):
                    o = slice(64 * (b % 2), 64 * (b % 2) + 64)
                    t = b // 2
                    last = mm(B[u][3 if t < 2 else 0][o, 256 * (t % 2):256 * (t % 2) + 256], Q[u][lo, 64 * b:64 * b + 64],
                              km(u)[:, :, 64 * b:64 * b + 64])
                p.done(last, "scores", u)
            for t in range(T):
                for u in R:
                    if t == 0:
                        p.need("dve", "p_hi", u)
                        p.need("act", "v", u)
                    for g in range(4):
                        last = nc.tensor.transpose(B[u][t][:, 128 * g:128 * g + 128], pbd[u][:, 4 * t + g, :], eye)
                    p.done(last, f"pT{t}", u)
            for u in R:
                p.need("act", "pT2", u)
                p.need("dve", "pT3", u)
                for t in range(T):
                    for g in range(4):
                        last = mm(B[u][0][lo, 128 * t:128 * t + 128], vm(u)[:, t, 64 * g:64 * g + 64],
                                  pT[u][:, 4 * t + g, :], start=(g == 0), stop=(g == 3))
                p.done(last, "attended", u)
            for u in R:
                p.need("act", "oT", u)
                for t in range(T):
                    last = mm(B[u][1][:, 64 * t:64 * t + 64], oT[u][lo, 128 * t:128 * t + 128], W("l0f_wo"))
                p.done(last, "wo", u)
            flip_tensor(p, "f", r, "f.out")
            for u in R:
                p.need("act", "f.xT", u)
                for t in range(T):
                    last = mm(B[u][2][:, 8 * t:8 * t + 8], xT[u][lo, 128 * t:128 * t + 128], W("l0f_router"))
                p.done(last, "logits", u)
            for u in R:
                p.need("dve", "gates", u)
                for t in range(T):
                    last = nc.tensor.transpose(B[u][3][0:8, 128 * t:128 * t + 128], st8(u, 160)[:, t, :], eye)
                p.done(last, "gatesT", u)
            for j in range(NTILE + 1):
                if j < NTILE:
                    cols = slice(128 * j, 128 * j + 128)
                    for u in R:
                        if j:
                            p.need("act", f"silu{j - 1}", u)
                        p.done(mm(B[u][1][:], W("l0f_w1")[:, cols], xT[u][lo, :]), f"gate{j}", u)
                    for u in R:
                        if j:
                            p.need("dve", f"up{j - 1}", u)
                        p.done(mm(B[u][2][:], W("l0f_w3")[:, cols], xT[u][lo, :]), f"up{j}", u)
                    for u in R:
                        if j:
                            p.need("dve", f"hid{j - 1}", u)
                        else:
                            p.need("act", "gatesT", u)
                        p.done(mm(B[u][3][:], W("expand")[:, cols], tmp[u][0:8, :]), f"share{j}", u)
                if j:
                    for u in R:
                        p.need("dve", f"hid{j - 1}", u)
                        p.done(mm(B[u][0][lo, :], W("l0f_w2")[:, 64 * (j - 1):64 * j], Q[u][:], start=(j == 1),
                                  stop=(j == NTILE)), f"down{j - 1}", u)
            for u in R:
                p.need("act", "yT", u)
                for t in range(T):
                    last = nc.tensor.transpose(B[u][1][:, 64 * t:64 * t + 64], oT[u][lo, 128 * t:128 * t + 128],
                                               eye[lo, lo])
                p.done(last, "y", u)

        def l0f_scalar(a):
            ln_scalar(a, "x", x)
            ln_scalar(a, "r", x, after="x.out")
            flip_scalar(a, "r", scale="l0f_ln1")
            for u in R:
                a.need("dve", "k", u)
                for g in range(4):
                    last = nc.scalar.activation(km(u)[:, g, :], K[u][lo, :], ACT.Identity, scale=W("headmask")[:, g:g + 1])
                a.done(last, "km", u)
            for u in R:
                a.need("pe", "v", u)
                for b in range(2):
                    last = nc.scalar.activation(vm(u)[:, 2 * b:2 * b + 2, :], tf(B[u][1 + b][:], 2), ACT.Identity)
                a.done(last, "v", u)
            exp_scalar(a, f_e, 0.25)
            for t in (0, 2):
                for u in R:
                    a.need("pe", f"pT{t}", u)
                    a.done(nc.scalar.activation(pT[u][:, 4 * t:4 * t + 4, :].rearrange("p t n -> p (t n)"), B[u][t][:],
                                                ACT.Identity), f"pT{t}", u)
            for u in R:
                a.need("pe", "attended", u)
                a.done(nc.scalar.activation(oT[u][lo, :], B[u][0][lo, :], ACT.Identity), "oT", u)
            ln_scalar(a, "f", x, after="x2")
            flip_scalar(a, "f", scale="l0f_ln2")
            small_exp(a, 8, "exp_router")
            for u in R:
                a.need("pe", "gatesT", u)
                a.done(nc.scalar.activation(tmp[u][0:8, :], B[u][3][0:8, :], ACT.Identity), "gatesT", u)
            for j in range(NTILE):
                for u in R:
                    a.need("pe", f"gate{j}", u)
                    if j:
                        a.need("dve", f"up{j - 1}", u)
                    a.done(nc.scalar.activation(K[u][:], B[u][1][:], ACT.Silu), f"silu{j}", u)
            for u in R:
                a.need("pe", f"down{NTILE - 1}", u)
                a.done(nc.scalar.activation(oT[u][lo, :], B[u][0][lo, :], ACT.Identity), "yT", u)

        def l0f_vector(d):
            ln_vector(d, "x", h, x)
            ln_scale(d, "r", x, r, 1e-6)
            for name, b, table, dst, wait in (("qa", 1, "cos", 0, "q"), ("qb", 2, "sin", 1, "qp")):
                for u in R:
                    d.need("pe", wait, u)
                    d.done(V.tensor_tensor(rope(H[u][lo, dst, :]), rope(B[u][b][lo, :]), bmid(W(table), BATCHES), ALU.mult),
                           name, u)
            for u in R:
                d.need("dve", "qb", u)
                d.done(V.tensor_tensor(Q[u][lo, :], H[u][lo, 0, :], H[u][lo, 1, :], ALU.add), "q", u)
            for name, b, table, dst, wait in (("ka", 3, "cos", 0, "k"), ("kb", 0, "sin", 1, "kp")):
                for u in R:
                    d.need("pe", wait, u)
                    d.need("dve", "q", u)
                    d.done(V.tensor_tensor(rope(H[u][lo, dst, :]), rope(B[u][b][lo, :]), bmid(W(table), BATCHES), ALU.mult),
                           name, u)
            for u in R:
                d.need("dve", "kb", u)
                d.done(V.tensor_tensor(K[u][lo, :], H[u][lo, 0, :], H[u][lo, 1, :], ALU.add), "k", u)
            for b, bank in ((0, 3), (1, 0)):
                for u in R:
                    d.need("pe", "scores", u)
                    d.done(V.tensor_tensor(f_e(u)[:, 8 * b:8 * b + 8, :], B[u][bank][:].rearrange("p (g n) -> p g n", g=8),
                                           bmid(W("causal"), 8), ALU.add), f"masked{b}", u)
            softmax_vector(d, f_e, f_e, 16, after=("dve", "masked1"))
            for name, part in (("p_lo", lo), ("p_hi", hi)):
                for u in R:
                    d.need("dve", "recip", u)
                    d.done(V.tensor_tensor(pbd[u][part, :, part], f_e(u)[part], bc(st[u][part, 48:64], 64), ALU.mult),
                           name, u)
            for t in (1, 3):
                for u in R:
                    d.need("pe", f"pT{t}", u)
                    d.done(V.tensor_copy(pT[u][:, 4 * t:4 * t + 4, :].rearrange("p t n -> p (t n)"), B[u][t][:]),
                           f"pT{t}", u)
            for u in R:
                d.need("pe", "wo", u)
                d.done(V.tensor_tensor(x[u][:], x[u][:], tf(B[u][1][:, 0:256]), ALU.add), "x2", u)
            ln_scale(d, "f", x, r, 1e-6)
            router = lambda u: tf(B[u][2][:, 0:32])
            small_softmax(d, router, 8, "logits", "exp_router")
            rank_vector(d, lambda u: st8(u, 96), 8, 2, "before", "probs")
            for u in R:
                d.need("dve", "chosen", u)
                d.done(V.tensor_tensor(st8(u, 160), st8(u, 96), st8(u, 128), ALU.mult), "kept", u)
            for u in R:
                d.need("dve", "kept", u)
                d.done(V.reduce_sum(st[u][:, 48:52], st8(u, 160), axis=AX.X), "kept_sum", u)
            for u in R:
                d.need("dve", "kept_sum", u)
                d.done(V.tensor_scalar(st[u][:, 48:52], st[u][:, 48:52], 1e-9, None, ALU.add), "kept_eps", u)
            for u in R:
                d.need("dve", "kept_eps", u)
                d.done(V.reciprocal(st[u][:, 48:52], st[u][:, 48:52]), "kept_recip", u)
            for u in R:
                d.need("dve", "kept_recip", u)
                d.done(V.tensor_tensor(st8(u, 160), st8(u, 160), bc(st[u][:, 48:52], 8), ALU.mult), "gates", u)
            for j in range(NTILE):
                for u in R:
                    d.need("act", f"silu{j}", u)
                    d.need("pe", f"up{j}", u)
                    if j:
                        d.need("pe", f"down{j - 1}", u)
                    d.done(V.tensor_tensor(Q[u][:], B[u][2][:], K[u][:], ALU.mult), f"up{j}", u)
                for u in R:
                    d.need("dve", f"up{j}", u)
                    d.need("pe", f"share{j}", u)
                    d.done(V.tensor_tensor(Q[u][:], B[u][3][:], Q[u][:], ALU.mult), f"hid{j}", u)
            for u in R:
                d.done(V.tensor_tensor(h[u][:], h[u][:], x[u][:], ALU.add), "h_x", u)
            for u in R:
                d.need("pe", "y", u)
                d.need("dve", "h_x", u)
                d.done(V.tensor_tensor(h[u][:], h[u][:], tf(B[u][1][:, 0:256]), ALU.add), "h", u)

        def small_softmax(d, src, n, after, exp_step, at=96, who="pe"):
            m, s = slice(80, 84), slice(84, 88)
            for u in R:
                d.need(who, after, u)
                d.done(V.reduce_max(st[u][:, m], src(u), axis=AX.X), "emax", u)
            for u in R:
                d.need("dve", "emax", u)
                d.done(V.tensor_tensor(st8(u, at, n), src(u), bc(st[u][:, m], n), ALU.subtract), "ediff", u)
            for u in R:
                d.need("act", exp_step, u)
                d.done(V.reduce_sum(st[u][:, s], st8(u, at, n), axis=AX.X), "esum", u)
            for u in R:
                d.need("dve", "esum", u)
                d.done(V.reciprocal(st[u][:, s], st[u][:, s]), "erecip", u)
            for u in R:
                d.need("dve", "erecip", u)
                d.done(V.tensor_tensor(st8(u, at, n), st8(u, at, n), bc(st[u][:, s], n), ALU.mult), "probs", u)

        def small_exp(a, n, step, at=96):
            for u in R:
                a.need("dve", "ediff", u)
                a.done(nc.scalar.activation(st8(u, at, n), st8(u, at, n), ACT.Exp), step, u)

        def l1a_tensor(p):
            flip_tensor(p, "x", r, "r.out")
            attn_tensor(p, "l1a")
            for u in R:
                p.need("act", "oT", u)
                for t in range(T):
                    last = mm(B[u][3][:, 64 * t:64 * t + 64], oT[u][:, 128 * t:128 * t + 128], W("l1a_l"))
                p.done(last, "proj", u)

        def l1a_scalar(a):
            ln_scalar(a, "x", x)
            ln_scalar(a, "r", r)
            flip_scalar(a, "x", scale="l1a_g", bias="l1a_b")
            attn_scalar(a, 1.0)
            ln_scalar(a, "o", r)

        def l1a_vector(d):
            ln_vector(d, "x", h, x)
            ln_vector(d, "r", x, r, first=lambda u: d.need("dve", "x.out", u))
            attn_vector(d, rel="l1a_rel", scale="l1a_scale")
            for u in R:
                d.need("pe", "proj", u)
                d.done(V.tensor_copy(x[u][:], tf(B[u][3][:, 0:256])), "proj", u)
            ln_vector(d, "o", x, r, first=lambda u: d.need("dve", "proj", u))
            for u in R:
                d.need("dve", "o.out", u)
                d.done(V.tensor_tensor(r[u][:], r[u][:], bmid(W("l1a_g2"), T), ALU.mult), "o.g", u)
            for u in R:
                d.done(V.tensor_tensor(h[u][:], h[u][:], bmid(W("l1a_b2"), T), ALU.add), "h_b", u)
            for u in R:
                d.need("dve", "o.g", u)
                d.need("dve", "h_b", u)
                d.done(V.tensor_tensor(h[u][:], h[u][:], r[u][:], ALU.add), "h", u)

        def gelu_hidden_tensor(p, w, tag):
            for a in range(2):
                for u in R:
                    if a == 0:
                        p.need("act", tag + ".xT", u)
                    p.done(mm(B[u][1 + a][:], W(w)[:, 128 * a:128 * a + 128], xT[u][lo, :]), f"hid{a}", u)

        def gelu_hidden_scalar(a, bias, func=None):
            for k in range(2):
                for u in R:
                    a.need("pe", f"hid{k}", u)
                    a.done(nc.scalar.activation(H[u][:, k, :], B[u][1 + k][:], ACT.Gelu if func is None else func,
                                                bias=W(bias)[:, k:k + 1]), f"hid{k}", u)

        def weigh_vector(d, t, bank, weight, n, after):
            part = lambda u: pT[u][:, 4 * (t % 2):4 * (t % 2) + 4, :].rearrange("p t n -> p (t n)")[:, 0:64 * n]
            for u in R:
                d.need("pe", after, u)
                if t >= 2:
                    d.need("dve", f"summed{t - 2}", u)
                d.done(V.tensor_tensor(part(u).rearrange("p (e f) -> p e f", e=n), bank(u),
                                       bc(weight(u)[:, t, :], 64), ALU.mult), f"weighed{t}", u)
            for u in R:
                d.need("dve", f"weighed{t}", u)
                d.done(V.reduce_sum(r[u][:, t, :], part(u).rearrange("p (e f) -> p f e", e=n), axis=AX.X),
                       f"summed{t}", u)

        def add_r(d, step="h", after=f"summed{T - 1}"):
            for u in R:
                d.need("dve", after, u)
                d.done(V.tensor_tensor(h[u][:], h[u][:], r[u][:], ALU.add), step, u)

        def l1f_tensor(p):
            flip_tensor(p, "x", x, "x.out")
            gelu_hidden_tensor(p, "l1f_w1", "x")
            for u in R:
                p.need("act", "hid1", u)
                for t in range(T):
                    for a in range(2):
                        last = mm(B[u][3][:, 8 * t:8 * t + 8], H[u][:, a, 128 * t:128 * t + 128],
                                  W("l1f_wg")[:, 8 * a:8 * a + 8], start=(a == 0), stop=(a == 1))
                p.done(last, "logits", u)
            for t in range(T):
                for u in R:
                    if t == 3:
                        p.need("dve", "biased", u)
                    for a in range(2):
                        mm(B[u][t][:], H[u][:, a, 128 * t:128 * t + 128], W("l1f_wd")[:, 512 * a:512 * a + 512],
                           start=(a == 0), stop=False)
                    p.done(mm(B[u][t][:], W("ones")[:, 0:128], W("l1f_bd"), start=False, stop=True), f"out{t}", u)

        def l1f_scalar(a):
            ln_scalar(a, "x", x)
            flip_scalar(a, "x")
            gelu_hidden_scalar(a, "l1f_b1")
            small_exp(a, 8, "exp")

        def l1f_vector(d):
            ln_vector(d, "x", h, x)
            for u in R:
                d.need("pe", "logits", u)
                d.done(V.tensor_tensor(st8(u, 160), tf(B[u][3][:, 0:32]), bmid(W("l1f_bg"), T), ALU.add), "biased", u)
            small_softmax(d, lambda u: st8(u, 160), 8, "biased", "exp", who="dve")
            rank_vector(d, lambda u: st8(u, 96), 8, 1, "before", "probs")
            for u in R:
                d.need("dve", "chosen", u)
                d.done(V.tensor_tensor(st8(u, 128), st8(u, 96), st8(u, 128), ALU.mult), "gates", u)
            for u in R:
                d.need("dve", "gates", u)
            for t in range(T):
                weigh_vector(d, t, lambda u: B[u][t][:].rearrange("p (e f) -> p e f", e=8), lambda u: st8(u, 128), 8,
                             f"out{t}")
            add_r(d)

        a2_v = lambda u: tf(A16[u][:, 0:1024])
        a2_k = lambda u: A16[u][0:32, 1024:1536]
        a2_q = lambda u: A16[u][:, 1536:1664].rearrange("p (g r) -> p g r", r=4)
        a2_q4 = lambda u: tf(A16[u][:, 1664:2176])
        a2_k4 = lambda u: tf(A16[u][:, 2176:2688])
        a2_kv = lambda u: A16[u][:, 2688:3200].rearrange("p (g n) -> p g n", g=2)
        a2_o = lambda u: pT[u][:, 0:8, :].rearrange("p (a t) n -> p a (t n)", a=2)

        def spread(u, dst, k, part):
            rep = 2 * k + (0 if part is lo else 1)
            return dst(u)[part, k:T:2, 32 * rep:32 * rep + 32]

        def l2a_tensor(p):
            flip_tensor(p, "x", r, "r.out")
            gelu_hidden_tensor(p, "l2a_wx", "x")
            for u in R:
                p.need("act", "hid1", u)
                for t in range(T):
                    for a in range(2):
                        last = mm(B[u][3][:, 32 * t:32 * t + 32], H[u][:, a, 128 * t:128 * t + 128],
                                  W("l2a_wq")[:, 32 * a:32 * a + 32], start=(a == 0), stop=(a == 1))
                p.done(last, "q", u)
            for u in R:
                for a in range(2):
                    last = mm(B[u][0][0:32, :], W("l2a_wk")[:, 32 * a:32 * a + 32], H[u][:, a, :], start=(a == 0),
                              stop=(a == 1))
                p.done(last, "k", u)
            for u in R:
                for t in range(T):
                    for a in range(2):
                        c = 256 * (t % 2) + 128 * a
                        last = mm(B[u][1 + t // 2][:, c:c + 128], H[u][:, a, 128 * t:128 * t + 128], W("l2a_wv"))
                p.done(last, "v", u)
            for u in R:
                p.need("dve", "kprob", u)
                p.need("dve", "diff", u)
                for t in range(T):
                    last = nc.tensor.transpose(B[u][3][:, 32 * t:32 * t + 32], a2_k(u)[:, 128 * t:128 * t + 128],
                                               eye[0:32, 0:32])
                p.done(last, "kT", u)
            for u in R:
                p.need("act", "k4", u)
                p.need("act", "v", u)
                for t in range(T):
                    last = mm(B[u][0][:, 256 * (t // 2):256 * (t // 2) + 256], a2_k4(u)[:, t, :], a2_v(u)[:, t, :],
                              start=(t % 2 == 0), stop=(t % 2 == 1))
                p.done(last, "kv", u)
            for u in R:
                p.need("dve", "q4", u)
                for t in range(T):
                    last = nc.tensor.transpose(B[u][1][:, 128 * t:128 * t + 128], a2_q4(u)[:, t, :], eye)
                p.done(last, "q4T", u)
            for a in range(2):
                for u in R:
                    if a == 0:
                        p.need("act", "q4T", u)
                        p.need("dve", "kv", u)
                    for g in range(2):
                        last = mm(B[u][2 + a][:, 256 * g:256 * g + 256], a2_kv(u)[:, g, 128 * a:128 * a + 128],
                                  Q[u][:, 256 * g:256 * g + 256])
                    p.done(last, f"o{a}", u)
            for u in R:
                p.need("act", "o0", u)
                p.need("dve", "o1", u)
                for t in range(T):
                    for a in range(2):
                        last = mm(B[u][0][:, 64 * t:64 * t + 64], a2_o(u)[:, a, 128 * t:128 * t + 128],
                                  W("l2a_wo")[:, 64 * a:64 * a + 64], start=(a == 0), stop=(a == 1))
                p.done(last, "wo", u)
            flip_tensor(p, "f", r, "f.out")
            for a in range(2):
                for u in R:
                    if a == 0:
                        p.need("act", "f.xT", u)
                    p.done(mm(B[u][1 + a][:], W("l2a_w1")[:, 128 * a:128 * a + 128], xT[u][lo, :]), f"ff{a}", u)
            for u in R:
                p.need("act", "ff1", u)
                for t in range(T):
                    for a in range(2):
                        last = mm(B[u][3][:, 64 * t:64 * t + 64], H[u][:, a, 128 * t:128 * t + 128],
                                  W("l2a_w2")[:, 64 * a:64 * a + 64], start=(a == 0), stop=(a == 1))
                p.done(last, "ff", u)

        def l2a_pool(p):
            ln_pool(p, "x")
            for u in R:
                p.need("dve", "x.out", u)
                p.done(nc.gpsimd.memset(A16[u][:, 1664:2688], 0.0), "zeros", u)
            ln_pool(p, "r")
            ln_pool(p, "f")

        def l2a_scalar(a):
            ln_scalar(a, "x", x)
            ln_scalar(a, "r", r)
            flip_scalar(a, "x", scale="l2a_g", bias="l2a_b")
            gelu_hidden_scalar(a, "l2a_bx", func=ACT.Identity)
            exp_scalar(a, a2_q)
            for u in R:
                a.need("dve", "kdiff", u)
                a.done(nc.scalar.activation(a2_k(u), a2_k(u), ACT.Exp), "kexp", u)
            for u in R:
                a.need("pe", "v", u)
                for b in range(2):
                    last = nc.scalar.activation(a2_v(u)[:, 2 * b:2 * b + 2, :], tf(B[u][1 + b][:], 2), ACT.Identity)
                a.done(last, "v", u)
            for u in R:
                a.need("pe", "kT", u)
                a.need("pool", "zeros", u)
                for k in range(2):
                    for part in (lo, hi):
                        last = nc.scalar.activation(spread(u, a2_k4, k, part), tf(B[u][3][:, 0:128])[part, k:T:2, :],
                                                    ACT.Identity)
                a.done(last, "k4", u)
            for u in R:
                a.need("pe", "q4T", u)
                a.done(nc.scalar.activation(Q[u][:], B[u][1][:], ACT.Identity), "q4T", u)
            for u in R:
                a.need("pe", "o0", u)
                a.done(nc.scalar.activation(a2_o(u)[:, 0, :], B[u][2][:], ACT.Identity), "o0", u)
            ln_scalar(a, "f", r)
            flip_scalar(a, "f", scale="l2a_g2", bias="l2a_b2")
            for k in range(2):
                for u in R:
                    a.need("pe", f"ff{k}", u)
                    a.done(nc.scalar.activation(H[u][:, k, :], B[u][1 + k][:], ACT.Gelu, bias=W("l2a_fb1")[:, k:k + 1]),
                           f"ff{k}", u)

        def l2a_vector(d):
            ln_vector(d, "x", h, x)
            ln_vector(d, "r", x, r, first=lambda u: d.need("dve", "x.out", u))
            softmax_vector(d, lambda u: B[u][3][:, 0:128].rearrange("p (g r) -> p g r", r=4), a2_q, 32,
                           after=("pe", "q"))
            for u in R:
                d.need("pool", "zeros", u)
                d.need("dve", "recip", u)
                for k in range(2):
                    for part in (lo, hi):
                        last = V.tensor_tensor(spread(u, a2_q4, k, part).rearrange("p t (h r) -> p t h r", r=4),
                                               a2_q(u)[part].rearrange("p (t h) r -> p t h r", t=T)[:, k:T:2],
                                               bc(st[u][part, 48:80].rearrange("p (t h) -> p t h", t=T)[:, k:T:2], 4),
                                               ALU.mult)
                d.done(last, "q4", u)
            kb = lambda ap: ap.rearrange("p (b n) -> p b n", n=SEQ)
            for u in R:
                d.need("pe", "k", u)
                d.done(V.reduce_max(st[u][0:32, 80:88], kb(B[u][0][0:32, :]), axis=AX.X), "kmax", u)
            for u in R:
                d.need("dve", "kmax", u)
                d.done(V.tensor_tensor(kb(a2_k(u)), kb(B[u][0][0:32, :]), bc(st[u][0:32, 80:88], SEQ), ALU.subtract),
                       "kdiff", u)
            for u in R:
                d.need("act", "kexp", u)
                d.done(V.reduce_sum(st[u][0:32, 88:96], kb(a2_k(u)), axis=AX.X), "ksum", u)
            for u in R:
                d.need("dve", "ksum", u)
                d.done(V.reciprocal(st[u][0:32, 88:96], st[u][0:32, 88:96]), "krecip", u)
            for u in R:
                d.need("dve", "krecip", u)
                d.done(V.tensor_tensor(kb(a2_k(u)), kb(a2_k(u)), bc(st[u][0:32, 88:96], SEQ), ALU.mult), "kprob", u)
            for u in R:
                d.need("pe", "kv", u)
                d.done(V.tensor_tensor(a2_kv(u), tf(B[u][0][:], 2), bmid(W("diag32"), 2), ALU.mult), "kv", u)
            for u in R:
                d.need("pe", "o1", u)
                d.done(V.tensor_copy(a2_o(u)[:, 1, :], B[u][3][:]), "o1", u)
            for u in R:
                d.done(V.tensor_tensor(x[u][:], x[u][:], bmid(W("l2a_bo"), T), ALU.add), "x_bo", u)
            for u in R:
                d.need("pe", "wo", u)
                d.need("dve", "x_bo", u)
                d.done(V.tensor_tensor(x[u][:], x[u][:], tf(B[u][0][:, 0:256]), ALU.add), "fx", u)
            ln_vector(d, "f", x, r, first=lambda u: d.need("dve", "fx", u))
            for u in R:
                d.done(V.tensor_tensor(x[u][:], x[u][:], bmid(W("l2a_fb2"), T), ALU.add), "fx_b", u)
            for u in R:
                d.need("dve", "fx_b", u)
                d.done(V.tensor_tensor(h[u][:], h[u][:], x[u][:], ALU.add), "h_fx", u)
            for u in R:
                d.need("pe", "ff", u)
                d.need("dve", "h_fx", u)
                d.done(V.tensor_tensor(h[u][:], h[u][:], tf(B[u][3][:, 0:256]), ALU.add), "h", u)

        e1 = lambda u, e: pT[u][:, 4 * (e % 2):4 * (e % 2) + 4, :].rearrange("p t n -> p (t n)")

        def l2f_tensor(p):
            flip_tensor(p, "x", x, "x.out")
            for u in R:
                p.need("act", "x.xT", u)
                for t in range(T):
                    last = mm(B[u][3][:, 4 * t:4 * t + 4], xT[u][lo, 128 * t:128 * t + 128], W("l2f_g"))
                p.done(last, "logits", u)
            for u in R:
                p.done(mm(B[u][0][lo, :], W("l2f_s1"), xT[u][lo, :]), "s1", u)
            for u in R:
                p.need("act", "s1", u)
                p.done(mm(B[u][1][:], W("l2f_s2"), Q[u][lo, :]), "s2", u)
            for u in R:
                p.need("act", "s2", u)
                for t in range(T):
                    last = mm(B[u][2][:, 64 * t:64 * t + 64], K[u][:, 128 * t:128 * t + 128], W("l2f_s3"))
                p.done(last, "s3", u)
            for e in range(5):
                if e < 4:
                    for u in R:
                        if e >= 2:
                            p.need("act", f"e1_{e - 2}", u)
                        p.done(mm(B[u][e % 2][:], W("l2f_e1")[:, 128 * e:128 * e + 128], xT[u][lo, :]), f"e1_{e}", u)
                if e:
                    k = e - 1
                    for u in R:
                        p.need("act", f"e1_{k}", u)
                        if k == 0:
                            p.need("dve", "biased", u)
                        if k == 2:
                            p.need("dve", "e2_0", u)
                        o = slice(64 * (k % 2), 64 * (k % 2) + 64)
                        p.done(mm(B[u][3][o, :], W("l2f_e2")[:, 64 * k:64 * k + 64], e1(u, k)), f"e2_{k}", u)
            for b in range(2):
                for u in R:
                    p.need("dve", "e2_1", u)
                    for t in (2 * b, 2 * b + 1):
                        o = B[u][b][:, 256 * (t % 2):256 * (t % 2) + 256]
                        mm(o, W("ones")[:, 0:128], W("l2f_eb3"), start=True, stop=False)
                        for k in range(2):
                            last = mm(o[:, 128 * k:128 * k + 128], H[u][:, k, 128 * t:128 * t + 128],
                                      W("l2f_e3")[:, 128 * k:128 * k + 128], start=False, stop=(k == 1))
                    p.done(last, f"out{b}", u)

        def l2f_scalar(a):
            ln_scalar(a, "x", x)
            flip_scalar(a, "x")
            for u in R:
                a.need("pe", "s1", u)
                a.done(nc.scalar.activation(Q[u][lo, :], B[u][0][lo, :], ACT.Relu, bias=W("l2f_sb1")), "s1", u)
            for u in R:
                a.need("pe", "s2", u)
                a.done(nc.scalar.activation(K[u][:], B[u][1][:], ACT.Relu, bias=W("l2f_sb2")), "s2", u)
            small_exp(a, 4, "exp")
            for e in range(4):
                for u in R:
                    a.need("pe", f"e1_{e}", u)
                    if e >= 2:
                        a.need("pe", f"e2_{e - 2}", u)
                    a.done(nc.scalar.activation(e1(u, e), B[u][e % 2][:], ACT.Relu, bias=W("l2f_eb1")[:, e:e + 1]),
                           f"e1_{e}", u)
            for u in R:
                a.need("dve", "tdiff", u)
                a.done(nc.scalar.activation(st8(u, 96, 4), st8(u, 96, 4), ACT.Exp), "texp", u)

        def l2f_vector(d):
            ln_vector(d, "x", h, x)
            for u in R:
                d.need("pe", "logits", u)
                d.done(V.tensor_tensor(st8(u, 160, 4), tf(B[u][3][:, 0:16]), bmid(W("l2f_gb"), T), ALU.add), "biased", u)
            small_softmax(d, lambda u: st8(u, 160, 4), 4, "biased", "exp", who="dve")
            for k in range(2):
                for u in R:
                    d.need("pe", f"e2_{2 * k + 1}", u)
                    d.done(V.tensor_scalar(H[u][:, k, :], B[u][3][:], W("l2f_eb2")[:, k:k + 1], 0.0, ALU.add, ALU.max),
                           f"e2_{k}", u)
            rank_vector(d, lambda u: st8(u, 96, 4), 4, 2, "before4", "probs")
            for u in R:
                d.need("dve", "chosen", u)
                d.done(V.reduce_max(st[u][:, 80:84], st8(u, 96, 4), axis=AX.X), "tmax", u)
            for u in R:
                d.need("dve", "tmax", u)
                d.done(V.tensor_tensor(st8(u, 96, 4), st8(u, 96, 4), bc(st[u][:, 80:84], 4), ALU.subtract), "tdiff", u)
            for u in R:
                d.need("act", "texp", u)
                d.done(V.tensor_tensor(st8(u, 128, 4), st8(u, 96, 4), st8(u, 128, 4), ALU.mult), "tkept", u)
            for u in R:
                d.need("dve", "tkept", u)
                d.done(V.reduce_sum(st[u][:, 84:88], st8(u, 128, 4), axis=AX.X), "tsum", u)
            for u in R:
                d.need("dve", "tsum", u)
                d.done(V.reciprocal(st[u][:, 84:88], st[u][:, 84:88]), "trecip", u)
            for u in R:
                d.need("dve", "trecip", u)
                d.done(V.tensor_tensor(st8(u, 128, 4), st8(u, 128, 4), bc(st[u][:, 84:88], 4), ALU.mult), "gates", u)
            for u in R:
                d.done(V.tensor_tensor(h[u][:], h[u][:], bmid(W("l2f_sb3"), T), ALU.add), "h_b", u)
            for u in R:
                d.need("pe", "s3", u)
                d.need("dve", "h_b", u)
                d.done(V.tensor_tensor(h[u][:], h[u][:], tf(B[u][2][:, 0:256]), ALU.add), "h_s", u)
            for u in R:
                d.need("dve", "gates", u)
            for t in range(T):
                weigh_vector(d, t, lambda u: B[u][t // 2][:, 256 * (t % 2):256 * (t % 2) + 256]
                             .rearrange("p (e f) -> p e f", e=4), lambda u: st8(u, 128, 4), 4, f"out{t // 2}")
            add_r(d)

        V8 = lambda u: tf(A16[u][:, 0:2048])
        o3 = lambda u, k: pT[u][:, 4 * k:4 * k + 4, :].rearrange("p t n -> p (t n)")

        def l3a_tensor(p):
            flip_tensor(p, "x", x, "x.out")
            for t in (1, 2, 3, 0):
                for u in R:
                    if t == 1:
                        p.need("act", "x.xT", u)
                    p.done(mm(B[u][t][:], xT[u][lo, 128 * t:128 * t + 128], W("l3a_v")), f"v{t}", u)
            for k in range(4):
                cols = slice(128 * k, 128 * k + 128)
                for u in R:
                    if k == 0:
                        p.need("act", "v0", u)
                    else:
                        p.need("act", f"o{k - 1}", u)
                    p.done(mm(B[u][0][:], W("l3a_q")[:, cols], xT[u][lo, :]), f"q{k}", u)
                for u in R:
                    if k == 0:
                        p.need("dve", "v1", u)
                    else:
                        p.need("dve", f"k{k - 1}", u)
                    p.done(mm(B[u][1][:], W("l3a_k")[:, cols], xT[u][lo, :]), f"k{k}", u)
                for g, part in enumerate((lo, hi)):
                    for u in R:
                        if g == 0:
                            p.need("act", f"q{k}", u)
                            p.need("dve", f"k{k}", u)
                        if k == 0 and g == 0:
                            p.need("dve", "v3", u)
                            p.need("act", "v2", u)
                        for b in range(BATCHES):
                            o = slice(64 * (b % 2), 64 * (b % 2) + 64)
                            last = mm(B[u][2 + g][o, 64 * (b // 2):64 * (b // 2) + 64], K[u][part, 64 * b:64 * b + 64],
                                      Q[u][part, 64 * b:64 * b + 64])
                        p.done(last, f"s{k}_{g}", u)
                for u in R:
                    p.need("act", f"p{k}_1", u)
                    for g, part in enumerate((lo, hi)):
                        for t in range(T):
                            last = mm(B[u][0][part, 128 * t:128 * t + 128],
                                      V8(u)[:, t, 64 * (2 * k + g):64 * (2 * k + g) + 64], pbd[u][:, 4 * g + t, :])
                    p.done(last, f"o{k}", u)
            for u in R:
                p.need("act", "o3", u)
                p.need("dve", "k3", u)
                for t in range(T):
                    for k in range(4):
                        last = mm(B[u][1][:, 64 * t:64 * t + 64], o3(u, k)[:, 128 * t:128 * t + 128],
                                  W("l3a_o")[:, 64 * k:64 * k + 64], start=(k == 0), stop=(k == 3))
                p.done(last, "wo", u)

        def l3a_scalar(a):
            ln_scalar(a, "x", x)
            flip_scalar(a, "x")
            for t in (2, 0):
                for u in R:
                    a.need("pe", f"v{t}", u)
                    a.done(nc.scalar.activation(V8(u)[:, t, :], B[u][t][:], ACT.Identity), f"v{t}", u)
            for k in range(4):
                for u in R:
                    a.need("pe", f"q{k}", u)
                    a.done(nc.scalar.activation(Q[u][:], B[u][0][:], ACT.Identity), f"q{k}", u)
                for g in range(2):
                    for u in R:
                        a.need("pe", f"s{k}_{g}", u)
                        for part in (lo, hi):
                            last = nc.scalar.activation(pbd[u][part, 4 * g:4 * g + 4, part],
                                                        tf(B[u][2 + g][:, 0:256])[part], ACT.Sigmoid, scale=8.0)
                        a.done(last, f"p{k}_{g}", u)
                for u in R:
                    a.need("pe", f"o{k}", u)
                    a.done(nc.scalar.activation(o3(u, k), B[u][0][:], ACT.Identity), f"o{k}", u)

        def l3a_vector(d):
            ln_vector(d, "x", h, x)
            for t in (1, 3):
                for u in R:
                    d.need("pe", f"v{t}", u)
                    d.done(V.tensor_copy(V8(u)[:, t, :], B[u][t][:]), f"v{t}", u)
            for k in range(4):
                for u in R:
                    d.need("pe", f"k{k}", u)
                    d.done(V.tensor_copy(K[u][:], B[u][1][:]), f"k{k}", u)
            for u in R:
                d.need("pe", "wo", u)
                d.done(V.scalar_tensor_tensor(out=h[u][:], in0=tf(B[u][1][:, 0:256]), scalar=0.0, in1=h[u][:],
                                              op0=ALU.max, op1=ALU.add), "h", u)

        he = lambda u, e: A16[u][:, 512 * e:512 * e + 512]

        def l3f_tensor(p):
            flip_tensor(p, "x", x, "x.out")
            for u in R:
                p.need("act", "x.xT", u)
                for t in range(T):
                    last = mm(B[u][3][:, 8 * t:8 * t + 8], xT[u][lo, 128 * t:128 * t + 128], W("l3f_g"))
                p.done(last, "logits", u)
            for e in range(8):
                for u in R:
                    if e >= 2:
                        p.need("act", f"hid{e - 2}", u)
                    p.done(mm(B[u][e % 2][:], W("l3f_w1")[:, 128 * e:128 * e + 128], xT[u][lo, :]), f"hid{e}", u)
            for t in range(T):
                for u in R:
                    if t == 0:
                        p.need("act", "hid7", u)
                    if t == 1:
                        p.need("dve", "biased", u)
                    if t >= 2:
                        p.need("dve", f"weighed{t - 2}", u)
                    o = B[u][2 + t % 2]
                    mm(o[:], W("ones")[:, 0:128], W("l3f_b2"), start=True, stop=False)
                    for e in range(8):
                        last = mm(o[:, 64 * e:64 * e + 64], he(u, e)[:, 128 * t:128 * t + 128],
                                  W("l3f_w2")[:, 64 * e:64 * e + 64], start=False, stop=(e == 7))
                    p.done(last, f"out{t}", u)

        def l3f_scalar(a):
            ln_scalar(a, "x", x)
            flip_scalar(a, "x")
            for e in range(8):
                for u in R:
                    a.need("pe", f"hid{e}", u)
                    a.done(nc.scalar.activation(he(u, e), B[u][e % 2][:], ACT.Gelu, bias=W("l3f_b1")[:, e:e + 1]),
                           f"hid{e}", u)

        def l3f_vector(d):
            ln_vector(d, "x", h, x)
            for u in R:
                d.need("pe", "logits", u)
                d.done(V.tensor_tensor(st8(u, 160), tf(B[u][3][:, 0:32]), bmid(W("l3f_bg"), T), ALU.add), "biased", u)
            rank_vector(d, lambda u: st8(u, 160), 8, 2, "before", "biased")
            for u in R:
                d.need("dve", "chosen", u)
            for t in range(T):
                weigh_vector(d, t, lambda u: B[u][2 + t % 2][:].rearrange("p (e f) -> p e f", e=8),
                             lambda u: st8(u, 128), 8, f"out{t}")
            add_r(d)

        STAGES = ("l0b", "l0f", "l1a", "l1f", "l2a", "l2f", "l3a", "l3f")
        norms = {"l0a": ("x",), "l0b": (), "l0f": ("x", "r", "f"), "l1a": ("x", "r", "o"), "l1f": ("x",),
                 "l2f": ("x",), "l3a": ("x",), "l3f": ("x",)}
        tensor = dict(l0b=l0b_tensor, l0f=l0f_tensor, l1a=l1a_tensor, l1f=l1f_tensor, l2a=l2a_tensor, l2f=l2f_tensor,
                      l3a=l3a_tensor, l3f=l3f_tensor)
        scalar = dict(l0b=l0b_scalar, l0f=l0f_scalar, l1a=l1a_scalar, l1f=l1f_scalar, l2a=l2a_scalar, l2f=l2f_scalar,
                      l3a=l3a_scalar, l3f=l3f_scalar)
        vector = dict(l0b=l0b_vector, l0f=l0f_vector, l1a=l1a_vector, l1f=l1f_vector, l2a=l2a_vector, l2f=l2f_vector,
                      l3a=l3a_vector, l3f=l3f_vector)
        NBN = 16
        block = ctx.enter_context(nc.Block())

        @block.sync
        def _(sp):
            sp.dma_start(wts[:], weights_dram).then_inc(loaded, 16)
            sp.dma_start(cst[:], consts_dram).then_inc(loaded, 16)
            tiles = tok.rearrange("(b t p) f -> b p t f", t=T, p=128)
            outs = out_dram.rearrange("(b t p) f -> b p t f", t=T, p=128)
            for u in R:
                sp.dma_start(h[u][:], tiles[u]).then_inc(h_in[u], 16)
            with sp.Fori(1, ITERS) as it:
                for u in R:
                    sp.wait_ge(sig.sem("l0a", "dve"), sig.count("l0a", "dve", "hx", u, it) - sig.count("l0a", "dve", "hx", u, 1) + sig.count("l0a", "dve", "hx", u, 0))
                    sp.wait_ge(ready, 1)
                    sp.dma_start(h[u][:], tiles[bass.ds(blk(it, u), 1)].rearrange("b p t f -> (b p) t f"))\
                        .then_inc(h_in[u], 16)
            with sp.Fori(0, ITERS) as it:
                for u in R:
                    sp.wait_ge(sig.sem(STAGES[-1], "dve"), sig.count(STAGES[-1], "dve", "h", u, it))
                    sp.wait_ge(ready, 1)
                    sp.dma_start(outs[bass.ds(blk(it, u), 1)].rearrange("b p t f -> (b p) t f"), h[u][:])\
                        .then_inc(out_sent[u], 16)
            for u in R:
                sp.wait_ge(out_sent[u], 16 * ITERS)

        @block.gpsimd
        def _(pool):
            pool.wait_ge(loaded, 32)
            with pool.Fori(0, ITERS) as it:
                ln_pool(Engine(sig, "pool", pool, "l0a", it), "x")
            pool.wait_ge(bn_done["dve"], 4)
            nc.gpsimd.tensor_tensor(bn[:, 19:20], bn[:, 18:19], W("mhalf")[lo, 0:1], ALU.pow).then_inc(bn_done["pool"], 1)
            with pool.Fori(0, ITERS) as it:
                for stage in STAGES:
                    p = Engine(sig, "pool", pool, stage, it, apart=(stage == "l2a"))
                    if stage == "l2a":
                        l2a_pool(p)
                    else:
                        for tag in norms[stage]:
                            ln_pool(p, tag)

        @block.tensor
        def _(pe):
            pe.wait_ge(loaded, 32)
            with pe.Fori(0, ITERS) as it:
                l0a_tensor(Engine(sig, "pe", pe, "l0a", it, apart=True))
            with pe.Fori(0, ITERS) as it:
                for stage in STAGES:
                    tensor[stage](Engine(sig, "pe", pe, stage, it, apart=True))

        @block.scalar
        def _(act):
            act.wait_ge(loaded, 32)
            with act.Fori(0, ITERS) as it:
                l0a_scalar(Engine(sig, "act", act, "l0a", it))
            act.wait_ge(bn_done["dve"], 2)
            for c in range(NBN):
                nc.scalar.activation(tmp[0][lo, :], hl[:, BLK * c:BLK * c + BLK], ACT.Square, bias=bn[:, 17:18],
                                     accum_out=bn[:, c:c + 1]).then_inc(bn_done["act"], 1)
                act.wait_ge(bn_done["act"], c + 1)
            
            with act.Fori(0, ITERS) as it:
                for stage in STAGES:
                    scalar[stage](Engine(sig, "act", act, stage, it))

        @block.vector
        def _(dve):
            for u in R:
                nc.vector.memset(xT[u][64:65, :], 1.0)
                nc.vector.memset(oT[u][64:65, :], 1.0)
                last = nc.vector.memset(pbd[u][:], 0.0)
            last.then_inc(ready, 1)
            dve.wait_ge(loaded, 32)
            with dve.Fori(0, ITERS) as it:
                l0a_vector(Engine(sig, "dve", dve, "l0a", it))
            done = bn_done["dve"]
            def step(ins, n):
                ins.then_inc(done, 1)
                dve.wait_ge(done, n)
            dve.wait_ge(sig.sem("l0a", "dve"), sig.count("l0a", "dve", "hl", U - 1, ITERS - 1))
            step(V.reduce_sum(bn[:, 16:17], hl[:], axis=AX.X), 1)
            step(V.tensor_scalar(bn[:, 17:18], bn[:, 16:17], -1.0 / TOKENS, None, ALU.mult), 2)
            dve.wait_ge(bn_done["act"], NBN)
            step(V.reduce_sum(bn[:, 18:19], bn[:, 0:NBN], axis=AX.X), 3)
            step(V.tensor_scalar(bn[:, 18:19], bn[:, 18:19], 1.0 / TOKENS, 1e-5, ALU.mult, ALU.add), 4)
            dve.wait_ge(bn_done["pool"], 1)
            step(V.tensor_tensor(bn[:, 20:21], bn[:, 19:20], W("l0a_gamma"), ALU.mult), 5)
            with dve.Fori(0, ITERS) as it:
                for n, stage in enumerate(STAGES):
                    d = Engine(sig, "dve", dve, stage, it)
                    d.before = STAGES[n - 1]
                    vector[stage](d)



def tokenizer_inputs(i):
    g = lambda k: np.asarray(i["L0_tok_" + k])
    d = {}
    d["x_pairs"] = np.asarray(i["x"]).reshape(PAIRS, 2, J, 2, COLS, 3).transpose(0, 1, 3, 5, 2, 4).reshape(PAIRS, 12, PIX)
    d["grid_rows"] = g("input_grid").reshape(J, 2, COLS, 2).transpose(1, 3, 0, 2).reshape(4, PIX)
    d["embed_w"], d["embed_b"] = g("P_w"), g("P_b")
    wr, wi = (g(k).transpose(0, 3, 1, 4, 2) for k in ("spec_wr", "spec_wi"))
    d["spec_uv"] = np.concatenate([np.concatenate([wr, wi], 2).reshape(LAYERS, MX, 64, CH),
                                   np.concatenate([wi, wr], 2).reshape(LAYERS, MX, 64, CH)], 3)
    d["conv_w"], d["conv_b"] = g("conv_w").transpose(0, 3, 2, 4, 1), g("conv_b")
    d["q1_w"], d["q1_b"], d["q2_w"], d["q2_b"] = g("Q1_w"), g("Q1_b"), g("Q2_w"), g("Q2_b")
    d["fwd"], d["inv"], d["tw"], d["eye"] = tokenizer_constants()
    return d


def kernel(**inputs):
    import concourse.bacc as bacc
    from concourse.bass_utils import run_bass_kernel_spmd

    nc = bacc.Bacc("TRN2", target_bir_lowering=False, num_devices=1)
    arrays = tokenizer_inputs(inputs)
    arrays["weights"], where_w = packed(block_weights(inputs))
    arrays["constants"], where_c = packed(block_constants())
    arrays = {"in_" + k: np.ascontiguousarray(v) for k, v in arrays.items()}
    a = {k[3:]: nc.dram_tensor(k, v.shape, mybir.dt.from_np(v.dtype), kind="ExternalInput").ap()
         for k, v in arrays.items()}
    out = nc.dram_tensor("out_0_dram", (IMGS, ROWS, COLS), F32, kind="ExternalOutput").ap()
    scratch = lambda name, shape: nc.dram_tensor(name, shape, F32, kind="Internal").ap()
    tokens = scratch("tokens", (IMGS, ROWS, COLS))
    build_tokenizer(nc, a["x_pairs"], a["grid_rows"], a["embed_w"], a["embed_b"], a["spec_uv"], a["conv_w"],
                    a["conv_b"], a["q1_w"], a["q1_b"], a["q2_w"], a["q2_b"], a["fwd"], a["inv"], a["tw"], a["eye"],
                    tokens.rearrange("g (j s) w -> g s j w", s=2),
                    scratch("h_rows", (PAIRS, 2, 2, WID, PIX)), scratch("g_modes", (IMGS, 2, WID, 2, MX * MY)),
                    scratch("m_modes", (PAIRS, 2, MODES, 64)))
    build_blocks(nc, tokens.rearrange("g n f -> (g n) f"), out.rearrange("g n f -> (g n) f"), a["weights"],
                 a["constants"], where_w, where_c)
    result = run_bass_kernel_spmd(nc, [arrays], core_ids=[0])
    return result.results[0]["out_0_dram"]
```

```python
import numpy as np
import concourse.bass as bass
from concourse import mybir
from contextlib import ExitStack

F32 = mybir.dt.float32
ACT = mybir.ActivationFunctionType
ALU = mybir.AluOpType
AX = mybir.AxisListType

IMGS, ROWS, COLS, WID, LAYERS = 128, 64, 64, 32, 4
MX, MY = 16, 16
J = ROWS // 2
PIX = J * COLS
MODES = 2 * MX * MY
CH = 512
NCH = PIX // CH
PAIRS = IMGS // 2
KXT = 4


ORDER = (0, 2, 1, 3)
EVEN_FIRST = np.concatenate([np.arange(0, 16, 2), np.arange(1, 16, 2)])


def tokenizer_constants():
    a = np.arange(8)
    cls = [(px, py) for px in range(2) for py in range(2)]
    j, w = np.arange(16).reshape(4, 4), np.arange(32)
    fwd = np.zeros((4, 4, 32, 4, 2, 8, 8))
    inv = np.zeros((4, 8, 8, 2, 16, 32))
    for k, (px, py) in enumerate(cls):
        kx, ky = 2 * a + px, 2 * a + py
        ang = 2 * np.pi * (kx[:, None] * 2 * j[:, :, None, None, None] / ROWS + ky * w[:, None, None] / COLS)
        fwd[:, :, :, k, 0], fwd[:, :, :, k, 1] = np.cos(ang), -np.sin(ang)
        c = np.where(ky == 0, 1.0, 2.0)[:, None, None] / (ROWS * COLS)
        ang = 2 * np.pi * (kx[:, None, None, None] * 2 * np.arange(16)[:, None] / ROWS + ky[:, None, None] * w / COLS)
        inv[k, :, :, 0], inv[k, :, :, 1] = c * np.cos(ang), -c * np.sin(ang)
    fwd = fwd.transpose(1, 2, 0, 3, 4, 5, 6).reshape(128, 4, 4, 128)
    inv = inv.reshape(4, 128, CH).transpose(1, 0, 2)
    kx = EVEN_FIRST
    tw = np.zeros((2, 2, WID, MX, 2, 4))
    for si in range(2):
        for so in range(2):
            phi = 2 * np.pi * kx * (so - si) / ROWS
            for ri in range(2):
                sg = 1 if ri == 0 else -1
                tw[si, ri, :, :, so, 0] = sg * np.cos(phi)
                tw[si, ri, :, :, so, 1] = -np.sin(phi)
                tw[si, ri, :, :, so, 2] = np.cos(phi)
                tw[si, ri, :, :, so, 3] = sg * np.sin(phi)
    return (np.ascontiguousarray(fwd, np.float32), np.ascontiguousarray(inv, np.float32),
            np.ascontiguousarray(tw.reshape(128, MX, 8).transpose(1, 0, 2), np.float32),
            np.eye(128, dtype=np.float32))


def build_tokenizer(nc, x_pairs, grid_rows, embed_w, embed_b, spec_uv, conv_w, conv_b, q1_w, q1_b, q2_w, q2_b,
                    fwd_dram, inv_dram, tw_dram, eye_dram, tok, h_dram, g_dram, m_dram):
    with ExitStack() as ctx:
        sb = lambda n, s: ctx.enter_context(nc.sbuf_tensor(n, s, F32))
        pb = lambda n: ctx.enter_context(nc.psum_tensor(n, [128, CH], F32))
        sem = lambda n: ctx.enter_context(nc.semaphore(n))

        arena = sb("arena", [128, 2 * 8192])
        modes_q = [arena[:, 8192 * u:8192 * u + 8192].rearrange("p (n m) -> p n m", n=IMGS) for u in range(2)]
        rows_in = [arena[:, 4096 * u:4096 * u + 4096].rearrange("p (a n) -> p a n", a=2) for u in range(2)]
        rows_out = [arena[:, 8192 + 2048 * u:8192 + 2048 * u + 2048] for u in range(2)]
        fwd = sb("fwd_basis", [128, 4, 4, 128])
        inv = sb("inv_basis", [128, 4, CH])
        eye = sb("eye", [128, 128])
        mode_tile = [sb(f"mode_tile{u}", [128, MX // KXT, 2, 64]) for u in range(2)]
        inverse = [sb(f"inverse{u}", [128, 4, CH]) for u in range(2)]
        inv_copy = [sb(f"inv_copy{k}", [128, CH]) for k in range(2)]
        z_sum = [sb(f"z_sum{k}", [128, CH]) for k in range(2)]
        by_row = sb("by_row", [128, 2, CH])
        folded = [sb(f"folded{k}", [128, 2, 2, CH // 2]) for k in range(2)]
        turned = [sb(f"turned{k}", [128, 2, 2, 2, 128]) for k in range(2)]
        modes_out = [sb(f"modes_out{u}", [128, MODES]) for u in range(2)]
        embed_bd = sb("embed_bd", [16, 128])
        embed_bias = sb("embed_bias", [128, 1])
        conv_bd = sb("conv_bd", [128, 4, 128])
        conv_bias = sb("conv_bias", [128, 1])
        q1_bd = sb("q1_bd", [128, 128])
        q1_bias = sb("q1_bias", [128, 1])
        q1_bias01 = sb("q1_bias01", [128, 1])
        q2_bd = sb("q2_bd", [128, 4])
        q2_bias = sb("q2_bias", [4, 1])
        uv = [sb(f"uv{u}", [128, 2, MY, WID]) for u in range(2)]
        twid = [sb(f"twid{u}", [128, 8]) for u in range(2)]
        partial = [sb(f"partial{u}", [128, MY, WID]) for u in range(2)]
        mix_w = [sb(f"mix_w{u}", [128, MY, 2, 2, WID]) for u in range(2)]
        mixed = [sb(f"mixed{u}", [128, MY * 128]) for u in range(2)]
        xg = [mixed[u][0:16, :] for u in range(2)]
        leaky = [turned[u][:, 0, :, :, :].rearrange("p y b n -> p (y b n)") for u in range(2)]
        tok_out = [mix_w[u][0:4, :, :, :, :].rearrange("p y r s o -> p (y r s o)") for u in range(2)]

        zbank = [pb("zbank0"), pb("zbank1")]
        tbank = [pb("tbank0"), pb("tbank1")]
        gbank = [pb("gbank0"), pb("gbank1")]
        abank = [pb("abank0"), pb("abank1")]
        mbank = [zbank[0], zbank[1], tbank[0], tbank[1]]

        consts = sem("consts_loaded")
        zeroed = sem("tiles_zeroed")
        zeroed_v = sem("borders_zeroed")
        conv_in = sem("conv_weights_loaded")
        q_ready = sem("q_bias_scaled")
        xg_in = [sem(f"xg_loaded{u}") for u in range(2)]
        rows_loaded = [sem(f"rows_loaded{u}") for u in range(2)]
        modes_loaded = [sem(f"modes_loaded{u}") for u in range(2)]
        z_done = sem("z_done")
        z_copied = sem("z_copied")
        z_based = sem("z_plus_base")
        z_full = sem("z_full")
        a_done = sem("inverse_done")
        a_copied = sem("inverse_copied")
        a_summed = sem("inverse_summed")
        h_new = sem("h_new")
        flip_done = sem("flip_done")
        turned_copied = sem("turned_copied")
        rows_folded = sem("rows_folded")
        cols_folded = sem("cols_folded")
        fwd_done = sem("fwd_done")
        g_ready = sem("g_ready")
        h_stored = [sem(f"h_stored{u}") for u in range(2)]
        g_stored = [sem(f"g_stored{u}") for u in range(2)]
        q1_done = sem("q1_done")
        q1_scaled = sem("q1_scaled")
        q1_leaky = sem("q1_leaky")
        q2_done = sem("q2_done")
        tok_ready = sem("tok_ready")
        tok_stored = [sem(f"tok_stored{u}") for u in range(2)]
        quarter_in = [sem(f"quarter_loaded{u}") for u in range(2)]
        uv_in = [sem(f"uv_loaded{u}") for u in range(2)]
        part_ready = sem("partial_ready")
        mixw_ready = sem("mix_weights_ready")
        mix_done = sem("mix_done")
        mixed_act = sem("mixed_copied_act")
        mixed_dve = sem("mixed_copied_dve")
        m_stored = [sem(f"m_stored{u}") for u in range(2)]

        NP = PAIRS // 2

        def over_pairs(eng, body):
            body(0)
            with eng.Fori(1, NP) as i:
                body(i)

        def sp_constants(sp):
            n = 0
            def load(dst, src):
                nonlocal n
                sp.dma_start(dst, src).then_inc(consts, 16)
                n += 1
            load(fwd[:], fwd_dram)
            load(inv[:], inv_dram)
            load(eye[:], eye_dram)
            for u in range(2):
                load(xg[u][0:4, :], grid_rows)
            sp.wait_ge(zeroed, 4)
            for a in range(2):
                for s in range(2):
                    col = slice(64 * a + 32 * s, 64 * a + 32 * s + 32)
                    load(embed_bd[2 * s:2 * s + 2, col], embed_w[0:2, :])
                    load(embed_bd[4 + 6 * a + 3 * s:4 + 6 * a + 3 * s + 3, col], embed_w[2:5, :])
            for k in range(4):
                part = slice(32 * k, 32 * k + 32)
                load(embed_bias[part, :], embed_b.rearrange("(c o) -> c o", o=1))
                load(q1_bias[part, :], q1_b.rearrange("(c o) -> c o", o=1))
                load(q1_bd[part, part], q1_w)
                load(q2_bd[part, k:k + 1], q2_w)
                load(q2_bias[k:k + 1, :], q2_b.rearrange("(c o) -> c o", o=1))
            assert n == NCONSTS, n

        NCONSTS = 5 + 8 + 20

        def sp_conv_weights(sp, l):
            for so in range(2):
                for dy in range(3):
                    for dw in range(2):
                        col = 64 * dw + 32 * so
                        sp.dma_start(conv_bd[32 * (so + dy):32 * (so + dy) + 32, dw:dw + 3, col:col + 32],
                                     conv_w[bass.ds(l, 1), dy, :, :, :].rearrange("l c x o -> (l c) x o"))\
                            .then_inc(conv_in, 16)
            for k in range(4):
                sp.dma_start(conv_bias[32 * k:32 * k + 32, :],
                             conv_b[bass.ds(l, 1), :].rearrange("l (c o) -> (l c) o", o=1)).then_inc(conv_in, 16)
        NCONV = 16

        def sp_store_rows(sp, u, n, before):
            sp.wait_ge(h_new, NCH * (before + n + 1))
            sp.wait_ge(zeroed, 4)
            sp.dma_start(h_dram[bass.ds(n, 1), :, :, :, :].rearrange("a g s c n -> (a g s c) n"),
                         rows_out[u]).then_inc(h_stored[u], 16)

        def sp_store_modes(sp, u, n, before):
            sp.wait_ge(g_ready, before + n + 1)
            sp.wait_ge(zeroed, 4)
            sp.dma_start(g_dram[:, :, :, :, bass.ds(2 * n, 2), :].rearrange("s c r q a m -> a (s c) (r q) m"),
                         modes_out[u][:].rearrange("p (k m) -> p k m", k=8)).then_inc(g_stored[u], 16)

        def sp_store_tokens(sp, u, n):
            sp.wait_ge(tok_ready, NCH * (n + 1))
            sp.wait_ge(zeroed, 4)
            for a in range(2):
                sp.dma_start(tok[bass.ds(2 * n + a, 1), :, :, :].rearrange("g s j w -> (g s) j w"),
                             tok_out[u][2 * a:2 * a + 2, :].rearrange("p (j w) -> p j w", w=COLS))\
                    .then_inc(tok_stored[u], 16)

        def sp_stores(sp, u, n, before):
            if not (isinstance(n, int) and n < 2):
                sp_store_modes(sp, u, n - 2, before)
            if not (isinstance(n, int) and n == 0):
                sp_store_rows(sp, 1 - u, n - 1, before)

        def sp_last_stores(sp, before):
            sp_store_modes(sp, 0, PAIRS - 2, before)
            sp_store_rows(sp, 1, PAIRS - 1, before)
            sp_store_modes(sp, 1, PAIRS - 1, before)

        def sp_embed(sp):
            def body(i):
                for u in range(2):
                    n = 2 * i + u
                    if not isinstance(i, int):
                        sp.wait_ge(z_done, NCH * (n - 1))
                        sp.wait_ge(zeroed, 4)
                    sp.dma_start(xg[u][4:16, :], x_pairs[bass.ds(n, 1), :, :].rearrange("a p n -> (a p) n"))\
                        .then_inc(xg_in[u], 16)
                    sp_stores(sp, u, n, 0)
            over_pairs(sp, body)
            sp_last_stores(sp, 0)

        def sp_layer(sp, l, last):
            for u in range(2):
                sp.wait_ge(m_stored[u], 16 * 8 * (l + 1))
                sp.wait_ge(zeroed, 4)
            sp.wait_ge(zeroed_v, l + 1)
            sp.wait_ge(zeroed, 4)
            def body(i):
                for u in range(2):
                    n = 2 * i + u
                    sp.wait_ge(z_done, NCH * ((l + 1) * PAIRS + n - 1))
                    sp.wait_ge(zeroed, 4)
                    pair = h_dram[bass.ds(n, 1), :, :, :, :]
                    sp.dma_start(rows_in[u][32:96, :, :], pair.rearrange("a g s c n -> (s c) (a g) n"))\
                        .then_inc(rows_loaded[u], 16)
                    sp.dma_start(rows_in[u][0:32, :, COLS:PIX],
                                 pair[:, :, 1, :, 0:PIX - COLS].rearrange("a g c n -> c (a g) n"))\
                        .then_inc(rows_loaded[u], 16)
                    sp.dma_start(rows_in[u][96:128, :, 0:PIX - COLS],
                                 pair[:, :, 0, :, COLS:PIX].rearrange("a g c n -> c (a g) n"))\
                        .then_inc(rows_loaded[u], 16)
                    for a in range(2):
                        sp.dma_start(mode_tile[u][:, :, a, :],
                                     m_dram[bass.ds(n, 1), a, :, :].rearrange("x (t p) c -> p (x t) c", p=128))\
                            .then_inc(modes_loaded[u], 16)
                    if not last:
                        sp_stores(sp, u, n, PAIRS * (l + 1))
                    elif not (isinstance(n, int) and n < 2):
                        sp_store_tokens(sp, u, n - 2)
            over_pairs(sp, body)
            if last:
                for u in range(2):
                    sp_store_tokens(sp, u, PAIRS - 2 + u)
            else:
                sp_last_stores(sp, PAIRS * (l + 1))

        def sp_mix(sp, l):
            def store_mixed(kx):
                sp.wait_ge(mixed_act, 32 * l + 2 * (kx + 1))
                sp.wait_ge(zeroed, 4)
                sp.wait_ge(mixed_dve, 32 * l + 2 * (kx + 1))
                sp.wait_ge(zeroed, 4)
                px, a = kx // 8, kx % 8
                rows = m_dram[:, :, 256 * px:256 * px + 256, :].rearrange("n g (y a b) c -> (n g) y a (b c)", y=2, a=8)
                sp.dma_start(rows[:, :, a, :], mixed[kx % 2][:].rearrange("p (y n) -> p y n", y=2))\
                    .then_inc(m_stored[kx % 2], 16)
            def load_weights(kx):
                v = kx % 2
                if kx >= 2:
                    sp.wait_ge(mixw_ready, 64 * l + 4 * (kx - 1))
                    sp.wait_ge(zeroed, 4)
                for s in range(2):
                    sp.dma_start(uv[v][64 * s:64 * s + 64, :, :, :].rearrange("p a y o -> p (a y o)"),
                                 spec_uv[bass.ds(l, 1), kx, :, :].rearrange("l p n -> (l p) n"))\
                        .then_inc(uv_in[v], 16)
                sp.dma_start(twid[v][:], tw_dram[kx, :, :]).then_inc(uv_in[v], 16)
            def load_modes(q, part):
                s, ri = part // 2, part % 2
                p = 64 * s + 32 * ri
                sp.dma_start(modes_q[q % 2][p:p + 32, :, :], g_dram[s, :, ri, q, :, :]).then_inc(quarter_in[q % 2], 16)
            load_weights(0)
            for u in range(2):
                sp.wait_ge(g_stored[u], 16 * NP * (l + 1))
                sp.wait_ge(zeroed, 4)
                sp.wait_ge(h_stored[u], 16 * NP * (l + 1))
                sp.wait_ge(zeroed, 4)
            for part in range(4):
                load_modes(0, part)
            for kx in range(MX):
                q, part = kx // 4, kx % 4
                if kx >= 1:
                    load_weights(kx)
                if kx >= 2:
                    store_mixed(kx - 2)
                if q < 3:
                    if part == 0 and q >= 1:
                        sp.wait_ge(mix_done, 64 * l + 16 * q)
                        sp.wait_ge(zeroed, 4)
                    load_modes(q + 1, part)
            store_mixed(MX - 2)
            store_mixed(MX - 1)

        block = ctx.enter_context(nc.Block())

        @block.sync
        def _(sp):
            sp_constants(sp)
            sp_embed(sp)
            def layer(l, last):
                sp.wait_ge(z_done, NCH * PAIRS * (l + 1))
                sp.wait_ge(zeroed, 4)
                sp.wait_ge(h_new, NCH * PAIRS * (l + 1))
                sp.wait_ge(zeroed, 4)
                sp_conv_weights(sp, l)
                sp_mix(sp, l)
                sp_layer(sp, l, last)
            with sp.Fori(0, LAYERS - 1) as l:
                layer(l, False)
            layer(LAYERS - 1, True)
            for u in range(2):
                sp.wait_ge(tok_stored[u], 32 * NP)
                sp.wait_ge(h_stored[u], 16 * NP * LAYERS)
                sp.wait_ge(g_stored[u], 16 * NP * LAYERS)
                sp.wait_ge(m_stored[u], 16 * 8 * LAYERS)

        @block.gpsimd
        def _(pool):
            nc.gpsimd.memset(embed_bd[:], 0.0).then_inc(zeroed, 1)
            nc.gpsimd.memset(q1_bd[:], 0.0).then_inc(zeroed, 1)
            nc.gpsimd.memset(q2_bd[:], 0.0).then_inc(zeroed, 1)
            nc.gpsimd.memset(conv_bd[:], 0.0).then_inc(zeroed, 1)

        def before_layers(kind, l):
            return (0, 0) if kind == "embed" else (PAIRS * (l + 1), PAIRS * l)

        def pe_inverse(pe, u, i, l, k):
            n = 2 * i + u + PAIRS * l
            if k == 0:
                pe.wait_ge(modes_loaded[u], 32 * (i + NP * l + 1))
            if k == 1 or not (isinstance(i, int) and 2 * i + u == 0):
                pe.wait_ge(a_summed, 4 * n + 2 * k)
            for px in range(2):
                last = nc.tensor.matmul(abank[px][:], mode_tile[u][:, 2 * px + k, :, :].rearrange("p a c -> p (a c)"),
                                        inv[:, 2 * px + k, :], start=True, stop=True)
            last.then_inc(a_done, 1)

        def pe_z(pe, u, i, kind, l, o):
            n = 2 * i + u
            before, layers = before_layers(kind, l)
            c, bank = ORDER[o], zbank[o % 2]
            cols = slice(CH * c, CH * c + CH)
            if kind == "embed":
                if not (isinstance(n, int) and NCH * n + o < 2):
                    pe.wait_ge(h_new, NCH * n + o - 1)
                if o == 0:
                    pe.wait_ge(xg_in[u], 16 * (i + 1))
                nc.tensor.matmul(bank[:], embed_bd[:], xg[u][:, cols], start=True, stop=True).then_inc(z_done, 1)
                return
            k = NCH * (n + layers) + o
            if not (isinstance(n, int) and NCH * n + o < 2):
                pe.wait_ge(z_copied, k - 1)
            if o == 0:
                pe.wait_ge(rows_loaded[u], 48 * (i + NP * l + 1))
            out = bank[:].rearrange("p (a j w) -> p a j w", a=2, w=COLS // 2)
            src = rows_in[u][:, :, cols].rearrange("p a (j w v) -> p a j w v", w=COLS // 2, v=2)
            end = COLS // 2
            nc.tensor.matmul(out, conv_bd[:, 1, :], src[:, :, :, :, 0], start=True, stop=False)
            nc.tensor.matmul(out, conv_bd[:, 2, :], src[:, :, :, :, 1], start=False, stop=False)
            nc.tensor.matmul(out[:, :, :, 1:end], conv_bd[:, 0, :], src[:, :, :, 0:end - 1, 1], start=False, stop=False)
            last = nc.tensor.matmul(out[:, :, :, 0:end - 1], conv_bd[:, 3, :], src[:, :, :, 1:end, 0],
                                    start=False, stop=True)
            last.then_inc(z_done, 1)

        def pe_flip(pe, n, before, q):
            g = n + before
            pe.wait_ge(cols_folded, 2 * g + q + 1)
            if not (isinstance(g, int) and g == 0 and q == 0):
                pe.wait_ge(turned_copied, 2 * g + q)
            for px in range(2):
                for py in range(2):
                    for b in range(2):
                        m = 128 * (2 * py + b)
                        last = nc.tensor.transpose(tbank[px][:, m:m + 128], folded[q][:, px, py, 128 * b:128 * b + 128],
                                                   eye[:])
            last.then_inc(flip_done, 1)

        def pe_forward(pe, u, n, before, q):
            g = n + before
            pe.wait_ge(turned_copied, 2 * g + q + 1)
            if q == 0 and not (isinstance(g, int) and g < 2):
                pe.wait_ge(g_ready, g - 1)
            for k in range(4):
                for b in range(2):
                    last = nc.tensor.matmul(gbank[u][:, 128 * k:128 * k + 128], turned[q][:, k // 2, k % 2, b, :],
                                            fwd[:, 2 * q + b, k, :], start=(q == 0 and k == 0 and b == 0),
                                            stop=(q == 1 and k == 3 and b == 1))
            last.then_inc(fwd_done, 1)

        def pe_pair(pe, u, i, kind, l):
            n = 2 * i + u
            before, _ = before_layers(kind, l)
            first = isinstance(n, int) and n == 0
            layer, fold = kind != "embed", kind != "last"
            late = fold and not first
            if layer:
                pe_inverse(pe, u, i, l, 0)
            if late:
                pe_forward(pe, 1 - u, n - 1, before, 0)
            pe_z(pe, u, i, kind, l, 0)
            if late:
                pe_flip(pe, n - 1, before, 1)
            if layer:
                pe_inverse(pe, u, i, l, 1)
            if not fold:
                pe_head(pe, u, n, 0)
                for o in range(1, NCH):
                    pe_z(pe, u, i, kind, l, o)
                    pe_head(pe, u, n, o)
                return
            pe_z(pe, u, i, kind, l, 1)
            if late:
                pe_forward(pe, 1 - u, n - 1, before, 1)
            pe_z(pe, u, i, kind, l, 2)
            pe_z(pe, u, i, kind, l, 3)
            pe_flip(pe, n, before, 0)

        def head_steps(n, o):
            steps = []
            for lag in (2, 3):
                m, c = (n, o - lag) if o >= lag else (n - 1, o - lag + NCH)
                k = NCH * m + c
                steps.append(None if isinstance(k, int) and not 0 <= k < NCH * PAIRS else (m, c, k))
            return steps

        def pe_head(pe, u, n, o):
            first, second = head_steps(n, o)
            if first is not None:
                m, o1, k = first
                pe.wait_ge(h_new, NCH * PAIRS * LAYERS + k + 1)
                if not (isinstance(k, int) and k < 2):
                    pe.wait_ge(q1_leaky, k - 1)
                c = ORDER[o1]
                rows = rows_out[u if o >= 2 else 1 - u]
                nc.tensor.matmul(tbank[o1 % 2][:], q1_bd[:], rows[:, CH * c:CH * c + CH], start=True, stop=True)\
                    .then_inc(q1_done, 1)
            if second is not None:
                m, o2, k = second
                pe.wait_ge(q1_leaky, k + 1)
                if not (isinstance(k, int) and k < 2):
                    pe.wait_ge(tok_ready, k - 1)
                nc.tensor.matmul(gbank[o2 % 2][0:4, :], q2_bd[:], leaky[o2 % 2], start=True, stop=True)\
                    .then_inc(q2_done, 1)

        def pe_last(pe, kind, l):
            before, _ = before_layers(kind, l)
            if kind != "last":
                pe_forward(pe, 1, PAIRS - 1, before, 0)
                pe_flip(pe, PAIRS - 1, before, 1)
                pe_forward(pe, 1, PAIRS - 1, before, 1)
            else:
                for o in range(3):
                    pe_head(pe, 0, PAIRS, o)

        @block.tensor
        def _(pe):
            pe.wait_ge(consts, 16 * NCONSTS)
            def run(kind, l):
                def body(i):
                    for u in range(2):
                        pe_pair(pe, u, i, kind, l)
                over_pairs(pe, body)
                pe_last(pe, kind, l)
            def mix(l):
                pe.wait_ge(h_new, NCH * PAIRS * (l + 1))
                pe.wait_ge(turned_copied, 2 * PAIRS * (l + 1))
                for kx in range(MX):
                    q = kx // 4
                    if kx % 4 == 0:
                        pe.wait_ge(quarter_in[q % 2], 16 * 4 * (2 * l + q // 2 + 1))
                    pe.wait_ge(mixw_ready, 64 * l + 4 * (kx + 1))
                    for y in range(4):
                        if kx >= 1:
                            pe.wait_ge(mixed_act if y % 2 == 0 else mixed_dve, 32 * l + 2 * kx - 1 + y // 2)
                        for yy in range(4):
                            ky = 4 * y + yy
                            m = 16 * (kx % 4) + ky
                            last = nc.tensor.matmul(mbank[y][:, 128 * yy:128 * yy + 128], modes_q[q % 2][:, :, m],
                                                    mix_w[kx % 2][:, ky, :, :, :].rearrange("p r s o -> p (r s o)"),
                                                    start=True, stop=True)
                        last.then_inc(mix_done, 1)
            run("embed", 0)
            def mix_out(l):
                pe.wait_ge(mixed_act, 32 * (l + 1))
                pe.wait_ge(mixed_dve, 32 * (l + 1))
            with pe.Fori(0, LAYERS - 1) as l:
                mix(l)
                mix_out(l)
                pe.wait_ge(conv_in, 16 * NCONV * (l + 1))
                run("mid", l)
            mix(LAYERS - 1)
            mix_out(LAYERS - 1)
            pe.wait_ge(conv_in, 16 * NCONV * LAYERS)
            run("last", LAYERS - 1)

        @block.scalar
        def _(act):
            def inverse_copy(n, layers, k):
                g = n + layers
                act.wait_ge(a_done, 2 * g + k + 1)
                if not (isinstance(n, int) and n == 0):
                    act.wait_ge(a_summed, 4 * g + 2 * k - 2)
                bias = {"bias": conv_bias[:]} if k == 0 else {}
                nc.scalar.activation(inv_copy[k][:], abank[0][:], ACT.Identity, **bias).then_inc(a_copied, 1)

            def embedded(u, n, o, i):
                act.wait_ge(z_done, NCH * n + o + 1)
                if o == 0 and not (isinstance(n, int) and n < 2):
                    act.wait_ge(h_stored[u], 16 * i)
                    act.wait_ge(cols_folded, 2 * (n - 1))
                c = ORDER[o]
                nc.scalar.activation(rows_out[u][:, CH * c:CH * c + CH], zbank[o % 2][:], ACT.Identity,
                                     bias=embed_bias[:]).then_inc(h_new, 1)

            def z_copy(n, kind, l, o):
                before, layers = before_layers(kind, l)
                act.wait_ge(z_done, NCH * (n + before) + o + 1)
                if not (isinstance(n, int) and NCH * n + o < 2):
                    act.wait_ge(h_new, NCH * (n + before) + o - 1)
                z = z_sum[o % 2][:].rearrange("p (m v) -> p m v", v=2)
                for a in range(2):
                    for dw in range(2):
                        last = nc.scalar.activation(z[64 * a:64 * a + 64, :, dw],
                                                    zbank[o % 2][64 * dw:64 * dw + 64, 256 * a:256 * a + 256],
                                                    ACT.Identity)
                last.then_inc(z_copied, 1)

            def turned_copy(g, q):
                act.wait_ge(flip_done, 2 * g + q + 1)
                if not (isinstance(g, int) and g == 0):
                    act.wait_ge(fwd_done, 2 * g + q - 1)
                for px in range(2):
                    last = nc.scalar.activation(turned[q][:, px, :, :, :].rearrange("p y b n -> p (y b n)"),
                                                tbank[px][:], ACT.Identity)
                last.then_inc(turned_copied, 1)

            def scaled(n, o):
                step = head_steps(n, o)[0]
                if step is None:
                    return
                _, o1, k = step
                act.wait_ge(q1_done, k + 1)
                if isinstance(k, int) and k < 2:
                    act.wait_ge(g_stored[k], 16 * NP * LAYERS)
                else:
                    act.wait_ge(q1_leaky, k - 1)
                nc.scalar.activation(modes_out[o1 % 2][:], tbank[o1 % 2][:], ACT.Identity, bias=q1_bias01[:],
                                     scale=0.01).then_inc(q1_scaled, 1)

            def pair(u, n, kind, l, i):
                before, layers = before_layers(kind, l)
                fold = kind != "last"
                late = fold and not (isinstance(n, int) and n == 0)
                if kind == "embed":
                    embedded(u, n, 0, i)
                    if late:
                        turned_copy(n - 1, 1)
                    for o in range(1, NCH):
                        embedded(u, n, o, i)
                    turned_copy(n, 0)
                    return
                inverse_copy(n, layers, 0)
                z_copy(n, kind, l, 0)
                if late:
                    turned_copy(n - 1 + before, 1)
                inverse_copy(n, layers, 1)
                if fold:
                    z_copy(n, kind, l, 1)
                    z_copy(n, kind, l, 2)
                    z_copy(n, kind, l, 3)
                    turned_copy(n + before, 0)
                    return
                scaled(n, 0)
                for o in range(1, NCH):
                    z_copy(n, kind, l, o)
                    scaled(n, o)

            def run(kind, l):
                def body(i):
                    for u in range(2):
                        pair(u, 2 * i + u, kind, l, i)
                over_pairs(act, body)
                if kind != "last":
                    turned_copy(PAIRS - 1 + before_layers(kind, l)[0], 1)
                else:
                    scaled(PAIRS, 0)
                    scaled(PAIRS, 1)

            def mix(l):
                for kx in range(MX + 1):
                    if kx < MX:
                        v = kx % 2
                        act.wait_ge(uv_in[v], 48 * (8 * l + kx // 2 + 1))
                        for k, (so, r) in enumerate([(0, 0), (0, 1), (1, 0), (1, 1)]):
                            g = 4 * kx + k
                            if g >= 2:
                                act.wait_ge(mixw_ready, 64 * l + g - 1)
                            nc.scalar.activation(partial[k % 2][:], uv[v][:, r, :, :], ACT.Identity,
                                                 scale=twid[v][:, 4 * so + 2 * r:4 * so + 2 * r + 1])\
                                .then_inc(part_ready, 1)
                    if kx >= 1:
                        m = kx - 1
                        for y in (0, 2):
                            act.wait_ge(mix_done, 64 * l + 4 * m + y + 1)
                            if m >= 2:
                                act.wait_ge(m_stored[m % 2], 16 * (8 * l + m // 2))
                            nc.scalar.activation(mixed[m % 2][:, CH * y:CH * y + CH], mbank[y][:], ACT.Identity)\
                                .then_inc(mixed_act, 1)

            def layer(l, kind):
                mix(l)
                act.wait_ge(conv_in, 16 * NCONV * (l + 1))
                run(kind, l)
            act.wait_ge(consts, 16 * NCONSTS)
            run("embed", 0)
            with act.Fori(0, LAYERS - 1) as l:
                layer(l, "mid")
            act.wait_ge(q_ready, 1)
            layer(LAYERS - 1, "last")

        @block.vector
        def _(dve):
            def inverse_sums(u, n, layers, k):
                dve.wait_ge(a_copied, 2 * (n + layers) + k + 1)
                if k == 0 and not (isinstance(n, int) and n < 2):
                    dve.wait_ge(z_full, NCH * (n + layers - 1))
                for part, op in ((0, ALU.add), (1, ALU.subtract)):
                    nc.vector.tensor_tensor(inverse[u][:, 2 * k + part, :], inv_copy[k][:], abank[1][:], op)\
                        .then_inc(a_summed, 1)

            def new_rows(u, n, kind, l, o):
                before, layers = before_layers(kind, l)
                g = n + before
                if o == 0 and not (isinstance(g, int) and g < 2):
                    dve.wait_ge(h_stored[u], 16 * stores_before(u, l, kind))
                    if kind != "last":
                        dve.wait_ge(cols_folded, 2 * (g - 1))
                    elif not isinstance(n, int):
                        dve.wait_ge(q1_done, NCH * (n - 1))
                c = ORDER[o]
                out = rows_out[u][:, CH * c:CH * c + CH]
                k = NCH * (n + layers) + o
                low = c // 2
                rows = slice(256 * (c % 2), 256 * (c % 2) + 256)
                jw = lambda ap: ap.rearrange("p (j v w) -> p j v w", v=2, w=COLS // 2)
                quarter = lambda m: inverse[u][:, m, rows].rearrange("p (j w) -> p j w", w=COLS // 2)
                base, delta = quarter(low), quarter(2 + low)
                total = jw(z_sum[o % 2][:])
                dve.wait_ge(z_copied, k + 1)
                if o == 0:
                    dve.wait_ge(a_summed, 4 * (n + layers) + 4)
                nc.vector.tensor_tensor(total, total, base.unsqueeze(2).broadcast_to([128, 8, 2, COLS // 2]), ALU.add)\
                    .then_inc(z_based, 1)
                dve.wait_ge(z_based, k + 1)
                nc.vector.tensor_tensor(total[:, :, 0, :], total[:, :, 0, :], delta, ALU.add)
                nc.vector.tensor_tensor(total[:, :, 1, :], total[:, :, 1, :], delta, ALU.subtract).then_inc(z_full, 1)
                dve.wait_ge(z_full, k + 1)
                nc.vector.scalar_tensor_tensor(out=out, in0=z_sum[o % 2][:], scalar=0.01, in1=z_sum[o % 2][:],
                                               op0=ALU.mult, op1=ALU.max).then_inc(h_new, 1)

            def fold(u, g, q):
                dve.wait_ge(h_new, NCH * g + 2 * q + 2)
                if not (isinstance(g, int) and g == 0 and q == 0):
                    dve.wait_ge(cols_folded, 2 * g + q)
                up, low = (rows_out[u][:, CH * c:CH * c + CH] for c in (ORDER[2 * q], ORDER[2 * q + 1]))
                nc.vector.tensor_tensor(by_row[:, 0, :], up, low, ALU.add)
                nc.vector.tensor_tensor(by_row[:, 1, :], up, low, ALU.subtract).then_inc(rows_folded, 1)
                dve.wait_ge(rows_folded, 2 * g + q + 1)
                if not (isinstance(g, int) and g == 0):
                    dve.wait_ge(flip_done, 2 * g + q - 1)
                v = by_row[:].rearrange("p x (j v w) -> p x j v w", v=2, w=COLS // 2)
                blocks = folded[q][:].rearrange("p x y (j w) -> p x y j w", w=COLS // 2)
                nc.vector.tensor_tensor(blocks[:, :, 0, :, :], v[:, :, :, 0, :], v[:, :, :, 1, :], ALU.add)
                nc.vector.tensor_tensor(blocks[:, :, 1, :, :], v[:, :, :, 0, :], v[:, :, :, 1, :], ALU.subtract)\
                    .then_inc(cols_folded, 1)

            def modes_copy(u, g, stores):
                dve.wait_ge(fwd_done, 2 * g + 2)
                if stores is not None:
                    dve.wait_ge(g_stored[u], 16 * stores)
                for k in range(4):
                    last = nc.vector.tensor_copy(
                        modes_out[u][:].rearrange("p (r x a y b) -> p r x a y b", r=2, x=2, a=8, y=2)[:, :, k // 2, :, k % 2, :],
                        gbank[u][:, 128 * k:128 * k + 128].rearrange("p (r a b) -> p r a b", r=2, a=8))
                last.then_inc(g_ready, 1)

            def late_part(u, n, kind, l, i):
                before, _ = before_layers(kind, l)
                g = n + before
                stores = None if isinstance(g, int) and g < 2 else i if kind == "embed" else i + NP * (l + 1)
                return g, stores

            def pair(u, n, kind, l, i):
                before, layers = before_layers(kind, l)
                late = kind != "last" and not (isinstance(n, int) and n == 0)
                if late:
                    g, stores = late_part(1 - u, n - 1, kind, l, i if u else i - 1)
                if kind != "embed":
                    inverse_sums(u, n, layers, 0)
                    inverse_sums(u, n, layers, 1)
                if kind == "embed":
                    fold(u, n, 0)
                    if late:
                        modes_copy(1 - u, g, stores)
                    fold(u, n, 1)
                    return
                new_rows(u, n, kind, l, 0)
                if kind == "last":
                    head(u, n, 0, i)
                    for o in range(1, NCH):
                        new_rows(u, n, kind, l, o)
                        head(u, n, o, i)
                    return
                new_rows(u, n, kind, l, 1)
                fold(u, n + before, 0)
                if late:
                    modes_copy(1 - u, g, stores)
                new_rows(u, n, kind, l, 2)
                new_rows(u, n, kind, l, 3)
                fold(u, n + before, 1)

            def head(u, n, o, i):
                first, second = head_steps(n, o)
                if first is not None:
                    _, o1, k = first
                    dve.wait_ge(q1_scaled, k + 1)
                    if not (isinstance(k, int) and k < 2):
                        dve.wait_ge(q2_done, k - 1)
                    nc.vector.scalar_tensor_tensor(out=leaky[o1 % 2], in0=tbank[o1 % 2][:], scalar=q1_bias[:],
                                                   in1=modes_out[o1 % 2][:], op0=ALU.add, op1=ALU.max)\
                        .then_inc(q1_leaky, 1)
                if second is not None:
                    _, o2, k = second
                    v = u if o >= 3 else 1 - u
                    dve.wait_ge(q2_done, k + 1)
                    if o2 == 0 and not isinstance(n, int):
                        dve.wait_ge(tok_stored[v], 32 * i)
                    c = ORDER[o2]
                    nc.vector.tensor_scalar(tok_out[v][:, CH * c:CH * c + CH], gbank[o2 % 2][0:4, :], q2_bias[:], None,
                                            ALU.add).then_inc(tok_ready, 1)

            cur = [0]
            def stores_before(u, l, kind):
                return cur[0] if kind == "embed" else (NP * LAYERS if kind == "last" else cur[0] + NP * (l + 1))

            def run(kind, l):
                def body(i):
                    cur[0] = i
                    for u in range(2):
                        pair(u, 2 * i + u, kind, l, i)
                over_pairs(dve, body)
                if kind == "last":
                    for o in range(3):
                        head(0, PAIRS, o, NP)
                else:
                    g, stores = late_part(1, PAIRS - 1, kind, l, NP - 1)
                    modes_copy(1, g, stores)

            def mix(l):
                for kx in range(MX + 1):
                    if kx < MX:
                        v = kx % 2
                        if kx >= 2:
                            dve.wait_ge(mix_done, 64 * l + 4 * (kx - 1))
                        dve.wait_ge(uv_in[v], 48 * (8 * l + kx // 2 + 1))
                        for k, (so, r) in enumerate([(0, 0), (0, 1), (1, 0), (1, 1)]):
                            dve.wait_ge(part_ready, 64 * l + 4 * kx + k + 1)
                            nc.vector.scalar_tensor_tensor(out=mix_w[v][:, :, r, so, :], in0=uv[v][:, 1 - r, :, :],
                                                           scalar=twid[v][:, 4 * so + 2 * r + 1:4 * so + 2 * r + 2],
                                                           in1=partial[k % 2][:], op0=ALU.mult, op1=ALU.add)\
                                .then_inc(mixw_ready, 1)
                    if kx >= 1:
                        m = kx - 1
                        for y in (1, 3):
                            dve.wait_ge(mix_done, 64 * l + 4 * m + y + 1)
                            if m >= 2:
                                dve.wait_ge(m_stored[m % 2], 16 * (8 * l + m // 2))
                            nc.vector.tensor_copy(mixed[m % 2][:, CH * y:CH * y + CH], mbank[y][:]).then_inc(mixed_dve, 1)
                dve.wait_ge(mix_done, 64 * (l + 1))
                for u in range(2):
                    nc.vector.memset(rows_in[u][0:32, :, 0:COLS], 0.0)
                    last = nc.vector.memset(rows_in[u][96:128, :, PIX - COLS:PIX], 0.0)
                last.then_inc(zeroed_v, 1)

            dve.wait_ge(consts, 16 * NCONSTS)
            nc.vector.tensor_scalar(q1_bias01[:], q1_bias[:], 0.01, None, ALU.mult).then_inc(q_ready, 1)
            run("embed", 0)
            with dve.Fori(0, LAYERS - 1) as l:
                mix(l)
                run("mid", l)
            mix(LAYERS - 1)
            run("last", LAYERS - 1)


TOKENS, DIM, SEQ = 8192, 64, 64
U = 2
R = range(U)
T = 4
BLK = 128 * T
ITERS = TOKENS // (BLK * U)
BATCHES = BLK // SEQ
HID = 170
NTILE = -(-8 * HID // 128)


def block_constants():
    c = {}
    c["eye"] = np.eye(128)
    c["mhalf"] = np.full((128, 4), -0.5)
    hd = 16
    inv_freq = 1.0 / 10000.0 ** (np.arange(0, hd, 2, dtype=np.float32) / hd)
    freqs = np.outer(np.arange(SEQ, dtype=np.float32), inv_freq)
    emb = np.concatenate([freqs, freqs], -1).astype(np.float32)
    sign = np.where(np.arange(hd) < hd // 2, -1.0, 1.0)
    c["cos"] = np.tile(np.cos(emb).T, (4, 1))
    c["sin"] = np.tile(np.sin(emb).T * sign[:, None], (4, 1))
    c["headmask"] = np.kron(np.eye(4), np.ones((16, 1)))
    n = np.arange(128) % SEQ
    c["causal"] = np.where(np.arange(SEQ)[None, :] <= n[:, None], 0.0, -1e30)
    e = np.arange(8)
    c["before"] = np.tile((e[None, :] < e[:, None]).astype(np.float32).reshape(1, 64), (128, 1))
    e = np.arange(4)
    c["before4"] = np.tile((e[None, :] < e[:, None]).astype(np.float32).reshape(1, 16), (128, 1))
    own = np.zeros((8, NTILE * 128))
    for e in range(8):
        own[e, e * HID:(e + 1) * HID] = 1.0
    c["expand"] = own
    c["diag32"] = np.tile(np.kron(np.eye(8), np.ones((4, 32))), (4, 1))
    c["ones"] = np.ones((1, BLK))
    return c


def block_weights(i):
    w = {}
    col = lambda v: np.asarray(v).reshape(-1, 1)
    row = lambda v: np.broadcast_to(np.asarray(v).reshape(1, -1), (128, np.asarray(v).size))
    aug = lambda m, b: np.concatenate([np.asarray(m), np.asarray(b).reshape(1, -1)], 0)
    a = "L0_attn_"
    for k, b in (("q", "q"), ("k", "k"), ("v", "v"), ("l", "l")):
        w["l0a_" + k] = aug(i[a + "W" + k], i[a + "b" + b])
    w["l0a_gamma"], w["l0a_beta"] = col(i[a + "gamma"]), col(i[a + "beta"])
    a = "L0_ffn_"
    w["l0f_ln1"], w["l0f_ln2"] = col(i[a + "ln1_w"]), col(i[a + "ln2_w"])
    wq, wk, wv = (np.asarray(i[a + k]).T for k in ("wq", "wk", "wv"))
    rep = np.repeat(np.arange(2), 2)
    rot = np.concatenate([np.arange(8, 16), np.arange(8)])
    q4 = wq.reshape(64, 4, 16)
    k4 = wk.reshape(64, 2, 16)[:, rep]
    w["l0f_q"], w["l0f_qp"] = q4.reshape(64, 64), q4[:, :, rot].reshape(64, 64)
    w["l0f_k"], w["l0f_kp"] = k4.reshape(64, 64), k4[:, :, rot].reshape(64, 64)
    v4 = wv.reshape(64, 2, 16)[:, rep]
    vm = np.zeros((64, 4, 4, 16), np.float32)
    for h in range(4):
        vm[:, h, h] = v4[:, h]
    w["l0f_v"] = vm.reshape(64, 256)
    w["l0f_wo"] = np.asarray(i[a + "wo"]).T
    w["l0f_router"] = np.asarray(i[a + "router_w"]).T
    for k in ("w1", "w3"):
        m = np.zeros((64, NTILE * 128), np.float32)
        m[:, :8 * HID] = np.asarray(i[a + k]).transpose(2, 0, 1).reshape(64, 8 * HID)
        w["l0f_" + k] = m
    m = np.zeros((NTILE * 128, 64), np.float32)
    m[:8 * HID] = np.asarray(i[a + "w2"]).transpose(0, 2, 1).reshape(8 * HID, 64)
    w["l0f_w2"] = m.reshape(NTILE, 128, 64).transpose(1, 0, 2).reshape(128, NTILE * 64)
    a = "L1_attn_"
    w["l1a_g"], w["l1a_b"] = col(i[a + "ln1_g"]), col(i[a + "ln1_b"])
    qw, qb = np.asarray(i[a + "qkv_w"]), np.asarray(i[a + "qkv_b"])
    for n, k in enumerate("qkv"):
        w["l1a_" + k] = aug(qw[:, 64 * n:64 * n + 64], qb[64 * n:64 * n + 64])
    w["l1a_l"] = aug(i[a + "proj_w"], i[a + "proj_b"])
    n = np.arange(128) % SEQ
    w["l1a_rel"] = np.asarray(i[a + "bias_table"])[np.arange(SEQ)[None, :] - n[:, None] + SEQ - 1]
    w["l1a_scale"] = np.broadcast_to(np.asarray(i[a + "scale"]).reshape(1, 1), (128, 1))
    w["l1a_g2"], w["l1a_b2"] = row(i[a + "ln2_g"]), row(i[a + "ln2_b"])
    a = "L1_ffn_"
    halves = lambda m: np.asarray(m).reshape(2, 128, -1).transpose(1, 0, 2).reshape(128, -1)
    w["l1f_w1"], w["l1f_b1"] = i[a + "W1"], halves(i[a + "b1"])
    w["l1f_wg"], w["l1f_bg"] = halves(i[a + "Wg"]), row(i[a + "bg"])
    w["l1f_wd"] = halves(np.asarray(i[a + "Wd"]).transpose(1, 0, 2).reshape(256, 512))
    w["l1f_bd"] = row(np.asarray(i[a + "bd"]).reshape(512))
    a = "L2_attn_"
    w["l2a_g"], w["l2a_b"] = col(i[a + "ln1_g"]), col(i[a + "ln1_b"])
    w["l2a_wx"], w["l2a_bx"] = i[a + "Wx"], halves(i[a + "bx"])
    for k in "qk":
        m = np.zeros((8, 32, 8, 4), np.float32)
        for h in range(8):
            m[h, :, h] = i[a + "W" + k]
        w["l2a_w" + k] = halves(m.reshape(256, 32))
    m = np.zeros((4, 32, 4, 32), np.float32)
    for h in range(4):
        m[h, :, h] = i[a + "Wv"]
    w["l2a_wv"] = m.reshape(128, 128)
    w["l2a_wo"], w["l2a_bo"] = halves(i[a + "Wo"]), row(i[a + "bo"])
    w["l2a_g2"], w["l2a_b2"] = col(i[a + "ln2_g"]), col(i[a + "ln2_b"])
    w["l2a_w1"], w["l2a_fb1"] = i[a + "W1"], halves(i[a + "b1"])
    w["l2a_w2"], w["l2a_fb2"] = halves(i[a + "W2"]), row(i[a + "b2"])
    a = "L2_ffn_"
    w["l2f_s1"], w["l2f_sb1"] = i[a + "sW1"], col(i[a + "sb1"])
    w["l2f_s2"], w["l2f_sb2"] = i[a + "sW2"], col(i[a + "sb2"])
    w["l2f_s3"], w["l2f_sb3"] = i[a + "sW3"], row(i[a + "sb3"])
    w["l2f_e1"] = np.asarray(i[a + "eW1"]).transpose(1, 0, 2).reshape(64, 512)
    w["l2f_eb1"] = np.asarray(i[a + "eb1"]).T
    w["l2f_e2"] = np.asarray(i[a + "eW2"]).transpose(1, 0, 2).reshape(128, 256)
    w["l2f_eb2"] = np.asarray(i[a + "eb2"]).reshape(2, 128).T
    m = np.zeros((2, 2, 64, 2, 64), np.float32)
    for e in range(4):
        m[e // 2, e % 2, :, e % 2] = np.asarray(i[a + "eW3"])[e]
    w["l2f_e3"] = m.reshape(2, 128, 128).transpose(1, 0, 2).reshape(128, 256)
    w["l2f_eb3"] = np.asarray(i[a + "eb3"]).reshape(1, 256)
    w["l2f_g"], w["l2f_gb"] = i[a + "gW"], row(i[a + "gb"])
    a = "L3_attn_"
    for k in "qkv":
        w["l3a_" + k] = np.asarray(i[a + "W" + k]).reshape(64, 64, 8).transpose(0, 2, 1).reshape(64, 512)
    m = np.asarray(i[a + "Wo"]).reshape(64, 8, 64).transpose(1, 0, 2).reshape(4, 128, 64)
    w["l3a_o"] = m.transpose(1, 0, 2).reshape(128, 256)
    a = "L3_ffn_"
    w["l3f_g"], w["l3f_bg"] = i[a + "Wg"], row(i[a + "bg"])
    w["l3f_w1"] = np.asarray(i[a + "W1"]).transpose(1, 0, 2).reshape(64, 1024)
    w["l3f_b1"] = np.asarray(i[a + "b1"]).T
    w["l3f_w2"] = np.asarray(i[a + "W2"]).transpose(1, 0, 2).reshape(128, 512)
    w["l3f_b2"] = row(np.asarray(i[a + "b2"]).reshape(512))
    return w


def packed(parts):
    total = sum(np.asarray(v).shape[1] for v in parts.values())
    out, at, where = np.zeros((128, total), np.float32), 0, {}
    for name, v in parts.items():
        p, n = np.asarray(v).shape
        out[:p, at:at + n] = v
        where[name] = (p, at, n)
        at += n
    return out, where


STEPS = {('l0a', 'act'): ['x.sq', 'x.xT', 'q', 'exp', 'pT', 'oT'],
 ('l0a', 'dve'): ['x.sum', 'x.centered', 'x.sumsq', 'x.var', 'x.out', 'k', 'v', 'max', 'diff', 'sum', 'recip',
                  'p_lo', 'p_hi', 'hx', 'hl'],
 ('l0a', 'pe'): ['x.flip', 'q', 'k', 'v', 'scores', 'pT', 'attended', 'hl'],
 ('l0a', 'pool'): ['x.rstd'],
 ('l0b', 'act'): ['y'],
 ('l0b', 'dve'): ['normed', 'h'],
 ('l0b', 'pe'): ['y'],
 ('l0f', 'act'): ['x.sq', 'r.sq', 'r.xT', 'km', 'v', 'exp', 'pT0', 'pT2', 'oT', 'f.sq', 'f.xT', 'exp_router',
                  'gatesT', 'silu0', 'silu1', 'silu2', 'silu3', 'silu4', 'silu5', 'silu6', 'silu7', 'silu8',
                  'silu9', 'silu10', 'yT'],
 ('l0f', 'dve'): ['x.sum', 'x.centered', 'x.sumsq', 'x.var', 'x.out', 'r.sumsq', 'r.var', 'r.out', 'qa', 'qb',
                  'q', 'ka', 'kb', 'k', 'masked0', 'masked1', 'max', 'diff', 'sum', 'recip', 'p_lo', 'p_hi',
                  'pT1', 'pT3', 'x2', 'f.sumsq', 'f.var', 'f.out', 'emax', 'ediff', 'esum', 'erecip', 'probs',
                  'greater', 'equal', 'tied', 'ahead', 'rank', 'chosen', 'kept', 'kept_sum', 'kept_eps',
                  'kept_recip', 'gates', 'up0', 'hid0', 'up1', 'hid1', 'up2', 'hid2', 'up3', 'hid3', 'up4',
                  'hid4', 'up5', 'hid5', 'up6', 'hid6', 'up7', 'hid7', 'up8', 'hid8', 'up9', 'hid9', 'up10',
                  'hid10', 'h_x', 'h'],
 ('l0f', 'pe'): ['r.flip', 'q', 'qp', 'k', 'kp', 'v', 'scores', 'pT0', 'pT1', 'pT2', 'pT3', 'attended', 'wo',
                 'f.flip', 'logits', 'gatesT', 'gate0', 'up0', 'share0', 'gate1', 'up1', 'share1', 'down0',
                 'gate2', 'up2', 'share2', 'down1', 'gate3', 'up3', 'share3', 'down2', 'gate4', 'up4',
                 'share4', 'down3', 'gate5', 'up5', 'share5', 'down4', 'gate6', 'up6', 'share6', 'down5',
                 'gate7', 'up7', 'share7', 'down6', 'gate8', 'up8', 'share8', 'down7', 'gate9', 'up9',
                 'share9', 'down8', 'gate10', 'up10', 'share10', 'down9', 'down10', 'y'],
 ('l0f', 'pool'): ['x.rstd', 'r.rstd', 'f.rstd'],
 ('l1a', 'act'): ['x.sq', 'r.sq', 'x.xT', 'q', 'exp', 'pT', 'oT', 'o.sq'],
 ('l1a', 'dve'): ['x.sum', 'x.centered', 'x.sumsq', 'x.var', 'x.out', 'r.sum', 'r.centered', 'r.sumsq',
                  'r.var', 'r.out', 'k', 'v', 'biased', 'max', 'diff', 'sum', 'recip', 'scaled', 'p_lo',
                  'p_hi', 'proj', 'o.sum', 'o.centered', 'o.sumsq', 'o.var', 'o.out', 'o.g', 'h_b', 'h'],
 ('l1a', 'pe'): ['x.flip', 'q', 'k', 'v', 'scores', 'pT', 'attended', 'proj'],
 ('l1a', 'pool'): ['x.rstd', 'r.rstd', 'o.rstd'],
 ('l1f', 'act'): ['x.sq', 'x.xT', 'hid0', 'hid1', 'exp'],
 ('l1f', 'dve'): ['x.sum', 'x.centered', 'x.sumsq', 'x.var', 'x.out', 'biased', 'emax', 'ediff', 'esum',
                  'erecip', 'probs', 'greater', 'equal', 'tied', 'ahead', 'rank', 'chosen', 'gates',
                  'raised0', 'weighed0', 'summed0', 'raised1', 'weighed1', 'summed1', 'raised2', 'weighed2',
                  'summed2', 'raised3', 'weighed3', 'summed3', 'h'],
 ('l1f', 'pe'): ['x.flip', 'hid0', 'hid1', 'logits', 'out0', 'out1', 'out2', 'out3'],
 ('l1f', 'pool'): ['x.rstd'],
 ('l2a', 'act'): ['x.sq', 'r.sq', 'x.xT', 'hid0', 'hid1', 'exp', 'kexp', 'v', 'k4', 'q4T', 'o0', 'f.sq',
                  'f.xT', 'ff0', 'ff1'],
 ('l2a', 'dve'): ['x.sum', 'x.centered', 'x.sumsq', 'x.var', 'x.out', 'r.sum', 'r.centered', 'r.sumsq',
                  'r.var', 'r.out', 'max', 'diff', 'sum', 'recip', 'q4', 'kmax', 'kdiff', 'ksum', 'krecip',
                  'kprob', 'kv', 'o1', 'x_bo', 'fx', 'f.sum', 'f.centered', 'f.sumsq', 'f.var', 'f.out',
                  'fx_b', 'h_fx', 'h'],
 ('l2a', 'pe'): ['x.flip', 'hid0', 'hid1', 'q', 'k', 'v', 'kT', 'kv', 'q4T', 'o0', 'o1', 'wo', 'f.flip',
                 'ff0', 'ff1', 'ff'],
 ('l2a', 'pool'): ['x.rstd', 'zeros', 'r.rstd', 'f.rstd'],
 ('l2f', 'act'): ['x.sq', 'x.xT', 's1', 's2', 'exp', 'e1_0', 'e1_1', 'e1_2', 'e1_3', 'texp'],
 ('l2f', 'dve'): ['x.sum', 'x.centered', 'x.sumsq', 'x.var', 'x.out', 'biased', 'emax', 'ediff', 'esum',
                  'erecip', 'probs', 'e2_0', 'e2_1', 'greater', 'equal', 'tied', 'ahead', 'rank', 'chosen',
                  'tmax', 'tdiff', 'tkept', 'tsum', 'trecip', 'gates', 'h_b', 'h_s', 'weighed0', 'summed0',
                  'weighed1', 'summed1', 'weighed2', 'summed2', 'weighed3', 'summed3', 'h'],
 ('l2f', 'pe'): ['x.flip', 'logits', 's1', 's2', 's3', 'e1_0', 'e1_1', 'e2_0', 'e1_2', 'e2_1', 'e1_3', 'e2_2',
                 'e2_3', 'out0', 'out1'],
 ('l2f', 'pool'): ['x.rstd'],
 ('l3a', 'act'): ['x.sq', 'x.xT', 'v2', 'v0', 'q0', 'p0_0', 'p0_1', 'o0', 'q1', 'p1_0', 'p1_1', 'o1', 'q2',
                  'p2_0', 'p2_1', 'o2', 'q3', 'p3_0', 'p3_1', 'o3'],
 ('l3a', 'dve'): ['x.sum', 'x.centered', 'x.sumsq', 'x.var', 'x.out', 'v1', 'v3', 'k0', 'k1', 'k2', 'k3',
                  'h'],
 ('l3a', 'pe'): ['x.flip', 'v1', 'v2', 'v3', 'v0', 'q0', 'k0', 's0_0', 's0_1', 'o0', 'q1', 'k1', 's1_0',
                 's1_1', 'o1', 'q2', 'k2', 's2_0', 's2_1', 'o2', 'q3', 'k3', 's3_0', 's3_1', 'o3', 'wo'],
 ('l3a', 'pool'): ['x.rstd'],
 ('l3f', 'act'): ['x.sq', 'x.xT', 'hid0', 'hid1', 'hid2', 'hid3', 'hid4', 'hid5', 'hid6', 'hid7'],
 ('l3f', 'dve'): ['x.sum', 'x.centered', 'x.sumsq', 'x.var', 'x.out', 'biased', 'greater', 'equal', 'tied',
                  'ahead', 'rank', 'chosen', 'raised0', 'weighed0', 'summed0', 'raised1', 'weighed1',
                  'summed1', 'raised2', 'weighed2', 'summed2', 'raised3', 'weighed3', 'summed3', 'h'],
 ('l3f', 'pe'): ['x.flip', 'logits', 'hid0', 'hid1', 'hid2', 'hid3', 'hid4', 'hid5', 'hid6', 'hid7', 'out0',
                 'out1', 'out2', 'out3'],
 ('l3f', 'pool'): ['x.rstd']}


class Signals:

    def __init__(self, nc, ctx, steps):
        self.steps = steps
        self.sems = {}
        for key in self.steps:
            self.sems[key] = ctx.enter_context(nc.semaphore("%s_%s_done" % key))

    def sem(self, stage, who):
        return self.sems[stage, who]

    def count(self, stage, who, step, u, it):
        names = self.steps[stage, who]
        return it * (len(names) * U) + (names.index(step) * U + u + 1)


class Engine:

    def __init__(self, signals, who, eng, stage, it, apart=False):
        self.s, self.who, self.eng, self.stage, self.it, self.apart = signals, who, eng, stage, it, apart

    def need(self, who, step, u):
        self.eng.wait_ge(self.s.sem(self.stage, who), self.s.count(self.stage, who, step, u, self.it))
        if self.apart:
            self.eng.nop(nofuse=True)

    def done(self, instruction, step, u):
        instruction.then_inc(self.s.sem(self.stage, self.who), 1)


def build_blocks(nc, tok, out_dram, weights_dram, consts_dram, where_w, where_c):
    with ExitStack() as ctx:
        sb = lambda n, s: ctx.enter_context(nc.sbuf_tensor(n, s, F32))
        sem = lambda n: ctx.enter_context(nc.semaphore(n))
        wts = sb("weights", [128, weights_dram.shape[1]])
        cst = sb("constants", [128, consts_dram.shape[1]])

        def W(name):
            src, where = (wts, where_w) if name in where_w else (cst, where_c)
            p, at, n = where[name]
            return src[0:p, at:at + n]

        hl = sb("hl", [64, TOKENS])
        hx = sb("hx", [128, TOKENS // 128, 64])
        bn = sb("bn", [64, 24])
        per = lambda n, s: [sb(f"{n}{u}", s) for u in R]
        h, x, r, sq = (per(n, [128, T, 64]) for n in ("h", "x", "r", "sq"))
        xT, oT = per("xT", [65, BLK]), per("oT", [65, BLK])
        Q, K = per("qt", [128, BLK]), per("kt", [128, BLK])
        H = per("hid", [128, 2, BLK])
        A16 = per("big", [128, 4096])
        pbd = per("pbd", [128, 16, 128])
        pT = per("pT", [128, 16, 128])
        tmp = [pT[u][:, 0:4, :].rearrange("p t n -> p (t n)") for u in R]
        st = per("st", [128, 192])
        B = [[ctx.enter_context(nc.psum_tensor(f"bank{u}_{b}", [128, 512], F32)) for b in range(4)] for u in R]

        loaded = sem("weights_loaded")
        h_in = [sem(f"h_loaded{u}") for u in R]
        out_sent = [sem(f"out_sent{u}") for u in R]
        ready = sem("constant_tiles_ready")
        bn_done = {w: sem(f"bn_{w}") for w in ("dve", "act", "pool")}
        sig = Signals(nc, ctx, STEPS)
        eye = W("eye")
        lo, hi = slice(0, 64), slice(64, 128)

        def bc(ap, n):
            return ap.unsqueeze(ap.ndim).broadcast_to(list(ap.shape) + [n])

        def bmid(ap, n):
            return ap.unsqueeze(1).broadcast_to([ap.shape[0], n] + list(ap.shape[1:]))

        tf = lambda ap, t=T: ap.rearrange("p (t f) -> p t f", t=t)
        V = nc.vector

        def ln_vector(d, tag, src, dst, eps=1e-5, first=None):
            for u in R:
                if first:
                    first(u)
                else:
                    d.eng.wait_ge(sig.sem(d.before, "dve"), sig.count(d.before, "dve", "h", u, d.it))
                d.done(V.reduce_sum(st[u][:, 0:4], src[u][:], axis=AX.X), tag + ".sum", u)
            for u in R:
                d.need("dve", tag + ".sum", u)
                d.done(V.scalar_tensor_tensor(out=dst[u][:], in0=bc(st[u][:, 0:4], 64), scalar=-1.0 / 64,
                                              in1=src[u][:], op0=ALU.mult, op1=ALU.add), tag + ".centered", u)
            ln_scale(d, tag, dst, dst, eps)

        def ln_scale(d, tag, src, dst, eps):
            for u in R:
                d.need("act", tag + ".sq", u)
                d.done(V.reduce_sum(st[u][:, 4:8], sq[u][:], axis=AX.X), tag + ".sumsq", u)
            for u in R:
                d.need("dve", tag + ".sumsq", u)
                d.done(V.tensor_scalar(st[u][:, 4:8], st[u][:, 4:8], 1.0 / 64, eps, ALU.mult, ALU.add),
                       tag + ".var", u)
            for u in R:
                d.need("pool", tag + ".rstd", u)
                d.done(V.tensor_tensor(dst[u][:], src[u][:], bc(st[u][:, 8:12], 64), ALU.mult), tag + ".out", u)

        def ln_scalar(a, tag, src, after=".centered"):
            for u in R:
                a.need("dve", tag + after if after[0] == "." else after, u)
                a.done(nc.scalar.activation(sq[u][:], src[u][:], ACT.Square), tag + ".sq", u)

        def ln_pool(p, tag):
            for u in R:
                p.need("dve", tag + ".var", u)
                p.done(nc.gpsimd.tensor_tensor(st[u][:, 8:12], st[u][:, 4:8], W("mhalf"), ALU.pow), tag + ".rstd", u)

        def flip_tensor(p, tag, src, after, bank=0):
            for u in R:
                p.need("dve", after, u)
                for t in range(T):
                    last = nc.tensor.transpose(B[u][bank][lo, 128 * t:128 * t + 128], src[u][:, t, :], eye)
                p.done(last, tag + ".flip", u)

        def flip_scalar(a, tag, scale=None, bias=None):
            for u in R:
                a.need("pe", tag + ".flip", u)
                kw = {}
                if scale is not None:
                    kw["scale"] = W(scale)
                if bias is not None:
                    kw["bias"] = W(bias)
                a.done(nc.scalar.activation(xT[u][lo, :], B[u][0][lo, :], ACT.Identity, **kw), tag + ".xT", u)

        def mm(out, lhsT, rhs, start=True, stop=True):
            return nc.tensor.matmul(out, lhsT, rhs, start=start, stop=stop)

        def softmax_vector(d, src, e, g, p=128, after=None):
            for u in R:
                if after:
                    d.need(*after, u)
                d.done(V.reduce_max(st[u][0:p, 16:16 + g], src(u), axis=AX.X), "max", u)
            for u in R:
                d.need("dve", "max", u)
                n = e(u).shape[-1]
                d.done(V.tensor_tensor(e(u), src(u), bc(st[u][0:p, 16:16 + g], n), ALU.subtract), "diff", u)
            for u in R:
                d.need("act", "exp", u)
                d.done(V.reduce_sum(st[u][0:p, 48:48 + g], e(u), axis=AX.X), "sum", u)
            for u in R:
                d.need("dve", "sum", u)
                d.done(V.reciprocal(st[u][0:p, 48:48 + g], st[u][0:p, 48:48 + g]), "recip", u)

        def exp_scalar(a, e, scale=1.0):
            for u in R:
                a.need("dve", "diff", u)
                a.done(nc.scalar.activation(e(u), e(u), ACT.Exp, scale=scale), "exp", u)

        def rank_vector(d, score, n, k, before, after):
            g = lambda u: sq[u][:].rearrange("p t f -> p (t f)")[:, 0:T * n * n].rearrange("p (t e j) -> p t e j", t=T, e=n)
            q = lambda u: r[u][:].rearrange("p t f -> p (t f)")[:, 0:T * n * n].rearrange("p (t e j) -> p t e j", t=T, e=n)
            mine = lambda u: bc(score(u), n)
            other = lambda u: score(u).unsqueeze(2).broadcast_to([128, T, n, n])
            sel = lambda u: st[u][:, 128:128 + T * n].rearrange("p (t e) -> p t e", t=T)
            for u in R:
                d.need("dve", after, u)
                d.done(V.tensor_tensor(g(u), other(u), mine(u), ALU.is_gt), "greater", u)
            for u in R:
                d.done(V.tensor_tensor(q(u), other(u), mine(u), ALU.is_equal), "equal", u)
            for u in R:
                d.need("dve", "equal", u)
                d.done(V.tensor_tensor(q(u), q(u), bmid(W(before).rearrange("p (e j) -> p e j", e=n), T), ALU.mult),
                       "tied", u)
            for u in R:
                d.need("dve", "tied", u)
                d.done(V.tensor_tensor(g(u), g(u), q(u), ALU.add), "ahead", u)
            for u in R:
                d.need("dve", "ahead", u)
                d.done(V.reduce_sum(sel(u), g(u), axis=AX.X), "rank", u)
            for u in R:
                d.need("dve", "rank", u)
                d.done(V.tensor_scalar(sel(u), sel(u), k - 0.5, None, ALU.is_lt), "chosen", u)

        st8 = lambda u, at, n=8: st[u][:, at:at + T * n].rearrange("p (t e) -> p t e", t=T)

        a_q = lambda u: Q[u][lo, :]
        a_k = lambda u: K[u][lo, :]
        a_v = lambda u: tf(A16[u][:, 1024:1280])
        a_e = lambda u: tf(A16[u][:, 0:256])

        def attn_tensor(p, name):
            for u in R:
                p.need("act", "x.xT", u)
                p.done(mm(B[u][1][lo, :], W(name + "_q"), xT[u][:]), "q", u)
            for u in R:
                p.done(mm(B[u][2][lo, :], W(name + "_k"), xT[u][:]), "k", u)
            for u in R:
                for t in range(T):
                    last = mm(B[u][3][:, 64 * t:64 * t + 64], xT[u][:, 128 * t:128 * t + 128], W(name + "_v"))
                p.done(last, "v", u)
            for u in R:
                p.need("act", "q", u)
                p.need("dve", "k", u)
                for b in range(BATCHES):
                    o = slice(64 * (b % 2), 64 * (b % 2) + 64)
                    last = mm(B[u][0][o, 64 * (b // 2):64 * (b // 2) + 64], a_q(u)[:, 64 * b:64 * b + 64],
                              a_k(u)[:, 64 * b:64 * b + 64])
                p.done(last, "scores", u)
            for u in R:
                p.need("dve", "p_hi", u)
                for t in range(T):
                    last = nc.tensor.transpose(B[u][1][:, 128 * t:128 * t + 128], pbd[u][:, t, :], eye)
                p.done(last, "pT", u)
            for u in R:
                p.need("act", "pT", u)
                p.need("dve", "v", u)
                for t in range(T):
                    last = mm(B[u][2][lo, 128 * t:128 * t + 128], a_v(u)[:, t, :], pT[u][:, t, :])
                p.done(last, "attended", u)

        def attn_scalar(a, scale):
            for u in R:
                a.need("pe", "q", u)
                a.done(nc.scalar.activation(a_q(u), B[u][1][lo, :], ACT.Identity), "q", u)
            exp_scalar(a, a_e, scale)
            for u in R:
                a.need("pe", "pT", u)
                a.done(nc.scalar.activation(pT[u][:, 0:T, :].rearrange("p t n -> p (t n)"), B[u][1][:], ACT.Identity),
                       "pT", u)
            for u in R:
                a.need("pe", "attended", u)
                a.done(nc.scalar.activation(oT[u][lo, :], B[u][2][lo, :], ACT.Identity), "oT", u)

        def attn_vector(d, rel=None, scale=None):
            for u in R:
                d.need("pe", "k", u)
                d.done(V.tensor_copy(a_k(u), B[u][2][lo, :]), "k", u)
            for u in R:
                d.need("pe", "v", u)
                d.done(V.tensor_copy(a_v(u), tf(B[u][3][:, 0:256])), "v", u)
            src = lambda u: tf(B[u][0][:, 0:256])
            if rel:
                for u in R:
                    d.need("pe", "scores", u)
                    d.done(V.tensor_tensor(a_e(u), tf(B[u][0][:, 0:256]), bmid(W(rel), T), ALU.add), "biased", u)
                softmax_vector(d, a_e, a_e, T, after=("dve", "biased"))
            else:
                softmax_vector(d, src, a_e, T, after=("pe", "scores"))
            last = "recip"
            if scale:
                for u in R:
                    d.need("dve", "recip", u)
                    d.done(V.tensor_scalar(st[u][:, 48:52], st[u][:, 48:52], W(scale), None, ALU.mult), "scaled", u)
                last = "scaled"
            diag_vector(d, last)

        def diag_vector(d, after):
            for name, part in (("p_lo", lo), ("p_hi", hi)):
                for u in R:
                    d.need("dve", after, u)
                    d.done(V.tensor_tensor(pbd[u][part, 0:T, part], a_e(u)[part], bc(st[u][part, 48:52], 64), ALU.mult),
                           name, u)

        def blk(it, u):
            return U * it + u

        def l0a_tensor(p):
            flip_tensor(p, "x", x, "x.out")
            attn_tensor(p, "l0a")
            for u in R:
                p.need("act", "oT", u)
                p.done(mm(B[u][3][lo, :], W("l0a_l"), oT[u][:]), "hl", u)

        def l0a_scalar(a):
            ln_scalar(a, "x", x)
            flip_scalar(a, "x")
            attn_scalar(a, 1.0 / 64)

        def l0a_vector(d):
            def first(u):
                d.eng.wait_ge(h_in[u], d.it * 16 + 16)
            ln_vector(d, "x", h, x, first=first)
            attn_vector(d)
            for u in R:
                d.done(V.tensor_tensor(hx[:, bass.ds(T * blk(d.it, u), T), :], h[u][:], x[u][:], ALU.add), "hx", u)
            for u in R:
                d.need("pe", "hl", u)
                d.done(V.tensor_copy(hl[:, bass.ds(BLK * blk(d.it, u), BLK)], B[u][3][lo, :]), "hl", u)

        def l0b_scalar(a):
            for u in R:
                a.need("dve", "normed", u)
                a.done(nc.scalar.activation(Q[u][lo, :], Q[u][lo, :], ACT.Relu, bias=W("l0a_beta")), "y", u)

        def l0b_tensor(p):
            for u in R:
                p.need("act", "y", u)
                for t in range(T):
                    last = nc.tensor.transpose(B[u][0][:, 64 * t:64 * t + 64], Q[u][lo, 128 * t:128 * t + 128],
                                               eye[lo, lo])
                p.done(last, "y", u)

        def l0b_vector(d):
            for u in R:
                d.done(V.tensor_scalar(Q[u][lo, :], hl[:, bass.ds(BLK * blk(d.it, u), BLK)], bn[:, 17:18],
                                       bn[:, 20:21], ALU.add, ALU.mult), "normed", u)
            for u in R:
                d.need("pe", "y", u)
                d.eng.wait_ge(out_sent[u], d.it * 16 + 1)
                d.done(V.tensor_tensor(h[u][:], tf(B[u][0][:, 0:256]), hx[:, bass.ds(T * blk(d.it, u), T), :],
                                       ALU.add), "h", u)

        km = lambda u: A16[u][lo, 0:2048].rearrange("p (h n) -> p h n", h=4)
        vm = lambda u: tf(A16[u][:, 2048:3072])
        f_e = lambda u: A16[u][:, 3072:4096].rearrange("p (g n) -> p g n", g=16)
        rope = lambda ap: ap.rearrange("p (b n) -> p b n", n=SEQ)

        def l0f_tensor(p):
            flip_tensor(p, "r", r, "r.out")
            for name, b in (("q", 1), ("qp", 2), ("k", 3)):
                for u in R:
                    if b == 1:
                        p.need("act", "r.xT", u)
                    p.done(mm(B[u][b][lo, :], W("l0f_" + name), xT[u][lo, :]), name, u)
            for u in R:
                p.done(mm(B[u][0][lo, :], W("l0f_kp"), xT[u][lo, :]), "kp", u)
            for u in R:
                p.need("dve", "qb", u)
                for t in range(T):
                    last = mm(B[u][1 + t // 2][:, 256 * (t % 2):256 * (t % 2) + 256], xT[u][lo, 128 * t:128 * t + 128],
                              W("l0f_v"))
                p.done(last, "v", u)
            for u in R:
                p.need("act", "km", u)
                p.need("dve", "kb", u)
                for b in range(BATCHES):
                    o = slice(64 * (b % 2), 64 * (b % 2) + 64)
                    t = b // 2
                    last = mm(B[u][3 if t < 2 else 0][o, 256 * (t % 2):256 * (t % 2) + 256], Q[u][lo, 64 * b:64 * b + 64],
                              km(u)[:, :, 64 * b:64 * b + 64])
                p.done(last, "scores", u)
            for t in range(T):
                for u in R:
                    if t == 0:
                        p.need("dve", "p_hi", u)
                        p.need("act", "v", u)
                    for g in range(4):
                        last = nc.tensor.transpose(B[u][t][:, 128 * g:128 * g + 128], pbd[u][:, 4 * t + g, :], eye)
                    p.done(last, f"pT{t}", u)
            for u in R:
                p.need("act", "pT2", u)
                p.need("dve", "pT3", u)
                for t in range(T):
                    for g in range(4):
                        last = mm(B[u][0][lo, 128 * t:128 * t + 128], vm(u)[:, t, 64 * g:64 * g + 64],
                                  pT[u][:, 4 * t + g, :], start=(g == 0), stop=(g == 3))
                p.done(last, "attended", u)
            for u in R:
                p.need("act", "oT", u)
                for t in range(T):
                    last = mm(B[u][1][:, 64 * t:64 * t + 64], oT[u][lo, 128 * t:128 * t + 128], W("l0f_wo"))
                p.done(last, "wo", u)
            flip_tensor(p, "f", r, "f.out")
            for u in R:
                p.need("act", "f.xT", u)
                for t in range(T):
                    last = mm(B[u][2][:, 8 * t:8 * t + 8], xT[u][lo, 128 * t:128 * t + 128], W("l0f_router"))
                p.done(last, "logits", u)
            for u in R:
                p.need("dve", "gates", u)
                for t in range(T):
                    last = nc.tensor.transpose(B[u][3][0:8, 128 * t:128 * t + 128], st8(u, 160)[:, t, :], eye)
                p.done(last, "gatesT", u)
            for j in range(NTILE + 1):
                if j < NTILE:
                    cols = slice(128 * j, 128 * j + 128)
                    for u in R:
                        if j:
                            p.need("act", f"silu{j - 1}", u)
                        p.done(mm(B[u][1][:], W("l0f_w1")[:, cols], xT[u][lo, :]), f"gate{j}", u)
                    for u in R:
                        if j:
                            p.need("dve", f"up{j - 1}", u)
                        p.done(mm(B[u][2][:], W("l0f_w3")[:, cols], xT[u][lo, :]), f"up{j}", u)
                    for u in R:
                        if j:
                            p.need("dve", f"hid{j - 1}", u)
                        else:
                            p.need("act", "gatesT", u)
                        p.done(mm(B[u][3][:], W("expand")[:, cols], tmp[u][0:8, :]), f"share{j}", u)
                if j:
                    for u in R:
                        p.need("dve", f"hid{j - 1}", u)
                        p.done(mm(B[u][0][lo, :], W("l0f_w2")[:, 64 * (j - 1):64 * j], Q[u][:], start=(j == 1),
                                  stop=(j == NTILE)), f"down{j - 1}", u)
            for u in R:
                p.need("act", "yT", u)
                for t in range(T):
                    last = nc.tensor.transpose(B[u][1][:, 64 * t:64 * t + 64], oT[u][lo, 128 * t:128 * t + 128],
                                               eye[lo, lo])
                p.done(last, "y", u)

        def l0f_scalar(a):
            ln_scalar(a, "x", x)
            ln_scalar(a, "r", x, after="x.out")
            flip_scalar(a, "r", scale="l0f_ln1")
            for u in R:
                a.need("dve", "k", u)
                for g in range(4):
                    last = nc.scalar.activation(km(u)[:, g, :], K[u][lo, :], ACT.Identity, scale=W("headmask")[:, g:g + 1])
                a.done(last, "km", u)
            for u in R:
                a.need("pe", "v", u)
                for b in range(2):
                    last = nc.scalar.activation(vm(u)[:, 2 * b:2 * b + 2, :], tf(B[u][1 + b][:], 2), ACT.Identity)
                a.done(last, "v", u)
            exp_scalar(a, f_e, 0.25)
            for t in (0, 2):
                for u in R:
                    a.need("pe", f"pT{t}", u)
                    a.done(nc.scalar.activation(pT[u][:, 4 * t:4 * t + 4, :].rearrange("p t n -> p (t n)"), B[u][t][:],
                                                ACT.Identity), f"pT{t}", u)
            for u in R:
                a.need("pe", "attended", u)
                a.done(nc.scalar.activation(oT[u][lo, :], B[u][0][lo, :], ACT.Identity), "oT", u)
            ln_scalar(a, "f", x, after="x2")
            flip_scalar(a, "f", scale="l0f_ln2")
            small_exp(a, 8, "exp_router")
            for u in R:
                a.need("pe", "gatesT", u)
                a.done(nc.scalar.activation(tmp[u][0:8, :], B[u][3][0:8, :], ACT.Identity), "gatesT", u)
            for j in range(NTILE):
                for u in R:
                    a.need("pe", f"gate{j}", u)
                    if j:
                        a.need("dve", f"up{j - 1}", u)
                    a.done(nc.scalar.activation(K[u][:], B[u][1][:], ACT.Silu), f"silu{j}", u)
            for u in R:
                a.need("pe", f"down{NTILE - 1}", u)
                a.done(nc.scalar.activation(oT[u][lo, :], B[u][0][lo, :], ACT.Identity), "yT", u)

        def l0f_vector(d):
            ln_vector(d, "x", h, x)
            ln_scale(d, "r", x, r, 1e-6)
            for name, b, table, dst, wait in (("qa", 1, "cos", 0, "q"), ("qb", 2, "sin", 1, "qp")):
                for u in R:
                    d.need("pe", wait, u)
                    d.done(V.tensor_tensor(rope(H[u][lo, dst, :]), rope(B[u][b][lo, :]), bmid(W(table), BATCHES), ALU.mult),
                           name, u)
            for u in R:
                d.need("dve", "qb", u)
                d.done(V.tensor_tensor(Q[u][lo, :], H[u][lo, 0, :], H[u][lo, 1, :], ALU.add), "q", u)
            for name, b, table, dst, wait in (("ka", 3, "cos", 0, "k"), ("kb", 0, "sin", 1, "kp")):
                for u in R:
                    d.need("pe", wait, u)
                    d.need("dve", "q", u)
                    d.done(V.tensor_tensor(rope(H[u][lo, dst, :]), rope(B[u][b][lo, :]), bmid(W(table), BATCHES), ALU.mult),
                           name, u)
            for u in R:
                d.need("dve", "kb", u)
                d.done(V.tensor_tensor(K[u][lo, :], H[u][lo, 0, :], H[u][lo, 1, :], ALU.add), "k", u)
            for b, bank in ((0, 3), (1, 0)):
                for u in R:
                    d.need("pe", "scores", u)
                    d.done(V.tensor_tensor(f_e(u)[:, 8 * b:8 * b + 8, :], B[u][bank][:].rearrange("p (g n) -> p g n", g=8),
                                           bmid(W("causal"), 8), ALU.add), f"masked{b}", u)
            softmax_vector(d, f_e, f_e, 16, after=("dve", "masked1"))
            for name, part in (("p_lo", lo), ("p_hi", hi)):
                for u in R:
                    d.need("dve", "recip", u)
                    d.done(V.tensor_tensor(pbd[u][part, :, part], f_e(u)[part], bc(st[u][part, 48:64], 64), ALU.mult),
                           name, u)
            for t in (1, 3):
                for u in R:
                    d.need("pe", f"pT{t}", u)
                    d.done(V.tensor_copy(pT[u][:, 4 * t:4 * t + 4, :].rearrange("p t n -> p (t n)"), B[u][t][:]),
                           f"pT{t}", u)
            for u in R:
                d.need("pe", "wo", u)
                d.done(V.tensor_tensor(x[u][:], x[u][:], tf(B[u][1][:, 0:256]), ALU.add), "x2", u)
            ln_scale(d, "f", x, r, 1e-6)
            router = lambda u: tf(B[u][2][:, 0:32])
            small_softmax(d, router, 8, "logits", "exp_router")
            rank_vector(d, lambda u: st8(u, 96), 8, 2, "before", "probs")
            for u in R:
                d.need("dve", "chosen", u)
                d.done(V.tensor_tensor(st8(u, 160), st8(u, 96), st8(u, 128), ALU.mult), "kept", u)
            for u in R:
                d.need("dve", "kept", u)
                d.done(V.reduce_sum(st[u][:, 48:52], st8(u, 160), axis=AX.X), "kept_sum", u)
            for u in R:
                d.need("dve", "kept_sum", u)
                d.done(V.tensor_scalar(st[u][:, 48:52], st[u][:, 48:52], 1e-9, None, ALU.add), "kept_eps", u)
            for u in R:
                d.need("dve", "kept_eps", u)
                d.done(V.reciprocal(st[u][:, 48:52], st[u][:, 48:52]), "kept_recip", u)
            for u in R:
                d.need("dve", "kept_recip", u)
                d.done(V.tensor_tensor(st8(u, 160), st8(u, 160), bc(st[u][:, 48:52], 8), ALU.mult), "gates", u)
            for j in range(NTILE):
                for u in R:
                    d.need("act", f"silu{j}", u)
                    d.need("pe", f"up{j}", u)
                    if j:
                        d.need("pe", f"down{j - 1}", u)
                    d.done(V.tensor_tensor(Q[u][:], B[u][2][:], K[u][:], ALU.mult), f"up{j}", u)
                for u in R:
                    d.need("dve", f"up{j}", u)
                    d.need("pe", f"share{j}", u)
                    d.done(V.tensor_tensor(Q[u][:], B[u][3][:], Q[u][:], ALU.mult), f"hid{j}", u)
            for u in R:
                d.done(V.tensor_tensor(h[u][:], h[u][:], x[u][:], ALU.add), "h_x", u)
            for u in R:
                d.need("pe", "y", u)
                d.need("dve", "h_x", u)
                d.done(V.tensor_tensor(h[u][:], h[u][:], tf(B[u][1][:, 0:256]), ALU.add), "h", u)

        def small_softmax(d, src, n, after, exp_step, at=96, who="pe"):
            m, s = slice(80, 84), slice(84, 88)
            for u in R:
                d.need(who, after, u)
                d.done(V.reduce_max(st[u][:, m], src(u), axis=AX.X), "emax", u)
            for u in R:
                d.need("dve", "emax", u)
                d.done(V.tensor_tensor(st8(u, at, n), src(u), bc(st[u][:, m], n), ALU.subtract), "ediff", u)
            for u in R:
                d.need("act", exp_step, u)
                d.done(V.reduce_sum(st[u][:, s], st8(u, at, n), axis=AX.X), "esum", u)
            for u in R:
                d.need("dve", "esum", u)
                d.done(V.reciprocal(st[u][:, s], st[u][:, s]), "erecip", u)
            for u in R:
                d.need("dve", "erecip", u)
                d.done(V.tensor_tensor(st8(u, at, n), st8(u, at, n), bc(st[u][:, s], n), ALU.mult), "probs", u)

        def small_exp(a, n, step, at=96):
            for u in R:
                a.need("dve", "ediff", u)
                a.done(nc.scalar.activation(st8(u, at, n), st8(u, at, n), ACT.Exp), step, u)

        def l1a_tensor(p):
            flip_tensor(p, "x", r, "r.out")
            attn_tensor(p, "l1a")
            for u in R:
                p.need("act", "oT", u)
                for t in range(T):
                    last = mm(B[u][3][:, 64 * t:64 * t + 64], oT[u][:, 128 * t:128 * t + 128], W("l1a_l"))
                p.done(last, "proj", u)

        def l1a_scalar(a):
            ln_scalar(a, "x", x)
            ln_scalar(a, "r", r)
            flip_scalar(a, "x", scale="l1a_g", bias="l1a_b")
            attn_scalar(a, 1.0)
            ln_scalar(a, "o", r)

        def l1a_vector(d):
            ln_vector(d, "x", h, x)
            ln_vector(d, "r", x, r, first=lambda u: d.need("dve", "x.out", u))
            attn_vector(d, rel="l1a_rel", scale="l1a_scale")
            for u in R:
                d.need("pe", "proj", u)
                d.done(V.tensor_copy(x[u][:], tf(B[u][3][:, 0:256])), "proj", u)
            ln_vector(d, "o", x, r, first=lambda u: d.need("dve", "proj", u))
            for u in R:
                d.need("dve", "o.out", u)
                d.done(V.tensor_tensor(r[u][:], r[u][:], bmid(W("l1a_g2"), T), ALU.mult), "o.g", u)
            for u in R:
                d.done(V.tensor_tensor(h[u][:], h[u][:], bmid(W("l1a_b2"), T), ALU.add), "h_b", u)
            for u in R:
                d.need("dve", "o.g", u)
                d.need("dve", "h_b", u)
                d.done(V.tensor_tensor(h[u][:], h[u][:], r[u][:], ALU.add), "h", u)

        def gelu_hidden_tensor(p, w, tag):
            for a in range(2):
                for u in R:
                    if a == 0:
                        p.need("act", tag + ".xT", u)
                    p.done(mm(B[u][1 + a][:], W(w)[:, 128 * a:128 * a + 128], xT[u][lo, :]), f"hid{a}", u)

        def gelu_hidden_scalar(a, bias, func=None):
            for k in range(2):
                for u in R:
                    a.need("pe", f"hid{k}", u)
                    a.done(nc.scalar.activation(H[u][:, k, :], B[u][1 + k][:], ACT.Gelu if func is None else func,
                                                bias=W(bias)[:, k:k + 1]), f"hid{k}", u)

        def weigh_vector(d, t, bank, weight, n, after, bias=None):
            part = lambda u: pT[u][:, 4 * (t % 2):4 * (t % 2) + 4, :].rearrange("p t n -> p (t n)")[:, 0:64 * n]
            for u in R:
                d.need("pe", after, u)
                if t >= 2:
                    d.need("dve", f"summed{t - 2}", u)
                if bias is not None:
                    d.done(V.tensor_tensor(part(u).rearrange("p (e f) -> p e f", e=n), bank(u),
                                           bias.rearrange("p (e f) -> p e f", e=n), ALU.add), f"raised{t}", u)
            for u in R:
                if bias is not None:
                    d.need("dve", f"raised{t}", u)
                src = bank(u) if bias is None else part(u).rearrange("p (e f) -> p e f", e=n)
                d.done(V.tensor_tensor(part(u).rearrange("p (e f) -> p e f", e=n), src,
                                       bc(weight(u)[:, t, :], 64), ALU.mult), f"weighed{t}", u)
            for u in R:
                d.need("dve", f"weighed{t}", u)
                d.done(V.reduce_sum(r[u][:, t, :], part(u).rearrange("p (e f) -> p f e", e=n), axis=AX.X),
                       f"summed{t}", u)

        def add_r(d, step="h", after=f"summed{T - 1}"):
            for u in R:
                d.need("dve", after, u)
                d.done(V.tensor_tensor(h[u][:], h[u][:], r[u][:], ALU.add), step, u)

        def l1f_tensor(p):
            flip_tensor(p, "x", x, "x.out")
            gelu_hidden_tensor(p, "l1f_w1", "x")
            for u in R:
                p.need("act", "hid1", u)
                for t in range(T):
                    for a in range(2):
                        last = mm(B[u][3][:, 8 * t:8 * t + 8], H[u][:, a, 128 * t:128 * t + 128],
                                  W("l1f_wg")[:, 8 * a:8 * a + 8], start=(a == 0), stop=(a == 1))
                p.done(last, "logits", u)
            for t in range(T):
                for u in R:
                    if t == 3:
                        p.need("dve", "biased", u)
                    for a in range(2):
                        last = mm(B[u][t][:], H[u][:, a, 128 * t:128 * t + 128], W("l1f_wd")[:, 512 * a:512 * a + 512],
                                  start=(a == 0), stop=(a == 1))
                    p.done(last, f"out{t}", u)

        def l1f_scalar(a):
            ln_scalar(a, "x", x)
            flip_scalar(a, "x")
            gelu_hidden_scalar(a, "l1f_b1")
            small_exp(a, 8, "exp")

        def l1f_vector(d):
            ln_vector(d, "x", h, x)
            for u in R:
                d.need("pe", "logits", u)
                d.done(V.tensor_tensor(st8(u, 160), tf(B[u][3][:, 0:32]), bmid(W("l1f_bg"), T), ALU.add), "biased", u)
            small_softmax(d, lambda u: st8(u, 160), 8, "biased", "exp", who="dve")
            rank_vector(d, lambda u: st8(u, 96), 8, 1, "before", "probs")
            for u in R:
                d.need("dve", "chosen", u)
                d.done(V.tensor_tensor(st8(u, 128), st8(u, 96), st8(u, 128), ALU.mult), "gates", u)
            for u in R:
                d.need("dve", "gates", u)
            for t in range(T):
                weigh_vector(d, t, lambda u: B[u][t][:].rearrange("p (e f) -> p e f", e=8), lambda u: st8(u, 128), 8,
                             f"out{t}", W("l1f_bd"))
            add_r(d)

        a2_v = lambda u: tf(A16[u][:, 0:1024])
        a2_k = lambda u: A16[u][0:32, 1024:1536]
        a2_q = lambda u: A16[u][:, 1536:1664].rearrange("p (g r) -> p g r", r=4)
        a2_q4 = lambda u: tf(A16[u][:, 1664:2176])
        a2_k4 = lambda u: tf(A16[u][:, 2176:2688])
        a2_kv = lambda u: A16[u][:, 2688:3200].rearrange("p (g n) -> p g n", g=2)
        a2_o = lambda u: pT[u][:, 0:8, :].rearrange("p (a t) n -> p a (t n)", a=2)

        def spread(u, dst, k, part):
            rep = 2 * k + (0 if part is lo else 1)
            return dst(u)[part, k:T:2, 32 * rep:32 * rep + 32]

        def l2a_tensor(p):
            flip_tensor(p, "x", r, "r.out")
            gelu_hidden_tensor(p, "l2a_wx", "x")
            for u in R:
                p.need("act", "hid1", u)
                for t in range(T):
                    for a in range(2):
                        last = mm(B[u][3][:, 32 * t:32 * t + 32], H[u][:, a, 128 * t:128 * t + 128],
                                  W("l2a_wq")[:, 32 * a:32 * a + 32], start=(a == 0), stop=(a == 1))
                p.done(last, "q", u)
            for u in R:
                for a in range(2):
                    last = mm(B[u][0][0:32, :], W("l2a_wk")[:, 32 * a:32 * a + 32], H[u][:, a, :], start=(a == 0),
                              stop=(a == 1))
                p.done(last, "k", u)
            for u in R:
                for t in range(T):
                    for a in range(2):
                        c = 256 * (t % 2) + 128 * a
                        last = mm(B[u][1 + t // 2][:, c:c + 128], H[u][:, a, 128 * t:128 * t + 128], W("l2a_wv"))
                p.done(last, "v", u)
            for u in R:
                p.need("dve", "kprob", u)
                p.need("dve", "diff", u)
                for t in range(T):
                    last = nc.tensor.transpose(B[u][3][:, 32 * t:32 * t + 32], a2_k(u)[:, 128 * t:128 * t + 128],
                                               eye[0:32, 0:32])
                p.done(last, "kT", u)
            for u in R:
                p.need("act", "k4", u)
                p.need("act", "v", u)
                for t in range(T):
                    last = mm(B[u][0][:, 256 * (t // 2):256 * (t // 2) + 256], a2_k4(u)[:, t, :], a2_v(u)[:, t, :],
                              start=(t % 2 == 0), stop=(t % 2 == 1))
                p.done(last, "kv", u)
            for u in R:
                p.need("dve", "q4", u)
                for t in range(T):
                    last = nc.tensor.transpose(B[u][1][:, 128 * t:128 * t + 128], a2_q4(u)[:, t, :], eye)
                p.done(last, "q4T", u)
            for a in range(2):
                for u in R:
                    if a == 0:
                        p.need("act", "q4T", u)
                        p.need("dve", "kv", u)
                    for g in range(2):
                        last = mm(B[u][2 + a][:, 256 * g:256 * g + 256], a2_kv(u)[:, g, 128 * a:128 * a + 128],
                                  Q[u][:, 256 * g:256 * g + 256])
                    p.done(last, f"o{a}", u)
            for u in R:
                p.need("act", "o0", u)
                p.need("dve", "o1", u)
                for t in range(T):
                    for a in range(2):
                        last = mm(B[u][0][:, 64 * t:64 * t + 64], a2_o(u)[:, a, 128 * t:128 * t + 128],
                                  W("l2a_wo")[:, 64 * a:64 * a + 64], start=(a == 0), stop=(a == 1))
                p.done(last, "wo", u)
            flip_tensor(p, "f", r, "f.out")
            for a in range(2):
                for u in R:
                    if a == 0:
                        p.need("act", "f.xT", u)
                    p.done(mm(B[u][1 + a][:], W("l2a_w1")[:, 128 * a:128 * a + 128], xT[u][lo, :]), f"ff{a}", u)
            for u in R:
                p.need("act", "ff1", u)
                for t in range(T):
                    for a in range(2):
                        last = mm(B[u][3][:, 64 * t:64 * t + 64], H[u][:, a, 128 * t:128 * t + 128],
                                  W("l2a_w2")[:, 64 * a:64 * a + 64], start=(a == 0), stop=(a == 1))
                p.done(last, "ff", u)

        def l2a_pool(p):
            ln_pool(p, "x")
            for u in R:
                p.need("dve", "x.out", u)
                p.done(nc.gpsimd.memset(A16[u][:, 1664:2688], 0.0), "zeros", u)
            ln_pool(p, "r")
            ln_pool(p, "f")

        def l2a_scalar(a):
            ln_scalar(a, "x", x)
            ln_scalar(a, "r", r)
            flip_scalar(a, "x", scale="l2a_g", bias="l2a_b")
            gelu_hidden_scalar(a, "l2a_bx", func=ACT.Identity)
            exp_scalar(a, a2_q)
            for u in R:
                a.need("dve", "kdiff", u)
                a.done(nc.scalar.activation(a2_k(u), a2_k(u), ACT.Exp), "kexp", u)
            for u in R:
                a.need("pe", "v", u)
                for b in range(2):
                    last = nc.scalar.activation(a2_v(u)[:, 2 * b:2 * b + 2, :], tf(B[u][1 + b][:], 2), ACT.Identity)
                a.done(last, "v", u)
            for u in R:
                a.need("pe", "kT", u)
                a.need("pool", "zeros", u)
                for k in range(2):
                    for part in (lo, hi):
                        last = nc.scalar.activation(spread(u, a2_k4, k, part), tf(B[u][3][:, 0:128])[part, k:T:2, :],
                                                    ACT.Identity)
                a.done(last, "k4", u)
            for u in R:
                a.need("pe", "q4T", u)
                a.done(nc.scalar.activation(Q[u][:], B[u][1][:], ACT.Identity), "q4T", u)
            for u in R:
                a.need("pe", "o0", u)
                a.done(nc.scalar.activation(a2_o(u)[:, 0, :], B[u][2][:], ACT.Identity), "o0", u)
            ln_scalar(a, "f", r)
            flip_scalar(a, "f", scale="l2a_g2", bias="l2a_b2")
            for k in range(2):
                for u in R:
                    a.need("pe", f"ff{k}", u)
                    a.done(nc.scalar.activation(H[u][:, k, :], B[u][1 + k][:], ACT.Gelu, bias=W("l2a_fb1")[:, k:k + 1]),
                           f"ff{k}", u)

        def l2a_vector(d):
            ln_vector(d, "x", h, x)
            ln_vector(d, "r", x, r, first=lambda u: d.need("dve", "x.out", u))
            softmax_vector(d, lambda u: B[u][3][:, 0:128].rearrange("p (g r) -> p g r", r=4), a2_q, 32,
                           after=("pe", "q"))
            for u in R:
                d.need("pool", "zeros", u)
                d.need("dve", "recip", u)
                for k in range(2):
                    for part in (lo, hi):
                        last = V.tensor_tensor(spread(u, a2_q4, k, part).rearrange("p t (h r) -> p t h r", r=4),
                                               a2_q(u)[part].rearrange("p (t h) r -> p t h r", t=T)[:, k:T:2],
                                               bc(st[u][part, 48:80].rearrange("p (t h) -> p t h", t=T)[:, k:T:2], 4),
                                               ALU.mult)
                d.done(last, "q4", u)
            kb = lambda ap: ap.rearrange("p (b n) -> p b n", n=SEQ)
            for u in R:
                d.need("pe", "k", u)
                d.done(V.reduce_max(st[u][0:32, 80:88], kb(B[u][0][0:32, :]), axis=AX.X), "kmax", u)
            for u in R:
                d.need("dve", "kmax", u)
                d.done(V.tensor_tensor(kb(a2_k(u)), kb(B[u][0][0:32, :]), bc(st[u][0:32, 80:88], SEQ), ALU.subtract),
                       "kdiff", u)
            for u in R:
                d.need("act", "kexp", u)
                d.done(V.reduce_sum(st[u][0:32, 88:96], kb(a2_k(u)), axis=AX.X), "ksum", u)
            for u in R:
                d.need("dve", "ksum", u)
                d.done(V.reciprocal(st[u][0:32, 88:96], st[u][0:32, 88:96]), "krecip", u)
            for u in R:
                d.need("dve", "krecip", u)
                d.done(V.tensor_tensor(kb(a2_k(u)), kb(a2_k(u)), bc(st[u][0:32, 88:96], SEQ), ALU.mult), "kprob", u)
            for u in R:
                d.need("pe", "kv", u)
                d.done(V.tensor_tensor(a2_kv(u), tf(B[u][0][:], 2), bmid(W("diag32"), 2), ALU.mult), "kv", u)
            for u in R:
                d.need("pe", "o1", u)
                d.done(V.tensor_copy(a2_o(u)[:, 1, :], B[u][3][:]), "o1", u)
            for u in R:
                d.done(V.tensor_tensor(x[u][:], x[u][:], bmid(W("l2a_bo"), T), ALU.add), "x_bo", u)
            for u in R:
                d.need("pe", "wo", u)
                d.need("dve", "x_bo", u)
                d.done(V.tensor_tensor(x[u][:], x[u][:], tf(B[u][0][:, 0:256]), ALU.add), "fx", u)
            ln_vector(d, "f", x, r, first=lambda u: d.need("dve", "fx", u))
            for u in R:
                d.done(V.tensor_tensor(x[u][:], x[u][:], bmid(W("l2a_fb2"), T), ALU.add), "fx_b", u)
            for u in R:
                d.need("dve", "fx_b", u)
                d.done(V.tensor_tensor(h[u][:], h[u][:], x[u][:], ALU.add), "h_fx", u)
            for u in R:
                d.need("pe", "ff", u)
                d.need("dve", "h_fx", u)
                d.done(V.tensor_tensor(h[u][:], h[u][:], tf(B[u][3][:, 0:256]), ALU.add), "h", u)

        e1 = lambda u, e: pT[u][:, 4 * (e % 2):4 * (e % 2) + 4, :].rearrange("p t n -> p (t n)")

        def l2f_tensor(p):
            flip_tensor(p, "x", x, "x.out")
            for u in R:
                p.need("act", "x.xT", u)
                for t in range(T):
                    last = mm(B[u][3][:, 4 * t:4 * t + 4], xT[u][lo, 128 * t:128 * t + 128], W("l2f_g"))
                p.done(last, "logits", u)
            for u in R:
                p.done(mm(B[u][0][lo, :], W("l2f_s1"), xT[u][lo, :]), "s1", u)
            for u in R:
                p.need("act", "s1", u)
                p.done(mm(B[u][1][:], W("l2f_s2"), Q[u][lo, :]), "s2", u)
            for u in R:
                p.need("act", "s2", u)
                for t in range(T):
                    last = mm(B[u][2][:, 64 * t:64 * t + 64], K[u][:, 128 * t:128 * t + 128], W("l2f_s3"))
                p.done(last, "s3", u)
            for e in range(5):
                if e < 4:
                    for u in R:
                        if e >= 2:
                            p.need("act", f"e1_{e - 2}", u)
                        p.done(mm(B[u][e % 2][:], W("l2f_e1")[:, 128 * e:128 * e + 128], xT[u][lo, :]), f"e1_{e}", u)
                if e:
                    k = e - 1
                    for u in R:
                        p.need("act", f"e1_{k}", u)
                        if k == 0:
                            p.need("dve", "biased", u)
                        if k == 2:
                            p.need("dve", "e2_0", u)
                        o = slice(64 * (k % 2), 64 * (k % 2) + 64)
                        p.done(mm(B[u][3][o, :], W("l2f_e2")[:, 64 * k:64 * k + 64], e1(u, k)), f"e2_{k}", u)
            for b in range(2):
                for u in R:
                    p.need("dve", "e2_1", u)
                    for t in (2 * b, 2 * b + 1):
                        o = B[u][b][:, 256 * (t % 2):256 * (t % 2) + 256]
                        mm(o, W("ones")[:, 0:128], W("l2f_eb3"), start=True, stop=False)
                        for k in range(2):
                            last = mm(o[:, 128 * k:128 * k + 128], H[u][:, k, 128 * t:128 * t + 128],
                                      W("l2f_e3")[:, 128 * k:128 * k + 128], start=False, stop=(k == 1))
                    p.done(last, f"out{b}", u)

        def l2f_scalar(a):
            ln_scalar(a, "x", x)
            flip_scalar(a, "x")
            for u in R:
                a.need("pe", "s1", u)
                a.done(nc.scalar.activation(Q[u][lo, :], B[u][0][lo, :], ACT.Relu, bias=W("l2f_sb1")), "s1", u)
            for u in R:
                a.need("pe", "s2", u)
                a.done(nc.scalar.activation(K[u][:], B[u][1][:], ACT.Relu, bias=W("l2f_sb2")), "s2", u)
            small_exp(a, 4, "exp")
            for e in range(4):
                for u in R:
                    a.need("pe", f"e1_{e}", u)
                    if e >= 2:
                        a.need("pe", f"e2_{e - 2}", u)
                    a.done(nc.scalar.activation(e1(u, e), B[u][e % 2][:], ACT.Relu, bias=W("l2f_eb1")[:, e:e + 1]),
                           f"e1_{e}", u)
            for u in R:
                a.need("dve", "tdiff", u)
                a.done(nc.scalar.activation(st8(u, 96, 4), st8(u, 96, 4), ACT.Exp), "texp", u)

        def l2f_vector(d):
            ln_vector(d, "x", h, x)
            for u in R:
                d.need("pe", "logits", u)
                d.done(V.tensor_tensor(st8(u, 160, 4), tf(B[u][3][:, 0:16]), bmid(W("l2f_gb"), T), ALU.add), "biased", u)
            small_softmax(d, lambda u: st8(u, 160, 4), 4, "biased", "exp", who="dve")
            for k in range(2):
                for u in R:
                    d.need("pe", f"e2_{2 * k + 1}", u)
                    d.done(V.tensor_scalar(H[u][:, k, :], B[u][3][:], W("l2f_eb2")[:, k:k + 1], 0.0, ALU.add, ALU.max),
                           f"e2_{k}", u)
            rank_vector(d, lambda u: st8(u, 96, 4), 4, 2, "before4", "probs")
            for u in R:
                d.need("dve", "chosen", u)
                d.done(V.reduce_max(st[u][:, 80:84], st8(u, 96, 4), axis=AX.X), "tmax", u)
            for u in R:
                d.need("dve", "tmax", u)
                d.done(V.tensor_tensor(st8(u, 96, 4), st8(u, 96, 4), bc(st[u][:, 80:84], 4), ALU.subtract), "tdiff", u)
            for u in R:
                d.need("act", "texp", u)
                d.done(V.tensor_tensor(st8(u, 128, 4), st8(u, 96, 4), st8(u, 128, 4), ALU.mult), "tkept", u)
            for u in R:
                d.need("dve", "tkept", u)
                d.done(V.reduce_sum(st[u][:, 84:88], st8(u, 128, 4), axis=AX.X), "tsum", u)
            for u in R:
                d.need("dve", "tsum", u)
                d.done(V.reciprocal(st[u][:, 84:88], st[u][:, 84:88]), "trecip", u)
            for u in R:
                d.need("dve", "trecip", u)
                d.done(V.tensor_tensor(st8(u, 128, 4), st8(u, 128, 4), bc(st[u][:, 84:88], 4), ALU.mult), "gates", u)
            for u in R:
                d.done(V.tensor_tensor(h[u][:], h[u][:], bmid(W("l2f_sb3"), T), ALU.add), "h_b", u)
            for u in R:
                d.need("pe", "s3", u)
                d.need("dve", "h_b", u)
                d.done(V.tensor_tensor(h[u][:], h[u][:], tf(B[u][2][:, 0:256]), ALU.add), "h_s", u)
            for u in R:
                d.need("dve", "gates", u)
            for t in range(T):
                weigh_vector(d, t, lambda u: B[u][t // 2][:, 256 * (t % 2):256 * (t % 2) + 256]
                             .rearrange("p (e f) -> p e f", e=4), lambda u: st8(u, 128, 4), 4, f"out{t // 2}")
            add_r(d)

        V8 = lambda u: tf(A16[u][:, 0:2048])
        o3 = lambda u, k: pT[u][:, 4 * k:4 * k + 4, :].rearrange("p t n -> p (t n)")

        def l3a_tensor(p):
            flip_tensor(p, "x", x, "x.out")
            for t in (1, 2, 3, 0):
                for u in R:
                    if t == 1:
                        p.need("act", "x.xT", u)
                    p.done(mm(B[u][t][:], xT[u][lo, 128 * t:128 * t + 128], W("l3a_v")), f"v{t}", u)
            for k in range(4):
                cols = slice(128 * k, 128 * k + 128)
                for u in R:
                    if k == 0:
                        p.need("act", "v0", u)
                    else:
                        p.need("act", f"o{k - 1}", u)
                    p.done(mm(B[u][0][:], W("l3a_q")[:, cols], xT[u][lo, :]), f"q{k}", u)
                for u in R:
                    if k == 0:
                        p.need("dve", "v1", u)
                    else:
                        p.need("dve", f"k{k - 1}", u)
                    p.done(mm(B[u][1][:], W("l3a_k")[:, cols], xT[u][lo, :]), f"k{k}", u)
                for g, part in enumerate((lo, hi)):
                    for u in R:
                        if g == 0:
                            p.need("act", f"q{k}", u)
                            p.need("dve", f"k{k}", u)
                        if k == 0 and g == 0:
                            p.need("dve", "v3", u)
                            p.need("act", "v2", u)
                        for b in range(BATCHES):
                            o = slice(64 * (b % 2), 64 * (b % 2) + 64)
                            last = mm(B[u][2 + g][o, 64 * (b // 2):64 * (b // 2) + 64], K[u][part, 64 * b:64 * b + 64],
                                      Q[u][part, 64 * b:64 * b + 64])
                        p.done(last, f"s{k}_{g}", u)
                for u in R:
                    p.need("act", f"p{k}_1", u)
                    for g, part in enumerate((lo, hi)):
                        for t in range(T):
                            last = mm(B[u][0][part, 128 * t:128 * t + 128],
                                      V8(u)[:, t, 64 * (2 * k + g):64 * (2 * k + g) + 64], pbd[u][:, 4 * g + t, :])
                    p.done(last, f"o{k}", u)
            for u in R:
                p.need("act", "o3", u)
                p.need("dve", "k3", u)
                for t in range(T):
                    for k in range(4):
                        last = mm(B[u][1][:, 64 * t:64 * t + 64], o3(u, k)[:, 128 * t:128 * t + 128],
                                  W("l3a_o")[:, 64 * k:64 * k + 64], start=(k == 0), stop=(k == 3))
                p.done(last, "wo", u)

        def l3a_scalar(a):
            ln_scalar(a, "x", x)
            flip_scalar(a, "x")
            for t in (2, 0):
                for u in R:
                    a.need("pe", f"v{t}", u)
                    a.done(nc.scalar.activation(V8(u)[:, t, :], B[u][t][:], ACT.Identity), f"v{t}", u)
            for k in range(4):
                for u in R:
                    a.need("pe", f"q{k}", u)
                    a.done(nc.scalar.activation(Q[u][:], B[u][0][:], ACT.Identity), f"q{k}", u)
                for g in range(2):
                    for u in R:
                        a.need("pe", f"s{k}_{g}", u)
                        for part in (lo, hi):
                            last = nc.scalar.activation(pbd[u][part, 4 * g:4 * g + 4, part],
                                                        tf(B[u][2 + g][:, 0:256])[part], ACT.Sigmoid, scale=8.0)
                        a.done(last, f"p{k}_{g}", u)
                for u in R:
                    a.need("pe", f"o{k}", u)
                    a.done(nc.scalar.activation(o3(u, k), B[u][0][:], ACT.Identity), f"o{k}", u)

        def l3a_vector(d):
            ln_vector(d, "x", h, x)
            for t in (1, 3):
                for u in R:
                    d.need("pe", f"v{t}", u)
                    d.done(V.tensor_copy(V8(u)[:, t, :], B[u][t][:]), f"v{t}", u)
            for k in range(4):
                for u in R:
                    d.need("pe", f"k{k}", u)
                    d.done(V.tensor_copy(K[u][:], B[u][1][:]), f"k{k}", u)
            for u in R:
                d.need("pe", "wo", u)
                d.done(V.scalar_tensor_tensor(out=h[u][:], in0=tf(B[u][1][:, 0:256]), scalar=0.0, in1=h[u][:],
                                              op0=ALU.max, op1=ALU.add), "h", u)

        he = lambda u, e: A16[u][:, 512 * e:512 * e + 512]

        def l3f_tensor(p):
            flip_tensor(p, "x", x, "x.out")
            for u in R:
                p.need("act", "x.xT", u)
                for t in range(T):
                    last = mm(B[u][3][:, 8 * t:8 * t + 8], xT[u][lo, 128 * t:128 * t + 128], W("l3f_g"))
                p.done(last, "logits", u)
            for e in range(8):
                for u in R:
                    if e >= 2:
                        p.need("act", f"hid{e - 2}", u)
                    p.done(mm(B[u][e % 2][:], W("l3f_w1")[:, 128 * e:128 * e + 128], xT[u][lo, :]), f"hid{e}", u)
            for t in range(T):
                for u in R:
                    if t == 0:
                        p.need("act", "hid7", u)
                    if t == 1:
                        p.need("dve", "biased", u)
                    if t >= 2:
                        p.need("dve", f"raised{t - 2}", u)
                    o = B[u][2 + t % 2]
                    for e in range(8):
                        last = mm(o[:, 64 * e:64 * e + 64], he(u, e)[:, 128 * t:128 * t + 128],
                                  W("l3f_w2")[:, 64 * e:64 * e + 64])
                    p.done(last, f"out{t}", u)

        def l3f_scalar(a):
            ln_scalar(a, "x", x)
            flip_scalar(a, "x")
            for e in range(8):
                for u in R:
                    a.need("pe", f"hid{e}", u)
                    a.done(nc.scalar.activation(he(u, e), B[u][e % 2][:], ACT.Gelu, bias=W("l3f_b1")[:, e:e + 1]),
                           f"hid{e}", u)

        def l3f_vector(d):
            ln_vector(d, "x", h, x)
            for u in R:
                d.need("pe", "logits", u)
                d.done(V.tensor_tensor(st8(u, 160), tf(B[u][3][:, 0:32]), bmid(W("l3f_bg"), T), ALU.add), "biased", u)
            rank_vector(d, lambda u: st8(u, 160), 8, 2, "before", "biased")
            for u in R:
                d.need("dve", "chosen", u)
            for t in range(T):
                weigh_vector(d, t, lambda u: B[u][2 + t % 2][:].rearrange("p (e f) -> p e f", e=8),
                             lambda u: st8(u, 128), 8, f"out{t}", W("l3f_b2"))
            add_r(d)

        STAGES = ("l0b", "l0f", "l1a", "l1f", "l2a", "l2f", "l3a", "l3f")
        norms = {"l0a": ("x",), "l0b": (), "l0f": ("x", "r", "f"), "l1a": ("x", "r", "o"), "l1f": ("x",),
                 "l2f": ("x",), "l3a": ("x",), "l3f": ("x",)}
        tensor = dict(l0b=l0b_tensor, l0f=l0f_tensor, l1a=l1a_tensor, l1f=l1f_tensor, l2a=l2a_tensor, l2f=l2f_tensor,
                      l3a=l3a_tensor, l3f=l3f_tensor)
        scalar = dict(l0b=l0b_scalar, l0f=l0f_scalar, l1a=l1a_scalar, l1f=l1f_scalar, l2a=l2a_scalar, l2f=l2f_scalar,
                      l3a=l3a_scalar, l3f=l3f_scalar)
        vector = dict(l0b=l0b_vector, l0f=l0f_vector, l1a=l1a_vector, l1f=l1f_vector, l2a=l2a_vector, l2f=l2f_vector,
                      l3a=l3a_vector, l3f=l3f_vector)
        NBN = 16
        block = ctx.enter_context(nc.Block())

        @block.sync
        def _(sp):
            sp.dma_start(wts[:], weights_dram).then_inc(loaded, 16)
            sp.dma_start(cst[:], consts_dram).then_inc(loaded, 16)
            tiles = tok.rearrange("(b t p) f -> b p t f", t=T, p=128)
            outs = out_dram.rearrange("(b t p) f -> b p t f", t=T, p=128)
            for u in R:
                sp.dma_start(h[u][:], tiles[u]).then_inc(h_in[u], 16)
            with sp.Fori(1, ITERS) as it:
                for u in R:
                    sp.wait_ge(sig.sem("l0a", "dve"), sig.count("l0a", "dve", "hx", u, it) - sig.count("l0a", "dve", "hx", u, 1) + sig.count("l0a", "dve", "hx", u, 0))
                    sp.wait_ge(ready, 1)
                    sp.dma_start(h[u][:], tiles[bass.ds(blk(it, u), 1)].rearrange("b p t f -> (b p) t f"))\
                        .then_inc(h_in[u], 16)
            with sp.Fori(0, ITERS) as it:
                for u in R:
                    sp.wait_ge(sig.sem(STAGES[-1], "dve"), sig.count(STAGES[-1], "dve", "h", u, it))
                    sp.wait_ge(ready, 1)
                    sp.dma_start(outs[bass.ds(blk(it, u), 1)].rearrange("b p t f -> (b p) t f"), h[u][:])\
                        .then_inc(out_sent[u], 16)
            for u in R:
                sp.wait_ge(out_sent[u], 16 * ITERS + 1)

        @block.gpsimd
        def _(pool):
            pool.wait_ge(loaded, 32)
            with pool.Fori(0, ITERS) as it:
                ln_pool(Engine(sig, "pool", pool, "l0a", it), "x")
            pool.wait_ge(bn_done["dve"], 4)
            nc.gpsimd.tensor_tensor(bn[:, 19:20], bn[:, 18:19], W("mhalf")[lo, 0:1], ALU.pow).then_inc(bn_done["pool"], 1)
            with pool.Fori(0, ITERS) as it:
                for stage in STAGES:
                    p = Engine(sig, "pool", pool, stage, it, apart=(stage == "l2a"))
                    if stage == "l2a":
                        l2a_pool(p)
                    else:
                        for tag in norms[stage]:
                            ln_pool(p, tag)

        @block.tensor
        def _(pe):
            pe.wait_ge(loaded, 32)
            with pe.Fori(0, ITERS) as it:
                l0a_tensor(Engine(sig, "pe", pe, "l0a", it, apart=True))
            with pe.Fori(0, ITERS) as it:
                for stage in STAGES:
                    tensor[stage](Engine(sig, "pe", pe, stage, it, apart=True))

        @block.scalar
        def _(act):
            act.wait_ge(loaded, 32)
            with act.Fori(0, ITERS) as it:
                l0a_scalar(Engine(sig, "act", act, "l0a", it))
            act.wait_ge(bn_done["dve"], 2)
            for c in range(NBN):
                nc.scalar.activation(tmp[0][lo, :], hl[:, BLK * c:BLK * c + BLK], ACT.Square, bias=bn[:, 17:18],
                                     accum_out=bn[:, c:c + 1]).then_inc(bn_done["act"], 1)
                act.wait_ge(bn_done["act"], c + 1)
            
            with act.Fori(0, ITERS) as it:
                for stage in STAGES:
                    scalar[stage](Engine(sig, "act", act, stage, it))

        @block.vector
        def _(dve):
            for u in R:
                nc.vector.memset(xT[u][64:65, :], 1.0)
                nc.vector.memset(oT[u][64:65, :], 1.0).then_inc(out_sent[u], 1)
                last = nc.vector.memset(pbd[u][:], 0.0)
            last.then_inc(ready, 1)
            dve.wait_ge(loaded, 32)
            with dve.Fori(0, ITERS) as it:
                l0a_vector(Engine(sig, "dve", dve, "l0a", it))
            done = bn_done["dve"]
            def step(ins, n):
                ins.then_inc(done, 1)
                dve.wait_ge(done, n)
            dve.wait_ge(sig.sem("l0a", "dve"), sig.count("l0a", "dve", "hl", U - 1, ITERS - 1))
            step(V.reduce_sum(bn[:, 16:17], hl[:], axis=AX.X), 1)
            step(V.tensor_scalar(bn[:, 17:18], bn[:, 16:17], -1.0 / TOKENS, None, ALU.mult), 2)
            dve.wait_ge(bn_done["act"], NBN)
            step(V.reduce_sum(bn[:, 18:19], bn[:, 0:NBN], axis=AX.X), 3)
            step(V.tensor_scalar(bn[:, 18:19], bn[:, 18:19], 1.0 / TOKENS, 1e-5, ALU.mult, ALU.add), 4)
            dve.wait_ge(bn_done["pool"], 1)
            step(V.tensor_tensor(bn[:, 20:21], bn[:, 19:20], W("l0a_gamma"), ALU.mult), 5)
            with dve.Fori(0, ITERS) as it:
                for n, stage in enumerate(STAGES):
                    d = Engine(sig, "dve", dve, stage, it)
                    d.before = STAGES[n - 1]
                    vector[stage](d)



def tokenizer_inputs(i):
    g = lambda k: np.asarray(i["L0_tok_" + k])
    d = {}
    d["x_pairs"] = np.asarray(i["x"]).reshape(PAIRS, 2, J, 2, COLS, 3).transpose(0, 1, 3, 5, 2, 4).reshape(PAIRS, 12, PIX)
    d["grid_rows"] = g("input_grid").reshape(J, 2, COLS, 2).transpose(1, 3, 0, 2).reshape(4, PIX)
    d["embed_w"], d["embed_b"] = g("P_w"), g("P_b")
    wr, wi = (g(k).transpose(0, 3, 1, 4, 2)[:, EVEN_FIRST][:, :, :, EVEN_FIRST] for k in ("spec_wr", "spec_wi"))
    d["spec_uv"] = np.concatenate([np.concatenate([wr, wi], 2).reshape(LAYERS, MX, 64, CH),
                                   np.concatenate([wi, wr], 2).reshape(LAYERS, MX, 64, CH)], 3)
    d["conv_w"], d["conv_b"] = g("conv_w").transpose(0, 3, 2, 4, 1), g("conv_b")
    d["q1_w"], d["q1_b"], d["q2_w"], d["q2_b"] = g("Q1_w"), g("Q1_b"), g("Q2_w"), g("Q2_b")
    d["fwd"], d["inv"], d["tw"], d["eye"] = tokenizer_constants()
    return d


def kernel(**inputs):
    import concourse.bacc as bacc
    from concourse.bass_utils import run_bass_kernel_spmd

    nc = bacc.Bacc("TRN2", target_bir_lowering=False, num_devices=1)
    arrays = tokenizer_inputs(inputs)
    arrays["weights"], where_w = packed(block_weights(inputs))
    arrays["constants"], where_c = packed(block_constants())
    arrays = {"in_" + k: np.ascontiguousarray(v) for k, v in arrays.items()}
    a = {k[3:]: nc.dram_tensor(k, v.shape, mybir.dt.from_np(v.dtype), kind="ExternalInput").ap()
         for k, v in arrays.items()}
    out = nc.dram_tensor("out_0_dram", (IMGS, ROWS, COLS), F32, kind="ExternalOutput").ap()
    scratch = lambda name, shape: nc.dram_tensor(name, shape, F32, kind="Internal").ap()
    tokens = scratch("tokens", (IMGS, ROWS, COLS))
    build_tokenizer(nc, a["x_pairs"], a["grid_rows"], a["embed_w"], a["embed_b"], a["spec_uv"], a["conv_w"],
                    a["conv_b"], a["q1_w"], a["q1_b"], a["q2_w"], a["q2_b"], a["fwd"], a["inv"], a["tw"], a["eye"],
                    tokens.rearrange("g (j s) w -> g s j w", s=2),
                    scratch("h_rows", (PAIRS, 2, 2, WID, PIX)), scratch("g_modes", (2, WID, 2, 4, IMGS, MX * MY // 4)),
                    scratch("m_modes", (PAIRS, 2, MODES, 64)))
    build_blocks(nc, tokens.rearrange("g n f -> (g n) f"), out.rearrange("g n f -> (g n) f"), a["weights"],
                 a["constants"], where_w, where_c)
    result = run_bass_kernel_spmd(nc, [arrays], core_ids=[0])
    return result.results[0]["out_0_dram"]
```
